# Optimizing a Trainium2 kernel written in Bass

```python
import numpy as np
import jax
import jax.numpy as jnp

def _softmax(x, axis=-1):
    return jax.nn.softmax(x, axis=axis)

def _gelu(x):
    return jax.nn.gelu(x, approximate=True)

def _silu(x):
    return jax.nn.silu(x)

def _sigmoid(x):
    return jax.nn.sigmoid(x)

def _layernorm(x, axis=-1, eps=1e-05):
    m = jnp.mean(x, axis=axis, keepdims=True)
    v = jnp.var(x, axis=axis, keepdims=True)
    return (x - m) / jnp.sqrt(v + eps)

def _scatter_add(tgt, idx, src, axis=0):
    return tgt.at[idx].add(src)

def _segment_sum(src, seg, n):
    return jax.ops.segment_sum(src, seg, n)
kernel_name = 'mk_metaformer_d1_conv_nchw256_r2_008c9d'

def setup_inputs(seed: int=0):
    np.random.seed(seed)
    _w = jnp.asarray

    def _rec_inputs():
        import jax
        import jax.numpy as jnp
        _gk = jax.random.key(seed)
        x = -0.0002928 + 1 * jax.random.normal(jax.random.fold_in(_gk, 1), (4, 128, 32, 32), jnp.float32)
        return x
    x = _rec_inputs()

    def _L0_conv_setup():
        import jax, jax.numpy as jnp
        import numpy as np
        DIM = 128
        HEADS = 4
        HD = DIM // HEADS
        SCALE = HD ** (-0.5)
        CBS = 4
        CSTRIDE = 2
        SBS = 4
        NSEL = 16
        WS = 7
        B = 4
        H = 32
        W = 32

        def _unfold(x, bs, stride):
            b, h, w, c = x.shape
            nh = (h - bs) // stride + 1
            nw = (w - bs) // stride + 1
            cols = [x[:, kh:kh + nh * stride:stride, kw:kw + nw * stride:stride, :] for kh in range(bs) for kw in range(bs)]
            p = jnp.stack(cols, axis=-1)
            return p.reshape(b, nh * nw, c * bs * bs)

        def _rel_pos_index(ws):
            coords = np.stack(np.meshgrid(np.arange(ws), np.arange(ws), indexing='ij')).reshape(2, -1)
            rel = (coords[:, :, None] - coords[:, None, :]).transpose(1, 2, 0).copy()
            rel[:, :, 0] += ws - 1
            rel[:, :, 1] += ws - 1
            rel[:, :, 0] *= 2 * ws - 1
            return jnp.asarray(rel.sum(-1))

        def _mlp(x, w1, b1, w2, b2):
            return jax.nn.gelu(x @ w1 + b1, approximate=False) @ w2 + b2

        def _window_attn(x, qkv_w, qkv_b, proj_w, proj_b, bias_table):
            b, c, h, w = x.shape
            ws = WS
            ph = (ws - h % ws) % ws
            pw = (ws - w % ws) % ws
            xp = jnp.pad(x, ((0, 0), (0, 0), (0, ph), (0, pw)))
            hp, wp = (h + ph, w + pw)
            xw = xp.reshape(b, c, hp // ws, ws, wp // ws, ws).transpose(0, 2, 4, 3, 5, 1).reshape(-1, ws * ws, c)
            bw = xw.shape[0]
            qkv = (xw @ qkv_w + qkv_b).reshape(bw, ws * ws, 3, HEADS, HD).transpose(2, 0, 3, 1, 4)
            q, k, v = (qkv[0], qkv[1], qkv[2])
            attn = jnp.einsum('bhnd,bhmd->bhnm', q, k) * SCALE
            rpi = _rel_pos_index(ws)
            bias = bias_table[rpi.reshape(-1)].reshape(ws * ws, ws * ws, HEADS).transpose(2, 0, 1)
            attn = jax.nn.softmax(attn + bias[None], axis=-1)
            o = jnp.einsum('bhnm,bhmd->bhnd', attn, v).transpose(0, 2, 1, 3).reshape(bw, ws * ws, c)
            o = o @ proj_w + proj_b
            o = o.reshape(b, hp // ws, wp // ws, ws, ws, c).transpose(0, 5, 1, 3, 2, 4).reshape(b, c, hp, wp)
            return o[:, :, :h, :w]

        def _forward(x, qkv_cmp_w, qkv_cmp_b, qkv_slc_w, qkv_slc_b, cmpk_w1, cmpk_b1, cmpk_w2, cmpk_b2, cmpv_w1, cmpv_b1, cmpv_w2, cmpv_b2, pos_embed, win_qkv_w, win_qkv_b, win_proj_w, win_proj_b, win_bias_table, proj_cmp_w, proj_cmp_b, proj_slc_w, proj_slc_b, gate_w1, gate_b1, gate_w2, gate_b2):
            b, c, h, w = x.shape
            n = h * w
            xs = x.reshape(b, c, n).transpose(0, 2, 1)
            qkv = (xs @ qkv_cmp_w + qkv_cmp_b).reshape(b, n, 3, HEADS, HD).transpose(2, 0, 3, 1, 4)
            q_c, k_c, v_c = (qkv[0], qkv[1], qkv[2])
            k_flat = k_c.transpose(0, 2, 1, 3).reshape(b, n, c)
            v_flat = v_c.transpose(0, 2, 1, 3).reshape(b, n, c)
            fk = _unfold(k_flat.reshape(b, h, w, c), CBS, CSTRIDE)
            fv = _unfold(v_flat.reshape(b, h, w, c), CBS, CSTRIDE)
            nb = fk.shape[1]
            kpos = (fk.reshape(b, nb, CBS * CBS, c) + pos_embed[None]).reshape(b, nb, CBS * CBS * c)
            k_cmp = _mlp(kpos, cmpk_w1, cmpk_b1, cmpk_w2, cmpk_b2)
            v_cmp = _mlp(fv, cmpv_w1, cmpv_b1, cmpv_w2, cmpv_b2)
            kch = k_cmp.reshape(b, nb, HEADS, HD).transpose(0, 2, 1, 3)
            vch = v_cmp.reshape(b, nb, HEADS, HD).transpose(0, 2, 1, 3)
            attn_cmp = jax.nn.softmax(jnp.einsum('bhnd,bhmd->bhnm', q_c, kch) * SCALE, axis=-1)
            out_cmp = jnp.einsum('bhnm,bhmd->bhnd', attn_cmp, vch).transpose(0, 2, 1, 3).reshape(b, n, c)
            out_cmp = out_cmp @ proj_cmp_w + proj_cmp_b
            qkv2 = (xs @ qkv_slc_w + qkv_slc_b).reshape(b, n, 3, HEADS, HD).transpose(2, 0, 3, 1, 4)
            q_s, k_s, v_s = (qkv2[0], qkv2[1], qkv2[2])
            ks_flat = k_s.transpose(0, 2, 1, 3).reshape(b, n, c)
            vs_flat = v_s.transpose(0, 2, 1, 3).reshape(b, n, c)
            imp = attn_cmp.sum(axis=1).mean(axis=1)
            ns = min(NSEL, nb)
            _, idx = jax.lax.top_k(imp, ns)
            fkb = _unfold(ks_flat.reshape(b, h, w, c), SBS, SBS)
            fvb = _unfold(vs_flat.reshape(b, h, w, c), SBS, SBS)
            nb2 = fkb.shape[1]
            kb = fkb.reshape(b, nb2, SBS * SBS, c)
            vb = fvb.reshape(b, nb2, SBS * SBS, c)
            idx = jnp.clip(idx, 0, nb2 - 1)
            k_slc = jnp.take_along_axis(kb, idx[:, :, None, None], axis=1).reshape(b, ns * SBS * SBS, c)
            v_slc = jnp.take_along_axis(vb, idx[:, :, None, None], axis=1).reshape(b, ns * SBS * SBS, c)
            ksh = k_slc.reshape(b, -1, HEADS, HD).transpose(0, 2, 1, 3)
            vsh = v_slc.reshape(b, -1, HEADS, HD).transpose(0, 2, 1, 3)
            attn_slc = jax.nn.softmax(jnp.einsum('bhnd,bhmd->bhnm', q_s, ksh) * SCALE, axis=-1)
            out_slc = jnp.einsum('bhnm,bhmd->bhnd', attn_slc, vsh).transpose(0, 2, 1, 3).reshape(b, n, c)
            out_slc = out_slc @ proj_slc_w + proj_slc_b
            out_win = _window_attn(x, win_qkv_w, win_qkv_b, win_proj_w, win_proj_b, win_bias_table)
            out_win = out_win.reshape(b, c, n).transpose(0, 2, 1)
            g = jax.nn.sigmoid(jax.nn.gelu(xs @ gate_w1 + gate_b1, approximate=False) @ gate_w2 + gate_b2)
            out = g[..., 0:1] * out_cmp + g[..., 1:2] * out_slc + g[..., 2:3] * out_win
            return out.transpose(0, 2, 1).reshape(b, c, h, w)
        key = jax.random.key(seed)
        ks = jax.random.split(key, 16)
        s = 0.02
        d = {'x': jax.random.normal(ks[0], (B, DIM, H, W), jnp.float32), 'qkv_cmp_w': jax.random.normal(ks[1], (DIM, 3 * DIM)) * s, 'qkv_cmp_b': jnp.zeros((3 * DIM,)), 'qkv_slc_w': jax.random.normal(ks[2], (DIM, 3 * DIM)) * s, 'qkv_slc_b': jnp.zeros((3 * DIM,)), 'cmpk_w1': jax.random.normal(ks[3], (DIM * CBS * CBS, 2 * DIM)) * s, 'cmpk_b1': jnp.zeros((2 * DIM,)), 'cmpk_w2': jax.random.normal(ks[4], (2 * DIM, DIM)) * s, 'cmpk_b2': jnp.zeros((DIM,)), 'cmpv_w1': jax.random.normal(ks[5], (DIM * CBS * CBS, 2 * DIM)) * s, 'cmpv_b1': jnp.zeros((2 * DIM,)), 'cmpv_w2': jax.random.normal(ks[6], (2 * DIM, DIM)) * s, 'cmpv_b2': jnp.zeros((DIM,)), 'pos_embed': jax.random.normal(ks[7], (1, CBS * CBS, DIM)) * s, 'win_qkv_w': jax.random.normal(ks[8], (DIM, 3 * DIM)) * s, 'win_qkv_b': jnp.zeros((3 * DIM,)), 'win_proj_w': jax.random.normal(ks[9], (DIM, DIM)) * s, 'win_proj_b': jnp.zeros((DIM,)), 'win_bias_table': jax.random.normal(ks[10], ((2 * WS - 1) ** 2, HEADS)) * s, 'proj_cmp_w': jax.random.normal(ks[11], (DIM, DIM)) * s, 'proj_cmp_b': jnp.zeros((DIM,)), 'proj_slc_w': jax.random.normal(ks[12], (DIM, DIM)) * s, 'proj_slc_b': jnp.zeros((DIM,)), 'gate_w1': jax.random.normal(ks[13], (DIM, DIM // 4)) * s, 'gate_b1': jnp.zeros((DIM // 4,)), 'gate_w2': jax.random.normal(ks[14], (DIM // 4, 3)) * s, 'gate_b2': jnp.zeros((3,))}
        return d
    _L0_conv_all = _L0_conv_setup()
    _L0_conv_in = {k: v for k, v in _L0_conv_all.items() if k in ('qkv_cmp_w', 'qkv_cmp_b', 'qkv_slc_w', 'qkv_slc_b', 'cmpk_w1', 'cmpk_b1', 'cmpk_w2', 'cmpk_b2', 'cmpv_w1', 'cmpv_b1', 'cmpv_w2', 'cmpv_b2', 'pos_embed', 'win_qkv_w', 'win_qkv_b', 'win_proj_w', 'win_proj_b', 'win_bias_table', 'proj_cmp_w', 'proj_cmp_b', 'proj_slc_w', 'proj_slc_b', 'gate_w1', 'gate_b1', 'gate_w2', 'gate_b2')}
    del _L0_conv_all

    def _L0_ffn_setup():
        import jax, jax.numpy as jnp
        import numpy as np
        TOP_K = 2
        LN_EPS = 1e-05
        key = jax.random.key(seed)
        ks = jax.random.split(key, 8)
        B, S, D, E, H = (16, 512, 128, 8, 512)
        x = jax.random.normal(ks[0], (B, S, D), dtype=jnp.float32)
        Wr = jax.random.normal(ks[1], (D, E), dtype=jnp.float32) * 0.1
        br = jnp.zeros((E,), dtype=jnp.float32)
        ln_g = jnp.ones((E, D), dtype=jnp.float32)
        ln_b = jnp.zeros((E, D), dtype=jnp.float32)
        W1 = jax.random.normal(ks[2], (E, D, H), dtype=jnp.float32) * (1.0 / np.sqrt(D))
        b1 = jnp.zeros((E, H), dtype=jnp.float32)
        W2 = jax.random.normal(ks[3], (E, H, D), dtype=jnp.float32) * (1.0 / np.sqrt(H))
        b2 = jnp.zeros((E, D), dtype=jnp.float32)
        return {'x': x, 'Wr': Wr, 'br': br, 'ln_g': ln_g, 'ln_b': ln_b, 'W1': W1, 'b1': b1, 'W2': W2, 'b2': b2}
    _L0_ffn_all = _L0_ffn_setup()
    _L0_ffn_in = {k: v for k, v in _L0_ffn_all.items() if k in ('Wr', 'br', 'ln_g', 'ln_b', 'W1', 'b1', 'W2', 'b2')}
    del _L0_ffn_all
    return {'x': x, 'L0_conv_qkv_cmp_w': _L0_conv_in['qkv_cmp_w'], 'L0_conv_qkv_cmp_b': _L0_conv_in['qkv_cmp_b'], 'L0_conv_qkv_slc_w': _L0_conv_in['qkv_slc_w'], 'L0_conv_qkv_slc_b': _L0_conv_in['qkv_slc_b'], 'L0_conv_cmpk_w1': _L0_conv_in['cmpk_w1'], 'L0_conv_cmpk_b1': _L0_conv_in['cmpk_b1'], 'L0_conv_cmpk_w2': _L0_conv_in['cmpk_w2'], 'L0_conv_cmpk_b2': _L0_conv_in['cmpk_b2'], 'L0_conv_cmpv_w1': _L0_conv_in['cmpv_w1'], 'L0_conv_cmpv_b1': _L0_conv_in['cmpv_b1'], 'L0_conv_cmpv_w2': _L0_conv_in['cmpv_w2'], 'L0_conv_cmpv_b2': _L0_conv_in['cmpv_b2'], 'L0_conv_pos_embed': _L0_conv_in['pos_embed'], 'L0_conv_win_qkv_w': _L0_conv_in['win_qkv_w'], 'L0_conv_win_qkv_b': _L0_conv_in['win_qkv_b'], 'L0_conv_win_proj_w': _L0_conv_in['win_proj_w'], 'L0_conv_win_proj_b': _L0_conv_in['win_proj_b'], 'L0_conv_win_bias_table': _L0_conv_in['win_bias_table'], 'L0_conv_proj_cmp_w': _L0_conv_in['proj_cmp_w'], 'L0_conv_proj_cmp_b': _L0_conv_in['proj_cmp_b'], 'L0_conv_proj_slc_w': _L0_conv_in['proj_slc_w'], 'L0_conv_proj_slc_b': _L0_conv_in['proj_slc_b'], 'L0_conv_gate_w1': _L0_conv_in['gate_w1'], 'L0_conv_gate_b1': _L0_conv_in['gate_b1'], 'L0_conv_gate_w2': _L0_conv_in['gate_w2'], 'L0_conv_gate_b2': _L0_conv_in['gate_b2'], 'L0_ffn_Wr': _L0_ffn_in['Wr'], 'L0_ffn_br': _L0_ffn_in['br'], 'L0_ffn_ln_g': _L0_ffn_in['ln_g'], 'L0_ffn_ln_b': _L0_ffn_in['ln_b'], 'L0_ffn_W1': _L0_ffn_in['W1'], 'L0_ffn_b1': _L0_ffn_in['b1'], 'L0_ffn_W2': _L0_ffn_in['W2'], 'L0_ffn_b2': _L0_ffn_in['b2']}

def reference(x, L0_conv_qkv_cmp_w, L0_conv_qkv_cmp_b, L0_conv_qkv_slc_w, L0_conv_qkv_slc_b, L0_conv_cmpk_w1, L0_conv_cmpk_b1, L0_conv_cmpk_w2, L0_conv_cmpk_b2, L0_conv_cmpv_w1, L0_conv_cmpv_b1, L0_conv_cmpv_w2, L0_conv_cmpv_b2, L0_conv_pos_embed, L0_conv_win_qkv_w, L0_conv_win_qkv_b, L0_conv_win_proj_w, L0_conv_win_proj_b, L0_conv_win_bias_table, L0_conv_proj_cmp_w, L0_conv_proj_cmp_b, L0_conv_proj_slc_w, L0_conv_proj_slc_b, L0_conv_gate_w1, L0_conv_gate_b1, L0_conv_gate_w2, L0_conv_gate_b2, L0_ffn_Wr, L0_ffn_br, L0_ffn_ln_g, L0_ffn_ln_b, L0_ffn_W1, L0_ffn_b1, L0_ffn_W2, L0_ffn_b2):
    import jax
    import jax.numpy as jnp

    def _L0_conv_ref(x, qkv_cmp_w, qkv_cmp_b, qkv_slc_w, qkv_slc_b, cmpk_w1, cmpk_b1, cmpk_w2, cmpk_b2, cmpv_w1, cmpv_b1, cmpv_w2, cmpv_b2, pos_embed, win_qkv_w, win_qkv_b, win_proj_w, win_proj_b, win_bias_table, proj_cmp_w, proj_cmp_b, proj_slc_w, proj_slc_b, gate_w1, gate_b1, gate_w2, gate_b2):
        import jax, jax.numpy as jnp
        import numpy as np
        DIM = 128
        HEADS = 4
        HD = DIM // HEADS
        SCALE = HD ** (-0.5)
        CBS = 4
        CSTRIDE = 2
        SBS = 4
        NSEL = 16
        WS = 7
        B = 4
        H = 32
        W = 32

        def _unfold(x, bs, stride):
            b, h, w, c = x.shape
            nh = (h - bs) // stride + 1
            nw = (w - bs) // stride + 1
            cols = [x[:, kh:kh + nh * stride:stride, kw:kw + nw * stride:stride, :] for kh in range(bs) for kw in range(bs)]
            p = jnp.stack(cols, axis=-1)
            return p.reshape(b, nh * nw, c * bs * bs)

        def _rel_pos_index(ws):
            coords = np.stack(np.meshgrid(np.arange(ws), np.arange(ws), indexing='ij')).reshape(2, -1)
            rel = (coords[:, :, None] - coords[:, None, :]).transpose(1, 2, 0).copy()
            rel[:, :, 0] += ws - 1
            rel[:, :, 1] += ws - 1
            rel[:, :, 0] *= 2 * ws - 1
            return jnp.asarray(rel.sum(-1))

        def _mlp(x, w1, b1, w2, b2):
            return jax.nn.gelu(x @ w1 + b1, approximate=False) @ w2 + b2

        def _window_attn(x, qkv_w, qkv_b, proj_w, proj_b, bias_table):
            b, c, h, w = x.shape
            ws = WS
            ph = (ws - h % ws) % ws
            pw = (ws - w % ws) % ws
            xp = jnp.pad(x, ((0, 0), (0, 0), (0, ph), (0, pw)))
            hp, wp = (h + ph, w + pw)
            xw = xp.reshape(b, c, hp // ws, ws, wp // ws, ws).transpose(0, 2, 4, 3, 5, 1).reshape(-1, ws * ws, c)
            bw = xw.shape[0]
            qkv = (xw @ qkv_w + qkv_b).reshape(bw, ws * ws, 3, HEADS, HD).transpose(2, 0, 3, 1, 4)
            q, k, v = (qkv[0], qkv[1], qkv[2])
            attn = jnp.einsum('bhnd,bhmd->bhnm', q, k) * SCALE
            rpi = _rel_pos_index(ws)
            bias = bias_table[rpi.reshape(-1)].reshape(ws * ws, ws * ws, HEADS).transpose(2, 0, 1)
            attn = jax.nn.softmax(attn + bias[None], axis=-1)
            o = jnp.einsum('bhnm,bhmd->bhnd', attn, v).transpose(0, 2, 1, 3).reshape(bw, ws * ws, c)
            o = o @ proj_w + proj_b
            o = o.reshape(b, hp // ws, wp // ws, ws, ws, c).transpose(0, 5, 1, 3, 2, 4).reshape(b, c, hp, wp)
            return o[:, :, :h, :w]

        def _forward(x, qkv_cmp_w, qkv_cmp_b, qkv_slc_w, qkv_slc_b, cmpk_w1, cmpk_b1, cmpk_w2, cmpk_b2, cmpv_w1, cmpv_b1, cmpv_w2, cmpv_b2, pos_embed, win_qkv_w, win_qkv_b, win_proj_w, win_proj_b, win_bias_table, proj_cmp_w, proj_cmp_b, proj_slc_w, proj_slc_b, gate_w1, gate_b1, gate_w2, gate_b2):
            b, c, h, w = x.shape
            n = h * w
            xs = x.reshape(b, c, n).transpose(0, 2, 1)
            qkv = (xs @ qkv_cmp_w + qkv_cmp_b).reshape(b, n, 3, HEADS, HD).transpose(2, 0, 3, 1, 4)
            q_c, k_c, v_c = (qkv[0], qkv[1], qkv[2])
            k_flat = k_c.transpose(0, 2, 1, 3).reshape(b, n, c)
            v_flat = v_c.transpose(0, 2, 1, 3).reshape(b, n, c)
            fk = _unfold(k_flat.reshape(b, h, w, c), CBS, CSTRIDE)
            fv = _unfold(v_flat.reshape(b, h, w, c), CBS, CSTRIDE)
            nb = fk.shape[1]
            kpos = (fk.reshape(b, nb, CBS * CBS, c) + pos_embed[None]).reshape(b, nb, CBS * CBS * c)
            k_cmp = _mlp(kpos, cmpk_w1, cmpk_b1, cmpk_w2, cmpk_b2)
            v_cmp = _mlp(fv, cmpv_w1, cmpv_b1, cmpv_w2, cmpv_b2)
            kch = k_cmp.reshape(b, nb, HEADS, HD).transpose(0, 2, 1, 3)
            vch = v_cmp.reshape(b, nb, HEADS, HD).transpose(0, 2, 1, 3)
            attn_cmp = jax.nn.softmax(jnp.einsum('bhnd,bhmd->bhnm', q_c, kch) * SCALE, axis=-1)
            out_cmp = jnp.einsum('bhnm,bhmd->bhnd', attn_cmp, vch).transpose(0, 2, 1, 3).reshape(b, n, c)
            out_cmp = out_cmp @ proj_cmp_w + proj_cmp_b
            qkv2 = (xs @ qkv_slc_w + qkv_slc_b).reshape(b, n, 3, HEADS, HD).transpose(2, 0, 3, 1, 4)
            q_s, k_s, v_s = (qkv2[0], qkv2[1], qkv2[2])
            ks_flat = k_s.transpose(0, 2, 1, 3).reshape(b, n, c)
            vs_flat = v_s.transpose(0, 2, 1, 3).reshape(b, n, c)
            imp = attn_cmp.sum(axis=1).mean(axis=1)
            ns = min(NSEL, nb)
            _, idx = jax.lax.top_k(imp, ns)
            fkb = _unfold(ks_flat.reshape(b, h, w, c), SBS, SBS)
            fvb = _unfold(vs_flat.reshape(b, h, w, c), SBS, SBS)
            nb2 = fkb.shape[1]
            kb = fkb.reshape(b, nb2, SBS * SBS, c)
            vb = fvb.reshape(b, nb2, SBS * SBS, c)
            idx = jnp.clip(idx, 0, nb2 - 1)
            k_slc = jnp.take_along_axis(kb, idx[:, :, None, None], axis=1).reshape(b, ns * SBS * SBS, c)
            v_slc = jnp.take_along_axis(vb, idx[:, :, None, None], axis=1).reshape(b, ns * SBS * SBS, c)
            ksh = k_slc.reshape(b, -1, HEADS, HD).transpose(0, 2, 1, 3)
            vsh = v_slc.reshape(b, -1, HEADS, HD).transpose(0, 2, 1, 3)
            attn_slc = jax.nn.softmax(jnp.einsum('bhnd,bhmd->bhnm', q_s, ksh) * SCALE, axis=-1)
            out_slc = jnp.einsum('bhnm,bhmd->bhnd', attn_slc, vsh).transpose(0, 2, 1, 3).reshape(b, n, c)
            out_slc = out_slc @ proj_slc_w + proj_slc_b
            out_win = _window_attn(x, win_qkv_w, win_qkv_b, win_proj_w, win_proj_b, win_bias_table)
            out_win = out_win.reshape(b, c, n).transpose(0, 2, 1)
            g = jax.nn.sigmoid(jax.nn.gelu(xs @ gate_w1 + gate_b1, approximate=False) @ gate_w2 + gate_b2)
            out = g[..., 0:1] * out_cmp + g[..., 1:2] * out_slc + g[..., 2:3] * out_win
            return out.transpose(0, 2, 1).reshape(b, c, h, w)
        return _forward(x, qkv_cmp_w, qkv_cmp_b, qkv_slc_w, qkv_slc_b, cmpk_w1, cmpk_b1, cmpk_w2, cmpk_b2, cmpv_w1, cmpv_b1, cmpv_w2, cmpv_b2, pos_embed, win_qkv_w, win_qkv_b, win_proj_w, win_proj_b, win_bias_table, proj_cmp_w, proj_cmp_b, proj_slc_w, proj_slc_b, gate_w1, gate_b1, gate_w2, gate_b2)

    def _L0_ffn_ref(x, Wr, br, ln_g, ln_b, W1, b1, W2, b2):
        import jax, jax.numpy as jnp
        import numpy as np
        TOP_K = 2
        LN_EPS = 1e-05
        B, S, D = x.shape
        N = B * S
        xt = x.reshape(N, D)
        logits = xt @ Wr + br
        probs = jax.nn.softmax(logits, axis=-1)
        top_p, top_idx = jax.lax.top_k(probs, TOP_K)
        weights = top_p / top_p.sum(axis=-1, keepdims=True)
        mu = xt.mean(axis=-1, keepdims=True)
        var = ((xt - mu) ** 2).mean(axis=-1, keepdims=True)
        xn = (xt - mu) * jax.lax.rsqrt(var + LN_EPS)
        xe = xn[None, :, :] * ln_g[:, None, :] + ln_b[:, None, :]
        h = jax.nn.gelu(jnp.einsum('end,edh->enh', xe, W1) + b1[:, None, :], approximate=False)
        y = jnp.einsum('enh,ehd->end', h, W2) + b2[:, None, :]
        y_tok = jnp.transpose(y, (1, 0, 2))
        sel = jnp.take_along_axis(y_tok, top_idx[:, :, None], axis=1)
        out = (weights[:, :, None] * sel).sum(axis=1)
        return out.reshape(B, S, D)

    def _gn(v, G=32, eps=1e-05):
        B_, C_, H_, W_ = v.shape
        g = v.reshape(B_, G, C_ // G, H_, W_)
        m = jnp.mean(g, axis=(2, 3, 4), keepdims=True)
        s = jnp.var(g, axis=(2, 3, 4), keepdims=True)
        return ((g - m) / jnp.sqrt(s + eps)).reshape(v.shape)

    def _ln_c(v, eps=1e-06):
        m = jnp.mean(v, axis=1, keepdims=True)
        s = jnp.var(v, axis=1, keepdims=True)
        return (v - m) / jnp.sqrt(s + eps)

    def _ln_t(v, eps=1e-05):
        m = jnp.mean(v, axis=-1, keepdims=True)
        s = jnp.var(v, axis=-1, keepdims=True)
        return (v - m) / jnp.sqrt(s + eps)

    def _to_tokens(v):
        B_, C_, H_, W_ = v.shape
        return v.reshape(B_, C_, H_ * W_).transpose(0, 2, 1)

    def _from_tokens(t, like):
        B_, C_, H_, W_ = like.shape
        return t.transpose(0, 2, 1).reshape(B_, C_, H_, W_)
    x = x + _L0_conv_ref(_ln_c(x), L0_conv_qkv_cmp_w, L0_conv_qkv_cmp_b, L0_conv_qkv_slc_w, L0_conv_qkv_slc_b, L0_conv_cmpk_w1, L0_conv_cmpk_b1, L0_conv_cmpk_w2, L0_conv_cmpk_b2, L0_conv_cmpv_w1, L0_conv_cmpv_b1, L0_conv_cmpv_w2, L0_conv_cmpv_b2, L0_conv_pos_embed, L0_conv_win_qkv_w, L0_conv_win_qkv_b, L0_conv_win_proj_w, L0_conv_win_proj_b, L0_conv_win_bias_table, L0_conv_proj_cmp_w, L0_conv_proj_cmp_b, L0_conv_proj_slc_w, L0_conv_proj_slc_b, L0_conv_gate_w1, L0_conv_gate_b1, L0_conv_gate_w2, L0_conv_gate_b2)
    t = _to_tokens(x)
    t = t + _L0_ffn_ref(_ln_t(t), L0_ffn_Wr, L0_ffn_br, L0_ffn_ln_g, L0_ffn_ln_b, L0_ffn_W1, L0_ffn_b1, L0_ffn_W2, L0_ffn_b2)
    x = _from_tokens(t, x)
    return x

_drawn_inputs = setup_inputs


def setup_inputs(seed=0):
    import zlib

    import numpy as np

    out = dict(_drawn_inputs(seed))
    spreads = {'L0_conv_qkv_cmp_b': (0.0, 0.633),
     'L0_conv_qkv_slc_b': (0.0, 0.8),
     'L0_conv_cmpk_b1': (0.0, 0.8),
     'L0_conv_cmpk_b2': (0.0, 2.0),
     'L0_conv_cmpv_b1': (0.0, 0.415),
     'L0_conv_cmpv_b2': (0.0, 0.269),
     'L0_conv_win_qkv_b': (0.0, 0.1),
     'L0_conv_win_proj_b': (0.0, 0.1),
     'L0_conv_proj_cmp_b': (0.0, 0.1),
     'L0_conv_proj_slc_b': (0.0, 0.1),
     'L0_conv_gate_b1': (0.0, 0.8),
     'L0_conv_gate_b2': (0.0, 0.318),
     'L0_ffn_br': (0.0, 0.1),
     'L0_ffn_ln_g': (1.0, 0.2),
     'L0_ffn_ln_b': (0.0, 0.1),
     'L0_ffn_b1': (0.0, 0.1),
     'L0_ffn_b2': (0.0, 0.1)}
    factors = {'L0_conv_qkv_cmp_w': 5.828,
     'L0_conv_cmpk_w1': 5.117,
     'L0_conv_cmpk_w2': 5.191,
     'L0_conv_cmpv_w1': 5.251,
     'L0_conv_cmpv_w2': 4.287,
     'L0_conv_pos_embed': 8.0,
     'L0_conv_win_qkv_w': 3.497,
     'L0_conv_win_bias_table': 47.946,
     'L0_conv_gate_w1': 7.929,
     'L0_conv_gate_w2': 6.403}
    for name, (base, spread) in spreads.items():
        noise = np.random.default_rng([zlib.crc32(name.encode()), seed]).standard_normal(out[name].shape)
        drawn = base * np.exp(spread * noise) if base else spread * noise
        out[name] = jnp.asarray(drawn.astype(out[name].dtype))
    for name, factor in factors.items():
        out[name] = (out[name] * factor).astype(out[name].dtype)
    return out
```

```python
import concourse.bass as bass
from concourse import mybir
from contextlib import ExitStack

F32 = mybir.dt.float32
U32 = mybir.dt.uint32
ALU = mybir.AluOpType
ACT = mybir.ActivationFunctionType
AX = mybir.AxisListType

B, C, H, W = 4, 128, 32, 32
N = H * W
NT = N // 128
HEADS, HD = 4, 32
SCALE = HD ** -0.5
KS = 4
NPOS = KS * KS
NBH = (H - KS) // 2 + 1
NB = NBH * NBH
M0, M1 = 128, NB - 128
NSEL = 16
NBLK = (H // KS) * (W // KS)
WS = 7
GRID = 5
WTOK = WS * WS
GH = C // 4
SIDE = 2 * WS - 1
NWIN = GRID * GRID
NPAIR = (NWIN + 1) // 2
NGRP = (NPAIR + 1) // 2
E, HF = 8, 512
HC = HF // 128
EPS_C, EPS_T = 1e-6, 1e-5
O_LAG = 6
PW_LAG, OW_LAG = 2, 3
SEL_STEP = NGRP - 1
WPARTS = [(0, 10), (10, 10), (20, 5)]

COLS = ["bq_c", "bk_c", "bv_c", "bq_s", "bk_s", "bv_s", "bq_w", "bk_w", "b1k0", "b1k1", "b1v0", "b1v1",
        "b2k", "gate_b1", "gate_b2", "br", "m0", "m1"]
COL = {n: i for i, n in enumerate(COLS)}
COL_B1 = len(COLS)
COL_G = COL_B1 + E * HC
COL_LB = COL_G + E
COL_POS = COL_LB + E
NCOL = COL_POS + NPOS
ROW_BVW, ROW_B2V, ROW_PROJ, ROW_IOTA = 0, 128, 256, 640
NROW = 648


def psum_plan():
    plan, uses, at = {}, [0] * 8, [0]

    def fill(*names, pair=False):
        if pair and at[0] % 2:
            at[0] += 1
        for name in names:
            bank = at[0] % 8
            plan[name] = (bank, uses[bank])
            uses[bank] += 1
            at[0] += 1

    fill("xt0", "xt1", "xh0", "xh1", "kc0", "kc1", "vc0", "vc1", "qc0", "qc1", "gh0", "gh1",
         "kw0", "kw1", "kw2", "qw0", "qw1", "qw2", "gz0", "gz1", "gt", "mk0", "mk1", "mv0", "mv1", "k2")
    fill(*(f"vw{g}" for g in range(NGRP)))
    fill("v2")
    for s in "cs":
        for t in range(NT + 1):
            if t < NT:
                fill(f"S{s}{t}a", f"S{s}{t}b", pair=True)
            if t >= 1:
                fill(f"T{s}{t - 1}a", f"T{s}{t - 1}b")
            if t == O_LAG:
                fill(f"O{s}0")
        if s == "c":
            fill("qs0", "qs1", "Oc1")
            for g in range(NGRP + OW_LAG):
                if g < NGRP:
                    fill(f"SW{g}")
                if g == 0:
                    fill("imp")
                if 0 <= g - PW_LAG < NGRP:
                    fill(*(f"PW{p}" for p in pairs_of(g - PW_LAG)))
                if 0 <= g - OW_LAG < NGRP:
                    fill(f"OW{g - OW_LAG}")
                if g == SEL_STEP:
                    fill("ks", "vs")
            fill("vt")
        else:
            fill("Os1")
    fill(*(f"pj{t}" for t in range(NT)))
    fill("tt0", "tt1", "tn0", "tn1", "rl0", "rl1", "rt", "wt0", "wt1", "be0", "be1")
    for i in range(2 * E + 1):
        if i < 2 * E:
            fill(*(f"h{i}_{c}" for c in range(HC)))
        if i >= 1:
            fill(f"y{i - 1}")
    fill("out0", "out1")
    return plan, uses


def pairs_of(g):
    return [p for p in (2 * g, 2 * g + 1) if p < NPAIR]


def pair_rows(p):
    return 64 * (len(windows_of(p)) - 1) + WTOK


def group_shape(g):
    return HEADS * len(pairs_of(g)), pair_rows(2 * g)


def windows_of(p):
    return [w for w in (2 * p, 2 * p + 1) if w < NWIN]


def build(nc, x, wqkv_c, wqkv_s, wqkv_w, w1k, w1v, w2k, w2v, gate_w1, gate_w2, projs, wr, fw1, fw2, fb2,
          bias_tab, cols_d, rows_d, ident_d, out):
    plan, uses = psum_plan()
    DVE_LINKS = 70

    with ExitStack() as ctx:
        def sb(name, shape, dt=F32):
            return ctx.enter_context(nc.sbuf_tensor(name, shape, dt))

        def sem(name):
            return ctx.enter_context(nc.semaphore(name))

        qkvc_sb = sb("qkvc_sb", [128, 3 * C])
        qkvs_sb = sb("qkvs_sb", [128, 3 * C])
        qkvw_sb = sb("qkvw_sb", [128, 3 * C])
        w1k_sb = sb("w1k_sb", [128, NPOS, 2 * C])
        w1v_sb = sb("w1v_sb", [128, NPOS, 2 * C])
        w2k_sb = sb("w2k_sb", [128, 2, C])
        w2v_sb = sb("w2v_sb", [128, 2, C])
        gw1_sb = sb("gw1_sb", [128, 128])
        gw2_sb = sb("gw2_sb", [128, 3])
        proj_sb = sb("proj_sb", [128, 3, C])
        wr_sb = sb("wr_sb", [128, E])
        fw1_sb = sb("fw1_sb", [128, E, HF])
        fw2_sb = sb("fw2_sb", [128, E, HC, C])
        fb2_sb = sb("fb2_sb", [E, C])
        wbias = sb("wbias", [128, HEADS, WTOK])
        cols = sb("cols", [128, NCOL])
        rows = sb("rows", [128, NROW])
        ident = sb("ident", [128, 128])
        minus_half = sb("minus_half", [128, NT])

        def col(name, p0=0, p1=128):
            return cols[p0:p1, COL[name]:COL[name] + 1]

        x_sb = sb("x_sb", [128, N])
        x_tok = sb("x_tok", [128, NT, C])
        r_xhat = sb("r_xhat", [128, N])
        xhat_tok = r_xhat[:, :].rearrange("p (t c) -> p t c", t=NT)
        osT = r_xhat
        xhatT = sb("xhatT", [128, H, W])
        xblk = sb("xblk", [128, NBLK, NPOS])
        xwin = sb("xwin", [128, NWIN, WTOK])
        r_kc = sb("r_kc", [128, N])
        kcT = r_kc[:, :].rearrange("p (r c) -> p r c", r=H)
        ocT = r_kc
        r_vc = sb("r_vc", [128, N])
        vcT = r_vc[:, :].rearrange("p (r c) -> p r c", r=H)
        owT = r_vc
        qT = sb("qT", [128, N])
        r_gh = sb("r_gh", [128, N])
        gh = r_gh
        hk = r_gh[:, 0:2 * NB].rearrange("p (a m) -> p a m", a=2)
        hv = r_gh[:, 2 * NB:4 * NB].rearrange("p (a m) -> p a m", a=2)
        r_kp = sb("r_kp", [128, NPOS * NB])
        kp = r_kp[:, :].rearrange("p (s m) -> p s m", s=NPOS)
        vw = r_kp[0:WTOK, 0:NWIN * C].rearrange("p (w c) -> p w c", w=NWIN)
        kbdw = sb("kbdw", [128, HEADS, NWIN * WTOK])
        kbd = sb("kbd", [128, HEADS, 256])
        qwT = sb("qwT", [128, NWIN * WTOK])
        v_sb = sb("v_sb", [128, 2, C])
        r_P = sb("r_P", [128, 2 * HEADS * 256])
        Pb = r_P[:, :].rearrange("p (r h m) -> p r h m", r=2, h=HEADS)
        t_tok = r_P[:, 0:N].rearrange("p (t c) -> p t c", t=NT)
        acc = r_P[:, N:2 * N].rearrange("p (t c) -> p t c", t=NT)
        R = sb("R", [128, 2 * HEADS * N])
        PT = R[:, :].rearrange("p (a h n) -> p a h n", a=2, h=HEADS)
        at = [0]

        def part(n):
            at[0] += n
            return R[:, at[0] - n:at[0]]

        tw = part(3 * 392).rearrange("p (r n) -> p r n", r=3)
        ew = part(3 * 392).rearrange("p (r n) -> p r n", r=3)
        ptw = part(4 * 512).rearrange("p (r h n) -> p r h n", r=4, h=HEADS)
        xg = part(NSEL * NPOS).rearrange("p (k s) -> p k s", k=NSEL)
        kdup = part(2 * NSEL * NPOS).rearrange("p (k a s) -> p k a s", k=NSEL, a=2)
        kflip = part(2 * NSEL * NPOS).rearrange("p (k a s) -> p k a s", k=NSEL, a=2)
        khalf = part(NSEL * NPOS).rearrange("p (k s) -> p k s", k=NSEL)
        vselT = part(NSEL * NPOS)
        at[0] = 0
        gz = R[:, 0:N]
        hT = part(2 * HC * 512).rearrange("p (r c n) -> p r c n", r=2, c=HC)
        pj = R[:, at[0]:at[0] + 6 * C].rearrange("p (r n) -> p r n", r=2)
        xe = part(2 * 512).rearrange("p (r n) -> p r n", r=2)
        xtT = part(N)
        xnT = part(N)
        xo = part(N)
        xt_tok = r_xhat[:, :].rearrange("p (t c) -> p t c", t=NT)
        xn_tok = r_kc[:, :].rearrange("p (t c) -> p t c", t=NT)
        stats = sb("stats", [128, NT, 6])
        mv = sb("mv", [128, NT, 2])
        rstd = sb("rstd", [128, NT])
        vpe = sb("vpe", [128, NT])
        gtok = sb("gtok", [128, NT, 3])
        ge = sb("ge", [128, NT, 3])
        nmx = sb("nmx", [128, 2, HEADS])
        Z = sb("Z", [128, 2, HEADS])
        rZ = sb("rZ", [128, 2, HEADS])
        nmw = sb("nmw", [128, 3, 2 * HEADS])
        Zw = sb("Zw", [128, 3, 2 * HEADS])
        rZw = sb("rZw", [128, 3, 2 * HEADS])
        impacc = sb("impacc", [128, 2, NT])
        impcol = sb("impcol", [128, 2])
        imprun = sb("imprun", [1, 2, NB])
        top = sb("top", [1, 16])
        topi = sb("topi", [1, 16], U32)
        topc = sb("topc", [1, 16], U32)
        lg = sb("lg", [128, NT, E])
        lmax = sb("lmax", [128, NT, 8])
        lidx = sb("lidx", [128, NT, 8], U32)
        lidxf = sb("lidxf", [128, NT, 2])
        ldif = sb("ldif", [128, 3, NT])
        wtop = sb("wtop", [128, 2, NT])
        oneh = sb("oneh", [128, 2, NT, E])
        wtok = sb("wtok", [128, NT, E])

        ps = ctx.enter_context(nc.psum_tensor("ps", [128, 8 * 512], F32))

        bank_full = [sem(f"bank_full{i}") for i in range(8)]
        bank_read = [sem(f"bank_read{i}") for i in range(8)]
        const_in, proj_in, wk_in, wv_in = sem("const_in"), sem("proj_in"), sem("wk_in"), sem("wv_in")
        w2_in, win_in, tail_in, ffn_in = sem("w2_in"), sem("win_in"), sem("tail_in"), sem("ffn_in")
        bias_in = sem("bias_in")
        x_in, out_done = sem("x_in"), sem("out_done")
        zeroed = sem("zeroed")
        var_ready, rstd_ready = sem("var_ready"), sem("rstd_ready")
        xhat_tok_ready, xblk_ready = sem("xhat_tok_ready"), sem("xblk_ready")
        xwin_ready = sem("xwin_ready")
        kp_ready, gz_exp_ready, g_ready = sem("kp_ready"), sem("gz_exp_ready"), sem("g_ready")
        max_ready, prob_ready = sem("max_ready"), sem("prob_ready")
        impcol_ready, sel_ready, xg_ready = sem("impcol_ready"), sem("sel_ready"), sem("xg_ready")
        kbd_sel_ready, vselT_ready = sem("kbd_sel_ready"), sem("vselT_ready")
        wmax_ready, wsub_ready, wexp_ready = sem("wmax_ready"), sem("wsub_ready"), sem("wexp_ready")
        wrz_ready, wprob_ready = sem("wrz_ready"), sem("wprob_ready")
        xt_ready, xn_ready = sem("xt_ready"), sem("xn_ready")
        ldif_ready, lexp_ready, wtok_ready = sem("ldif_ready"), sem("lexp_ready"), sem("wtok_ready")
        xe_ready, acc_ready = sem("xe_ready"), sem("acc_ready")
        dve_done = sem("dve_done")

        def bank(name):
            k = plan[name][0]
            return ps[:, 512 * k:512 * k + 512]

        def free_for(b, name):
            k, n = plan[name]
            return bank_read[k], b * uses[k] + n + 1

        def filled(b, name):
            k, n = plan[name]
            return bank_full[k], b * uses[k] + n + 1

        def copied(b, name):
            k, n = plan[name]
            return bank_read[k], b * uses[k] + n + 2

        def full_sem(name):
            return bank_full[plan[name][0]]

        def read_sem(name):
            return bank_read[plan[name][0]]

        def window(w):
            r, c = divmod(w, GRID)
            return WS * r, min(WS, H - WS * r), WS * c, min(WS, W - WS * c)

        def keys_to_blocks(eng, ops, b, i):
            w0, nw = WPARTS[i]
            name = f"kw{i}"
            eng.wait_ge(zeroed, 6)
            eng.wait_ge(*filled(b, name))
            for h in range(HEADS):
                p0, p1 = HD * h, HD * h + HD
                dst = kbdw[p0:p1, h, w0 * WTOK:(w0 + nw) * WTOK]
                src = bank(name)[p0:p1, 0:nw * WTOK]
                if ops is nc.scalar:
                    last = ops.activation(dst, src, ACT.Identity, bias=col("bk_w", p0, p1))
                else:
                    last = ops.tensor_scalar(dst, src, col("bk_w", p0, p1), None, ALU.add)
            last.then_inc(read_sem(name), 1)

        block = ctx.enter_context(nc.Block())

        @block.sync
        def _(sp):
            sp.dma_start(x_sb[:, :], x[0, :, :]).then_inc(x_in, 16)
            sp.dma_start(ident[:, :], ident_d).then_inc(const_in, 16)
            sp.dma_start(cols[:, :], cols_d).then_inc(const_in, 16)
            sp.dma_start(rows[:, :], rows_d[0, :].partition_broadcast(128)).then_inc(const_in, 16)
            sp.dma_start(qkvc_sb[:, :], wqkv_c).then_inc(proj_in, 16)
            sp.dma_start(qkvw_sb[:, :], wqkv_w).then_inc(proj_in, 16)
            sp.wait_ge(zeroed, 4)
            for j in range(2):
                sp.dma_start(wbias[64 * j:64 * j + WTOK, :, :].rearrange("p h m -> p (h m)"), bias_tab).then_inc(bias_in, 16)
            sp.dma_start(w1k_sb[:, :, :], w1k.rearrange("(c s) n -> c s n", s=NPOS)).then_inc(wk_in, 16)
            sp.dma_start(w1v_sb[:, :, :], w1v.rearrange("(c s) n -> c s n", s=NPOS)).then_inc(wv_in, 16)
            sp.dma_start(w2k_sb[:, :, :], w2k.rearrange("(a p) n -> p a n", p=128)).then_inc(w2_in, 16)
            sp.dma_start(w2v_sb[:, :, :], w2v.rearrange("(a p) n -> p a n", p=128)).then_inc(w2_in, 16)
            sp.dma_start(qkvs_sb[:, :], wqkv_s).then_inc(tail_in, 16)
            sp.dma_start(proj_sb[:, :, :], projs.rearrange("a p n -> p a n")).then_inc(tail_in, 16)
            sp.dma_start(wr_sb[:, :], wr).then_inc(tail_in, 16)
            sp.dma_start(fb2_sb[:, :], fb2).then_inc(tail_in, 16)
            sp.dma_start(fw1_sb[:, :, :], fw1.rearrange("e p n -> p e n")).then_inc(ffn_in, 16)
            sp.dma_start(fw2_sb[:, :, :, :], fw2.rearrange("e (c p) n -> p e c n", p=128)).then_inc(ffn_in, 16)
            with sp.Fori(1, B) as b:
                sp.wait_ge(*filled(b - 1, "xt1"))
                sp.dma_start(x_sb[:, :], x[bass.ds(b, 1), :, :].rearrange("a p n -> (a p) n")).then_inc(x_in, 16)
            sp.wait_ge(out_done, 16 * B + 16)

        @block.gpsimd
        def _(pool):
            gp = nc.gpsimd
            gp.memset(minus_half[:, :], -0.5).then_inc(out_done, 16)
            gp.memset(xwin[:, :, :], 0.0).then_inc(zeroed, 1)
            gp.memset(gw1_sb[:, :], 0.0).then_inc(zeroed, 1)
            gp.memset(gw2_sb[:, :], 0.0).then_inc(zeroed, 1)
            gp.memset(wbias[:, :, :], 0.0).then_inc(zeroed, 1)
            pool.wait_ge(zeroed, 4)
            pool.dma_start(gw1_sb[:, 0:GH], gate_w1).then_inc(win_in, 16)
            pool.dma_start(gw2_sb[0:GH, :], gate_w2).then_inc(win_in, 16)
            gp.memset(kbdw[:, :, :], 0.0).then_inc(zeroed, 1)
            gp.memset(kbd[:, :, :], 0.0).then_inc(zeroed, 1)

            with pool.Fori(0, B) as b:

                def inverse_root(k):
                    pool.wait_ge(var_ready, b * 3 + k + 1)
                    gp.tensor_tensor(rstd[:, :], vpe[:, :], minus_half[:, :], ALU.pow).then_inc(rstd_ready, 1)

                inverse_root(0)
                pool.wait_ge(*copied(b, "xh0"))
                pool.wait_ge(*copied(b, "xh1"))
                pool.nop(nofuse=True)
                for wr in range(GRID):
                    nr = min(WS, H - WS * wr)
                    for wc, nw in ((0, GRID - 1), (GRID - 1, 1)):
                        ncol = WS if wc == 0 else W - WS * wc
                        last = gp.tensor_copy(
                            xwin[:, GRID * wr + wc:GRID * wr + wc + nw, :].rearrange("p w (r c) -> p w r c", r=WS)[:, :, 0:nr, 0:ncol],
                            xhatT[:, WS * wr:WS * wr + nr, WS * wc:WS * wc + nw * ncol].rearrange("p r (w c) -> p w r c", w=nw))
                last.then_inc(xwin_ready, 1)
                for br in range(H // KS):
                    last = gp.tensor_copy(
                        xblk[:, 8 * br:8 * br + 8, :].rearrange("p k (r c) -> p k r c", r=KS),
                        xhatT[:, KS * br:KS * br + KS, :].rearrange("p r (k c) -> p k r c", c=KS))
                last.then_inc(xblk_ready, 1)

                def select_tokens():
                    pool.wait_ge(xblk_ready, b + 1)
                    pool.wait_ge(sel_ready, b + 1)
                    pool.nop(nofuse=True)
                    for i in range(NSEL):
                        idx = pool.value_load(topc[0:1, i:i + 1], min_val=0, max_val=NBLK - 1)
                        last = gp.tensor_copy(xg[:, i, :], xblk[:, bass.ds(idx, 1), :].rearrange("p a s -> p (a s)"))
                    last.then_inc(xg_ready, 1)

                for g in range(NGRP + 1):
                    if g < NGRP:
                        n, np_ = group_shape(g)
                        pool.wait_ge(wmax_ready, b * NGRP + g + 1)
                        v = tw[0:np_, g % 3, 0:n * WTOK].rearrange("p (a m) -> p a m", m=WTOK)
                        gp.tensor_tensor(v, v, nmw[0:np_, g % 3, 0:n].unsqueeze(2).to_broadcast([np_, n, WTOK]),
                                         ALU.add).then_inc(wsub_ready, 1)
                    if g >= 1:
                        n, np_ = group_shape(g - 1)
                        k = (g - 1) % 3
                        pool.wait_ge(wrz_ready, b * NGRP + g)
                        v = ew[0:np_, k, 0:n * WTOK].rearrange("p (a m) -> p a m", m=WTOK)
                        gp.tensor_tensor(v, v, rZw[0:np_, k, 0:n].unsqueeze(2).to_broadcast([np_, n, WTOK]),
                                         ALU.mult).then_inc(wprob_ready, 1)
                    if g == 3:
                        select_tokens()
                inverse_root(1)
                inverse_root(2)

        @block.scalar
        def _(act):
            sc = nc.scalar
            with act.Fori(0, B) as b:
                act.wait_ge(const_in, 48)
                for i in range(2):
                    act.wait_ge(*filled(b, f"xt{i}"))
                    sc.activation(x_tok[:, 4 * i:4 * i + 4, :].rearrange("p t c -> p (t c)"), bank(f"xt{i}"),
                                  ACT.Copy).then_inc(read_sem(f"xt{i}"), 1)
                for i in range(2):
                    act.wait_ge(*filled(b, f"xh{i}"))
                    sc.activation(xhatT[:, 16 * i:16 * i + 16, :].rearrange("p r c -> p (r c)"), bank(f"xh{i}"),
                                  ACT.Copy).then_inc(read_sem(f"xh{i}"), 1)
                for i in range(2):
                    act.wait_ge(*filled(b, f"kc{i}"))
                    sc.activation(kcT[:, 16 * i:16 * i + 16, :].rearrange("p r c -> p (r c)"), bank(f"kc{i}"),
                                  ACT.Identity, bias=col("bk_c")).then_inc(read_sem(f"kc{i}"), 1)
                for i in range(2):
                    act.wait_ge(*filled(b, f"gh{i}"))
                    sc.activation(gh[:, 512 * i:512 * i + 512], bank(f"gh{i}"), ACT.Gelu,
                                  bias=col("gate_b1")).then_inc(read_sem(f"gh{i}"), 1)
                keys_to_blocks(act, sc, b, 1)
                for i in (0, 2):
                    w0, nw = WPARTS[i]
                    act.wait_ge(*filled(b, f"qw{i}"))
                    sc.activation(qwT[:, w0 * WTOK:(w0 + nw) * WTOK], bank(f"qw{i}")[:, 0:nw * WTOK],
                                  ACT.Identity, bias=col("bq_w")).then_inc(read_sem(f"qw{i}"), 1)
                for i in range(2):
                    act.wait_ge(*filled(b, f"gz{i}"))
                    sc.activation(gz[0:3, 512 * i:512 * i + 512], bank(f"gz{i}")[0:3, :], ACT.Identity,
                                  bias=col("gate_b2", 0, 3)).then_inc(read_sem(f"gz{i}"), 1)
                act.wait_ge(*filled(b, "gt"))
                sc.activation(ge[:, :, :].rearrange("p t g -> p (t g)"), bank("gt")[:, 0:3 * NT], ACT.Exp,
                              scale=-1.0).then_inc(read_sem("gt"), 1)
                for name, h, bias in (("mk", hk, "b1k"), ("mv", hv, "b1v")):
                    for a in range(2):
                        act.wait_ge(*filled(b, f"{name}{a}"))
                        sc.activation(h[:, a, :], bank(f"{name}{a}")[:, 0:NB], ACT.Gelu,
                                      bias=col(f"{bias}{a}")).then_inc(read_sem(f"{name}{a}"), 1)
                act.wait_ge(*filled(b, "k2"))
                for h in range(HEADS):
                    q = slice(HD * h, HD * h + HD)
                    last = sc.activation(kbd[q, h, 0:NB], bank("k2")[q, 0:NB], ACT.Identity,
                                         bias=col("b2k", HD * h, HD * h + HD))
                last.then_inc(read_sem("k2"), 1)

                def exps(s, base, t, m):
                    act.wait_ge(max_ready, b * 2 * NT + base + t + 1)
                    for h in range(HEADS):
                        name = f"S{s}{t}{'ab'[h // 2]}"
                        last = sc.activation(Pb[:, t % 2, h, 0:m], bank(name)[:, (h % 2) * m:(h % 2) * m + m], ACT.Exp,
                                             bias=nmx[:, t % 2, h:h + 1], accum_out=Z[:, t % 2, h:h + 1])
                        if h % 2:
                            last.then_inc(read_sem(name), 1)

                def second_chunk(s, t, m1):
                    name = f"T{s}{t}b"
                    act.wait_ge(*filled(b, name))
                    dst = PT[0:m1, 1, :, 128 * t:128 * t + 128]
                    src = bank(name)[0:m1, :].rearrange("p (h n) -> p h n", h=HEADS)
                    if s == "c":
                        sc.activation(dst, src, ACT.Copy, accum_out=impacc[0:m1, 1, t:t + 1]).then_inc(read_sem(name), 1)
                    else:
                        sc.activation(dst, src, ACT.Copy).then_inc(read_sem(name), 1)

                act.wait_ge(out_done, 16 * b + 16)
                for t in range(NT + 1):
                    if t < NT:
                        exps("c", 0, t, NB)
                    if t >= 1:
                        second_chunk("c", t - 1, M1)

                for g in range(NGRP + OW_LAG):
                    if g < NGRP:
                        n, np_ = group_shape(g)
                        act.wait_ge(wsub_ready, b * NGRP + g + 1)
                        sc.activation(ew[0:np_, g % 3, 0:n * WTOK], tw[0:np_, g % 3, 0:n * WTOK], ACT.Exp)\
                          .then_inc(wexp_ready, 1)
                    if 0 <= g - PW_LAG < NGRP:
                        for p in pairs_of(g - PW_LAG):
                            np_ = pair_rows(p)
                            act.wait_ge(*filled(b, f"PW{p}"))
                            sc.activation(ptw[0:WTOK, p % 4, :, 0:np_],
                                          bank(f"PW{p}")[0:WTOK, :].rearrange("p (h n) -> p h n", h=HEADS)[:, :, 0:np_],
                                          ACT.Copy).then_inc(read_sem(f"PW{p}"), 1)
                act.wait_ge(*filled(b, "vt"))
                sc.activation(v_sb[:, :, :].rearrange("p a c -> p (a c)"), bank("vt")[:, 0:2 * C],
                              ACT.Copy).then_inc(read_sem("vt"), 1)
                for t in range(NT + 1):
                    if t < NT:
                        exps("s", NT, t, 256)
                    if t >= 1:
                        second_chunk("s", t - 1, 128)

                for name, dst in (("tt", xtT), ("tn", xnT)):
                    for i in range(2):
                        act.wait_ge(*filled(b, f"{name}{i}"))
                        sc.activation(dst[:, 512 * i:512 * i + 512], bank(f"{name}{i}"), ACT.Copy)\
                          .then_inc(read_sem(f"{name}{i}"), 1)
                for i in range(2):
                    act.wait_ge(*filled(b, f"rl{i}"))
                    sc.activation(gz[0:E, 512 * i:512 * i + 512], bank(f"rl{i}")[0:E, :], ACT.Identity,
                                  bias=col("br", 0, E)).then_inc(read_sem(f"rl{i}"), 1)
                act.wait_ge(ldif_ready, b + 1)
                sc.activation(ldif[:, 1, :], ldif[:, 0, :], ACT.Exp).then_inc(lexp_ready, 1)
                for i in range(2):
                    act.wait_ge(*filled(b, f"wt{i}"))
                    sc.activation(gz[0:E, 512 * i:512 * i + 512], bank(f"wt{i}")[0:E, :], ACT.Copy)\
                      .then_inc(read_sem(f"wt{i}"), 1)
                for i in range(2 * E):
                    for c in range(HC):
                        act.wait_ge(*filled(b, f"h{i}_{c}"))
                        k = COL_B1 + (i % E) * HC + c
                        sc.activation(hT[:, i % 2, c, :], bank(f"h{i}_{c}"), ACT.Gelu, bias=cols[:, k:k + 1])\
                          .then_inc(read_sem(f"h{i}_{c}"), 1)
                for i in range(2):
                    act.wait_ge(*filled(b, f"out{i}"))
                    sc.activation(xo[:, 512 * i:512 * i + 512], bank(f"out{i}"), ACT.Copy)\
                      .then_inc(read_sem(f"out{i}"), 1)
                act.wait_ge(*copied(b, "out0"))
                act.wait_ge(*copied(b, "out1"))
                act.dma_start(out[bass.ds(b, 1), :, :].rearrange("a p n -> (a p) n"), xo).then_inc(out_done, 16)

        @block.vector
        def _(dve):
            ve = nc.vector
            for k in range(8):
                ve.memset(ps[:, 512 * k:512 * k + 512], 0.0).then_inc(bank_read[k], 1)
            with dve.Fori(0, B) as b:
                links = [0]

                def link(ins):
                    links[0] += 1
                    ins.then_inc(dve_done, 1)
                    dve.wait_ge(dve_done, b * DVE_LINKS + links[0])

                def normalise(k, src, dst, eps, ready):
                    for t in range(NT):
                        last = ve.bn_stats(stats[:, t, :], src[:, t, :])
                    link(last)
                    dve.nop(nofuse=True)
                    for t in range(NT):
                        last = ve.bn_aggr(mv[:, t, :], stats[:, t, :])
                    link(last)
                    ve.tensor_scalar(vpe[:, :], mv[:, :, 1], eps, None, ALU.add).then_inc(var_ready, 1)
                    dve.wait_ge(rstd_ready, b * 3 + k + 1)
                    for t in range(NT):
                        last = ve.tensor_scalar(dst[:, t, :], src[:, t, :], mv[:, t, 0:1], rstd[:, t:t + 1],
                                                ALU.subtract, ALU.mult)
                        if t % 4 == 3:
                            last.then_inc(ready, 1)

                dve.wait_ge(const_in, 48)
                dve.wait_ge(*copied(b, "xt0"))
                dve.wait_ge(*copied(b, "xt1"))
                normalise(0, x_tok, xhat_tok, EPS_C, xhat_tok_ready)
                dve.wait_ge(*copied(b, "kc0"))
                dve.wait_ge(*copied(b, "kc1"))
                for s in range(NPOS):
                    r, c = divmod(s, KS)
                    ve.tensor_scalar(kp[:, s, :].rearrange("p (r c) -> p r c", r=NBH),
                                     kcT[:, r:r + 2 * NBH - 1:2, c:c + 2 * NBH - 1:2],
                                     cols[:, COL_POS + s:COL_POS + s + 1], None, ALU.add).then_inc(kp_ready, 1)
                for i in range(2):
                    dve.wait_ge(*filled(b, f"vc{i}"))
                    ve.tensor_scalar(vcT[:, 16 * i:16 * i + 16, :].rearrange("p r c -> p (r c)"), bank(f"vc{i}"),
                                     col("bv_c"), None, ALU.add).then_inc(read_sem(f"vc{i}"), 1)

                def queries(name, bias):
                    for i in range(2):
                        dve.wait_ge(*filled(b, f"{name}{i}"))
                        ve.tensor_scalar(qT[:, 512 * i:512 * i + 512], bank(f"{name}{i}"), col(bias), SCALE,
                                         ALU.add, ALU.mult).then_inc(read_sem(f"{name}{i}"), 1)

                queries("qc", "bq_c")
                keys_to_blocks(dve, ve, b, 0)
                keys_to_blocks(dve, ve, b, 2)
                dve.wait_ge(*filled(b, "qw1"))
                w0, nw = WPARTS[1]
                ve.tensor_scalar(qwT[:, w0 * WTOK:(w0 + nw) * WTOK], bank("qw1")[:, 0:nw * WTOK],
                                 col("bq_w"), None, ALU.add).then_inc(read_sem("qw1"), 1)
                dve.wait_ge(*copied(b, "gt"))
                link(ve.tensor_scalar(ge[:, :, :], ge[:, :, :], 1.0, None, ALU.add))
                link(ve.reciprocal(gtok[:, :, :], ge[:, :, :]))
                for g in range(NGRP):
                    n = min(4, NWIN - 4 * g)
                    dve.wait_ge(*filled(b, f"vw{g}"))
                    ve.tensor_tensor(vw[:, 4 * g:4 * g + n, :],
                                     bank(f"vw{g}")[0:WTOK, 0:n * C].rearrange("p (w c) -> p w c", c=C),
                                     rows[0:WTOK, ROW_BVW:ROW_BVW + C].unsqueeze(1).to_broadcast([WTOK, n, C]),
                                     ALU.add).then_inc(read_sem(f"vw{g}"), 1)
                dve.wait_ge(*filled(b, "v2"))
                ve.tensor_tensor(v_sb[:, 0, :], bank("v2")[:, 0:C], rows[:, ROW_B2V:ROW_B2V + C], ALU.add)
                ve.tensor_tensor(v_sb[0:M1, 1, :], bank("v2")[0:M1, C:2 * C], rows[0:M1, ROW_B2V:ROW_B2V + C],
                                 ALU.add).then_inc(read_sem("v2"), 1)

                def maxima(s, t, m):
                    dve.wait_ge(*filled(b, f"S{s}{t}a"))
                    dve.wait_ge(*filled(b, f"S{s}{t}b"))
                    k = plan[f"S{s}{t}a"][0]
                    v = ps[:, 512 * k:512 * k + 1024].rearrange("p (a n) -> p a n", a=2)[:, :, 0:2 * m]
                    ve.tensor_reduce(nmx[:, t % 2, :].rearrange("p (a h) -> p a h", a=2),
                                     v.rearrange("p a (h m) -> p a h m", h=2), AX.X, ALU.max, negate=True)\
                      .then_inc(max_ready, 1)

                def divide(s, t, m):
                    dve.wait_ge(*copied(b, f"S{s}{t}b"))
                    link(ve.reciprocal(rZ[:, t % 2, :], Z[:, t % 2, :]))
                    for h in range(HEADS):
                        last = ve.tensor_scalar(Pb[:, t % 2, h, 0:m], Pb[:, t % 2, h, 0:m], rZ[:, t % 2, h:h + 1],
                                                None, ALU.mult)
                    last.then_inc(prob_ready, 1)

                def first_chunk(s, t):
                    name = f"T{s}{t}a"
                    dve.wait_ge(*filled(b, name))
                    dst = PT[:, 0, :, 128 * t:128 * t + 128]
                    src = bank(name).rearrange("p (h n) -> p h n", h=HEADS)
                    if s == "c":
                        ve.tensor_scalar(dst, src, 1.0, None, ALU.mult, ALU.add,
                                         accum_out=impacc[:, 0, t:t + 1]).then_inc(read_sem(name), 1)
                    else:
                        ve.tensor_copy(dst, src).then_inc(read_sem(name), 1)

                def branch_output(s, i, dst):
                    dve.wait_ge(*filled(b, f"O{s}{i}"))
                    ve.tensor_copy(dst[:, 512 * i:512 * i + 512], bank(f"O{s}{i}")).then_inc(read_sem(f"O{s}{i}"), 1)

                def tiles(s, m, dst):
                    for t in range(NT + 2):
                        if t < NT:
                            maxima(s, t, m)
                        if t >= 2:
                            first_chunk(s, t - 2)
                        if 1 <= t <= NT:
                            divide(s, t - 1, m)
                        if t == O_LAG + 1:
                            branch_output(s, 0, dst)

                tiles("c", NB, ocT)
                dve.wait_ge(*copied(b, f"Tc{NT - 1}a"))
                dve.wait_ge(*copied(b, f"Tc{NT - 1}b"))
                ve.tensor_reduce(impcol[:, 0:1], impacc[:, 0, :], AX.X, ALU.add)
                ve.tensor_reduce(impcol[0:M1, 1:2], impacc[0:M1, 1, :], AX.X, ALU.add).then_inc(impcol_ready, 1)
                queries("qs", "bq_s")
                branch_output("c", 1, ocT)

                def top_blocks():
                    dve.wait_ge(*filled(b, "imp"))
                    ve.tensor_copy(imprun[0:1, 0, :], bank("imp")[0:1, 0:NB]).then_inc(read_sem("imp"), 1)
                    dve.wait_ge(*copied(b, "imp"))
                    dve.nop(nofuse=True)
                    link(ve.max(top[0:1, 0:8], imprun[0:1, 0, :]))
                    dve.nop(nofuse=True)
                    ve.max_index(topi[0:1, 0:8], top[0:1, 0:8], imprun[0:1, 0, :])
                    link(ve.match_replace(imprun[0:1, 1, :], top[0:1, 0:8], imprun[0:1, 0, :], -1.0))
                    dve.nop(nofuse=True)
                    link(ve.max(top[0:1, 8:16], imprun[0:1, 1, :]))
                    dve.nop(nofuse=True)
                    link(ve.max_index(topi[0:1, 8:16], top[0:1, 8:16], imprun[0:1, 1, :]))
                    ve.tensor_scalar(topc[0:1, :], topi[0:1, :], float(NBLK - 1), None, ALU.min).then_inc(sel_ready, 1)

                def flip(name, bias):
                    dve.wait_ge(*filled(b, name))
                    ve.tensor_scalar(kdup[:, :, :, :],
                                     bank(name)[:, 0:NSEL * NPOS].rearrange("p (k s) -> p k s", s=NPOS)
                                     .unsqueeze(2).to_broadcast([128, NSEL, 2, NPOS]),
                                     col(bias), None, ALU.add).then_inc(read_sem(name), 1)
                    dve.wait_ge(*copied(b, name))
                    link(ve.transpose(kflip[:, :, :, :].rearrange("p k a s -> p (k a s)"),
                                      kdup[:, :, :, :].rearrange("p k a s -> p (k a s)")))
                    link(ve.tensor_scalar(khalf[:, :, :], kflip[:, :, 0, :], col("m0"), None, ALU.mult))

                def selected_keys():
                    flip("ks", "bk_s")
                    for h in range(HEADS):
                        p0, p1 = HD * h, HD * h + HD
                        last = ve.scalar_tensor_tensor(
                            out=kbd[p0:p1, h, :].rearrange("p (k i) -> p k i", i=NPOS), in0=kflip[p0:p1, :, 1, :],
                            scalar=col("m1", p0, p1), in1=khalf[p0:p1, :, :], op0=ALU.mult, op1=ALU.add)
                    last.then_inc(kbd_sel_ready, 1)
                    dve.wait_ge(kbd_sel_ready, b + 1)

                def selected_values():
                    flip("vs", "bv_s")
                    ve.scalar_tensor_tensor(
                        out=vselT[:, :].rearrange("p (k i) -> p k i", i=NPOS), in0=kflip[:, :, 1, :],
                        scalar=col("m1"), in1=khalf[:, :, :], op0=ALU.mult, op1=ALU.add).then_inc(vselT_ready, 1)

                dve.wait_ge(bias_in, 32)
                for g in range(NGRP + OW_LAG):
                    if g < NGRP:
                        n, np_ = group_shape(g)
                        k, m = g % 3, n * WTOK
                        dve.wait_ge(*filled(b, f"SW{g}"))
                        if n > HEADS:
                            ve.scalar_tensor_tensor(
                                out=tw[0:np_, k, 0:m].rearrange("p (a m) -> p a m", a=2),
                                in0=bank(f"SW{g}")[0:np_, 0:m].rearrange("p (a m) -> p a m", a=2), scalar=SCALE,
                                in1=wbias[0:np_, :, :].rearrange("p h m -> p (h m)").unsqueeze(1)
                                .to_broadcast([np_, 2, HEADS * WTOK]),
                                op0=ALU.mult, op1=ALU.add).then_inc(read_sem(f"SW{g}"), 1)
                        else:
                            ve.scalar_tensor_tensor(
                                out=tw[0:np_, k, 0:m], in0=bank(f"SW{g}")[0:np_, 0:m], scalar=SCALE,
                                in1=wbias[0:np_, :, :].rearrange("p h m -> p (h m)"),
                                op0=ALU.mult, op1=ALU.add).then_inc(read_sem(f"SW{g}"), 1)
                        dve.wait_ge(*copied(b, f"SW{g}"))
                        ve.tensor_reduce(nmw[0:np_, k, 0:n], tw[0:np_, k, 0:m].rearrange("p (a m) -> p a m", m=WTOK),
                                         AX.X, ALU.max, negate=True).then_inc(wmax_ready, 1)
                    if g == 0:
                        top_blocks()
                    if 1 <= g <= NGRP:
                        n, np_ = group_shape(g - 1)
                        k = (g - 1) % 3
                        dve.wait_ge(wexp_ready, b * NGRP + g)
                        link(ve.tensor_reduce(Zw[0:np_, k, 0:n],
                                              ew[0:np_, k, 0:n * WTOK].rearrange("p (a m) -> p a m", m=WTOK),
                                              AX.X, ALU.add))
                        ve.reciprocal(rZw[0:np_, k, 0:n], Zw[0:np_, k, 0:n]).then_inc(wrz_ready, 1)
                    if 0 <= g - OW_LAG < NGRP:
                        q = g - OW_LAG
                        dve.wait_ge(*filled(b, f"OW{q}"))
                        for w in range(4 * q, min(4 * q + 4, NWIN)):
                            r0, nr, c0, ncol = window(w)
                            last = ve.tensor_copy(
                                owT[:, :].rearrange("p (r c) -> p r c", c=W)[:, r0:r0 + nr, c0:c0 + ncol],
                                bank(f"OW{q}")[:, WTOK * (w % 4):WTOK * (w % 4) + WTOK]
                                .rearrange("p (r c) -> p r c", r=WS)[:, 0:nr, 0:ncol])
                        last.then_inc(read_sem(f"OW{q}"), 1)
                    if g == SEL_STEP + 1:
                        selected_keys()
                    if g == SEL_STEP + 2:
                        selected_values()
                tiles("s", 256, osT)
                branch_output("s", 1, osT)

                for t in range(NT):
                    dve.wait_ge(*filled(b, f"pj{t}"))
                    ve.tensor_tensor(pj[:, t % 2, :], bank(f"pj{t}")[:, 0:3 * C], rows[:, ROW_PROJ:ROW_PROJ + 3 * C],
                                     ALU.add).then_inc(read_sem(f"pj{t}"), 1)
                    dve.wait_ge(*copied(b, f"pj{t}"))
                    for i in range(3):
                        link(ve.scalar_tensor_tensor(
                            out=t_tok[:, t, :], in0=pj[:, t % 2, C * i:C * i + C], scalar=gtok[:, t, i:i + 1],
                            in1=(t_tok if i else x_tok)[:, t, :], op0=ALU.mult, op1=ALU.add))
                normalise(1, t_tok, xt_tok, EPS_T, xt_ready)
                dve.wait_ge(xt_ready, b * 2 + 2)
                normalise(2, xt_tok, xn_tok, EPS_T, xn_ready)

                dve.wait_ge(*filled(b, "rt"))
                ve.tensor_copy(lg[:, :, :].rearrange("p t e -> p (t e)"), bank("rt")[:, 0:NT * E])\
                  .then_inc(read_sem("rt"), 1)
                dve.wait_ge(*copied(b, "rt"))
                dve.nop(nofuse=True)
                for t in range(NT):
                    last = ve.max(lmax[:, t, :], lg[:, t, :])
                link(last)
                ve.tensor_tensor(ldif[:, 0, :], lmax[:, :, 1], lmax[:, :, 0], ALU.subtract).then_inc(ldif_ready, 1)
                for t in range(NT):
                    last = ve.max_index(lidx[:, t, :], lmax[:, t, :], lg[:, t, :])
                link(last)
                link(ve.tensor_copy(lidxf[:, :, :], lidx[:, :, 0:2]))
                for i in range(2):
                    last = ve.tensor_tensor(oneh[:, i, :, :],
                                            rows[:, ROW_IOTA:ROW_IOTA + E].unsqueeze(1).to_broadcast([128, NT, E]),
                                            lidxf[:, :, i:i + 1].to_broadcast([128, NT, E]), ALU.is_equal)
                dve.wait_ge(lexp_ready, b + 1)
                link(ve.tensor_scalar(ldif[:, 2, :], ldif[:, 1, :], 1.0, None, ALU.add))
                link(ve.reciprocal(wtop[:, 0, :], ldif[:, 2, :]))
                link(ve.tensor_tensor(wtop[:, 1, :], wtop[:, 0, :], ldif[:, 1, :], ALU.mult))
                for i in range(2):
                    last = ve.tensor_tensor(oneh[:, i, :, :], oneh[:, i, :, :],
                                            wtop[:, i, :].unsqueeze(2).to_broadcast([128, NT, E]), ALU.mult)
                link(last)
                ve.tensor_tensor(wtok[:, :, :], oneh[:, 0, :, :], oneh[:, 1, :, :], ALU.add).then_inc(wtok_ready, 1)
                dve.wait_ge(wtok_ready, b + 1)
                for i in range(2):
                    dve.wait_ge(*filled(b, f"be{i}"))
                    ve.tensor_tensor(acc[:, 4 * i:4 * i + 4, :].rearrange("p t c -> p (t c)"), bank(f"be{i}"),
                                     t_tok[:, 4 * i:4 * i + 4, :].rearrange("p t c -> p (t c)"), ALU.add)\
                      .then_inc(read_sem(f"be{i}"), 1)
                for i in range(2 * E + 2):
                    if i < 2 * E:
                        half, e = divmod(i, E)
                        dve.wait_ge(*copied(b, f"tn{half}"))
                        if i >= 2:
                            dve.wait_ge(*filled(b, f"h{i - 1}_0"))
                        ve.tensor_scalar(xe[:, i % 2, :], xnT[:, 512 * half:512 * half + 512],
                                         cols[:, COL_G + e:COL_G + e + 1], cols[:, COL_LB + e:COL_LB + e + 1],
                                         ALU.mult, ALU.add).then_inc(xe_ready, 1)
                    if i >= 2:
                        half, e = divmod(i - 2, E)
                        dve.wait_ge(*filled(b, f"y{i - 2}"))
                        dve.wait_ge(*copied(b, f"y{i - 3}" if i > 2 else "be1"))
                        for j in range(4):
                            t = 4 * half + j
                            last = ve.scalar_tensor_tensor(
                                out=acc[:, t, :], in0=bank(f"y{i - 2}")[:, C * j:C * j + C], scalar=wtok[:, t, e:e + 1],
                                in1=acc[:, t, :], op0=ALU.mult, op1=ALU.add)
                        last.then_inc(read_sem(f"y{i - 2}"), 1)
                assert links[0] == DVE_LINKS, links[0]

        @block.tensor
        def _(pe):
            mm, tr = nc.tensor.matmul, nc.tensor.transpose
            with pe.Fori(0, B) as b:

                def transposes(name, srcs, k, m):
                    pe.wait_ge(*free_for(b, name))
                    for j, src in enumerate(srcs):
                        last = tr(bank(name)[0:m, k * j:k * j + k], src, ident[0:k, 0:k])
                    last.then_inc(full_sem(name), 1)

                pe.wait_ge(const_in, 48)
                pe.wait_ge(x_in, b * 16 + 16)
                for i in range(2):
                    transposes(f"xt{i}", [x_sb[:, 512 * i + 128 * j:512 * i + 128 * j + 128] for j in range(4)], 128, 128)
                for i in range(2):
                    pe.wait_ge(xhat_tok_ready, b * 2 + i + 1)
                    transposes(f"xh{i}", [xhat_tok[:, 4 * i + j, :] for j in range(4)], 128, 128)
                pe.wait_ge(proj_in, 32)

                def project(name, weights, rhs, n, m=128):
                    pe.wait_ge(*free_for(b, name))
                    dst = bank(name)[0:m, 0:n]
                    mm(dst, weights, rhs, start=True, stop=True).then_inc(full_sem(name), 1)

                def pixels(i):
                    return xhatT[:, 16 * i:16 * i + 16, :]

                for i in range(2):
                    pe.wait_ge(*copied(b, f"xh{i}"))
                    project(f"kc{i}", qkvc_sb[:, C:2 * C], pixels(i), 512)
                for i in range(2):
                    project(f"vc{i}", qkvc_sb[:, 2 * C:3 * C], pixels(i), 512)
                for i in range(2):
                    project(f"qc{i}", qkvc_sb[:, 0:C], pixels(i), 512)
                pe.wait_ge(win_in, 32)
                for i in range(2):
                    project(f"gh{i}", gw1_sb[:, :], pixels(i), 512)
                pe.wait_ge(xwin_ready, b + 1)
                for name, k in (("kw", 1), ("qw", 0)):
                    for i, (w0, nw) in enumerate(WPARTS):
                        project(f"{name}{i}", qkvw_sb[:, C * k:C * k + C], xwin[:, w0:w0 + nw, :], nw * WTOK)
                for i in range(2):
                    pe.wait_ge(*copied(b, f"gh{i}"))
                    project(f"gz{i}", gw2_sb[:, :], gh[:, 512 * i:512 * i + 512], 512, m=3)
                for i in range(2):
                    pe.wait_ge(*copied(b, f"gz{i}"))
                pe.wait_ge(*free_for(b, "gt"))
                pe.nop(nofuse=True)
                for t in range(NT):
                    last = tr(bank("gt")[:, 3 * t:3 * t + 3], gz[0:3, 128 * t:128 * t + 128], ident[0:3, 0:3])
                last.then_inc(full_sem("gt"), 1)

                pe.wait_ge(wk_in, 16)
                pe.wait_ge(*free_for(b, "mk0"))
                pe.wait_ge(*free_for(b, "mk1"))
                for s in range(NPOS):
                    pe.wait_ge(kp_ready, b * NPOS + s + 1)
                    for a in range(2):
                        last = mm(bank(f"mk{a}")[:, 0:NB], w1k_sb[:, s, C * a:C * a + C], kp[:, s, :],
                                  start=(s == 0), stop=(s == NPOS - 1))
                        if s == NPOS - 1:
                            last.then_inc(full_sem(f"mk{a}"), 1)
                pe.wait_ge(wv_in, 16)
                for i in range(2):
                    pe.wait_ge(*copied(b, f"vc{i}"))
                for a in range(2):
                    pe.wait_ge(*free_for(b, f"mv{a}"))
                    for s in range(NPOS):
                        r, c = divmod(s, KS)
                        last = mm(bank(f"mv{a}")[:, 0:NB],
                                  w1v_sb[:, s, C * a:C * a + C], vcT[:, r:r + 2 * NBH - 1:2, c:c + 2 * NBH - 1:2],
                                  start=(s == 0), stop=(s == NPOS - 1))
                    last.then_inc(full_sem(f"mv{a}"), 1)
                pe.wait_ge(w2_in, 32)
                for a in range(2):
                    pe.wait_ge(*copied(b, f"mk{a}"))
                pe.wait_ge(*free_for(b, "k2"))
                for a in range(2):
                    last = mm(bank("k2")[:, 0:NB], w2k_sb[:, a, :], hk[:, a, :], start=(a == 0), stop=(a == 1))
                last.then_inc(full_sem("k2"), 1)
                for g in range(NGRP):
                    pe.wait_ge(*free_for(b, f"vw{g}"))
                    for w in range(4 * g, min(4 * g + 4, NWIN)):
                        last = mm(bank(f"vw{g}")[0:WTOK, C * (w % 4):C * (w % 4) + C], xwin[:, w, :],
                                  qkvw_sb[:, 2 * C:3 * C], start=True, stop=True)
                    last.then_inc(full_sem(f"vw{g}"), 1)
                for a in range(2):
                    pe.wait_ge(*copied(b, f"mv{a}"))
                pe.wait_ge(*free_for(b, "v2"))
                for i, m in enumerate((M0, M1)):
                    for a in range(2):
                        last = mm(bank("v2")[0:m, C * i:C * i + C], hv[:, a, M0 * i:M0 * i + m], w2v_sb[:, a, :],
                                  start=(a == 0), stop=(a == 1))
                last.then_inc(full_sem("v2"), 1)

                def branch_output(s, i, chunks):
                    for k in "ab":
                        pe.wait_ge(*copied(b, f"T{s}{4 * i + 3}{k}"))
                    name = f"O{s}{i}"
                    pe.wait_ge(*free_for(b, name))
                    for a, m in enumerate(chunks):
                        for h in range(HEADS):
                            last = mm(bank(name)[HD * h:HD * h + HD, :], v_sb[0:m, a, HD * h:HD * h + HD],
                                      PT[0:m, a, h, 512 * i:512 * i + 512], start=(a == 0), stop=(a == 1))
                    last.then_inc(full_sem(name), 1)

                def tiles(s, base, chunks):
                    mk = sum(chunks)
                    for t in range(NT + 1):
                        if t < NT:
                            for k in range(2):
                                name = f"S{s}{t}{'ab'[k]}"
                                pe.wait_ge(*free_for(b, name))
                                mm(bank(name)[:, 0:2 * mk], qT[:, 128 * t:128 * t + 128],
                                   kbd[:, 2 * k:2 * k + 2, 0:mk], start=True, stop=True).then_inc(full_sem(name), 1)
                        if t >= 1:
                            pe.wait_ge(prob_ready, b * 2 * NT + base + t)
                            for a, m in enumerate(chunks):
                                name = f"T{s}{t - 1}{'ab'[a]}"
                                transposes(name, [Pb[:, (t - 1) % 2, h, M0 * a:M0 * a + m] for h in range(HEADS)], 128, m)
                        if t == O_LAG:
                            branch_output(s, 0, chunks)

                pe.wait_ge(*copied(b, "qc1"))
                pe.wait_ge(*copied(b, "k2"))
                pe.wait_ge(*copied(b, "v2"))
                tiles("c", 0, (M0, M1))
                pe.wait_ge(tail_in, 64)
                for i in range(2):
                    project(f"qs{i}", qkvs_sb[:, 0:C], pixels(i), 512)
                branch_output("c", 1, (M0, M1))

                for i in range(len(WPARTS)):
                    pe.wait_ge(*copied(b, f"kw{i}"))
                    pe.wait_ge(*copied(b, f"qw{i}"))
                pe.wait_ge(*copied(b, f"vw{NGRP - 1}"))
                pe.nop(nofuse=True)
                for g in range(NGRP + OW_LAG):
                    if g < NGRP:
                        pe.wait_ge(*free_for(b, f"SW{g}"))
                        for i, p in enumerate(pairs_of(g)):
                            for j, w in enumerate(windows_of(p)):
                                last = mm(bank(f"SW{g}")[64 * j:64 * j + WTOK, HEADS * WTOK * i:HEADS * WTOK * (i + 1)],
                                          qwT[:, WTOK * w:WTOK * w + WTOK], kbdw[:, :, WTOK * w:WTOK * w + WTOK],
                                          start=True, stop=True)
                        last.then_inc(full_sem(f"SW{g}"), 1)
                    if g == 0:
                        pe.wait_ge(impcol_ready, b + 1)
                        pe.wait_ge(*free_for(b, "imp"))
                        mm(bank("imp")[0:1, 0:M0], impcol[:, 0:1], ident[:, :], start=True, stop=True)
                        mm(bank("imp")[0:1, M0:NB], impcol[0:M1, 1:2], ident[0:M1, 0:M1], start=True, stop=True)\
                            .then_inc(full_sem("imp"), 1)
                    if 0 <= g - PW_LAG < NGRP:
                        q = g - PW_LAG
                        pe.wait_ge(wprob_ready, b * NGRP + q + 1)
                        for i, p in enumerate(pairs_of(q)):
                            np_ = pair_rows(p)
                            pe.wait_ge(*free_for(b, f"PW{p}"))
                            pe.nop(nofuse=True)
                            for h in range(HEADS):
                                o = (HEADS * i + h) * WTOK
                                last = tr(bank(f"PW{p}")[0:WTOK, 128 * h:128 * h + np_],
                                          ew[0:np_, q % 3, o:o + WTOK], ident[0:np_, 0:np_])
                            last.then_inc(full_sem(f"PW{p}"), 1)
                    if 0 <= g - OW_LAG < NGRP:
                        q = g - OW_LAG
                        pe.wait_ge(*free_for(b, f"OW{q}"))
                        for i, p in enumerate(pairs_of(q)):
                            pe.wait_ge(*copied(b, f"PW{p}"))
                            pe.nop(nofuse=True)
                            for j, w in enumerate(windows_of(p)):
                                for h in range(HEADS):
                                    last = mm(bank(f"OW{q}")[HD * h:HD * h + HD, WTOK * (w % 4):WTOK * (w % 4) + WTOK],
                                              vw[:, w, HD * h:HD * h + HD], ptw[0:WTOK, p % 4, h, 64 * j:64 * j + WTOK],
                                              start=True, stop=True)
                        last.then_inc(full_sem(f"OW{q}"), 1)
                    if g == SEL_STEP:
                        pe.wait_ge(xg_ready, b + 1)
                        for name, k in (("ks", 1), ("vs", 2)):
                            project(name, qkvs_sb[:, C * k:C * k + C],
                                    xg[:, :, :].rearrange("p k s -> p (k s)"), NSEL * NPOS)
                pe.wait_ge(vselT_ready, b + 1)
                transposes("vt", [vselT[:, 128 * a:128 * a + 128] for a in range(2)], 128, 128)

                for i in range(2):
                    pe.wait_ge(*copied(b, f"qs{i}"))
                pe.wait_ge(kbd_sel_ready, b + 1)
                pe.wait_ge(*copied(b, "vt"))
                tiles("s", NT, (128, 128))
                branch_output("s", 1, (128, 128))

                pe.wait_ge(*copied(b, "Oc1"))
                pe.wait_ge(*copied(b, "Os1"))
                pe.wait_ge(*copied(b, f"OW{NGRP - 1}"))
                for t in range(NT):
                    name = f"pj{t}"
                    pe.wait_ge(*free_for(b, name))
                    for i, src in enumerate((ocT[:, 128 * t:128 * t + 128], osT[:, 128 * t:128 * t + 128],
                                             owT[:, 128 * t:128 * t + 128])):
                        last = mm(bank(name)[:, C * i:C * i + C], src, proj_sb[:, i, :], start=True, stop=True)
                    last.then_inc(full_sem(name), 1)
                for k, (name, src, ready) in enumerate((("tt", xt_tok, xt_ready), ("tn", xn_tok, xn_ready))):
                    for i in range(2):
                        pe.wait_ge(ready, b * 2 + i + 1)
                        transposes(f"{name}{i}", [src[:, 4 * i + j, :] for j in range(4)], 128, 128)
                for i in range(2):
                    pe.wait_ge(*copied(b, f"tt{i}"))
                    project(f"rl{i}", wr_sb[:, :], xtT[:, 512 * i:512 * i + 512], 512, m=E)
                for i in range(2):
                    pe.wait_ge(*copied(b, f"rl{i}"))
                pe.wait_ge(*free_for(b, "rt"))
                pe.nop(nofuse=True)
                for t in range(NT):
                    last = tr(bank("rt")[:, E * t:E * t + E], gz[0:E, 128 * t:128 * t + 128], ident[0:E, 0:E])
                last.then_inc(full_sem("rt"), 1)
                pe.wait_ge(wtok_ready, b + 1)
                for i in range(2):
                    transposes(f"wt{i}", [wtok[:, 4 * i + j, :] for j in range(4)], 128, E)
                for i in range(2):
                    pe.wait_ge(*copied(b, f"wt{i}"))
                    pe.wait_ge(*free_for(b, f"be{i}"))
                    for j in range(4):
                        t = 4 * i + j
                        last = mm(bank(f"be{i}")[:, C * j:C * j + C], gz[0:E, 128 * t:128 * t + 128], fb2_sb[:, :],
                                  start=True, stop=True)
                    last.then_inc(full_sem(f"be{i}"), 1)
                pe.wait_ge(ffn_in, 32)
                for i in range(2 * E + 1):
                    if i < 2 * E:
                        pe.wait_ge(xe_ready, b * 2 * E + i + 1)
                        for c in range(HC):
                            project(f"h{i}_{c}", fw1_sb[:, i % E, 128 * c:128 * c + 128], xe[:, i % 2, :], 512)
                    if i >= 1:
                        name = f"y{i - 1}"
                        for c in range(HC):
                            pe.wait_ge(*copied(b, f"h{i - 1}_{c}"))
                        pe.wait_ge(*free_for(b, name))
                        for j in range(4):
                            for c in range(HC):
                                last = mm(bank(name)[:, C * j:C * j + C], hT[:, (i - 1) % 2, c, 128 * j:128 * j + 128],
                                          fw2_sb[:, (i - 1) % E, c, :], start=(c == 0), stop=(c == HC - 1))
                        last.then_inc(full_sem(name), 1)
                for i in range(2):
                    pe.wait_ge(*copied(b, f"y{(i + 1) * E - 1}"))
                    transposes(f"out{i}", [acc[:, 4 * i + j, :] for j in range(4)], 128, 128)


def kernel(**inputs):
    import numpy as np
    import concourse.bacc as bacc
    from concourse.bass_utils import run_bass_kernel_spmd

    p = {k.replace("L0_conv_", "").replace("L0_ffn_", "f_"): np.asarray(v) for k, v in inputs.items()}
    cols = np.zeros((128, NCOL), np.float32)

    def put(name, v):
        v = v.reshape(-1)
        cols[:v.size, COL[name]] = v

    L = C // NPOS
    ws = p["qkv_slc_w"].reshape(C, 3, NPOS, L)
    wqkv_s = np.concatenate([ws[:, 0].reshape(C, C), ws[:, 1].transpose(0, 2, 1).reshape(C, C),
                             ws[:, 2].transpose(0, 2, 1).reshape(C, C)], axis=1)
    for s, k in (("c", "cmp"), ("s", "slc"), ("w", "win")):
        bias = p[f"qkv_{k}_b" if s != "w" else "win_qkv_b"]
        put(f"bq_{s}", bias[0:C])
        if s != "s":
            put(f"bk_{s}", bias[C:2 * C])
        if s == "c":
            put("bv_c", bias[2 * C:])
        if s == "s":
            put("bk_s", bias[C:2 * C].reshape(NPOS, L).T)
            put("bv_s", bias[2 * C:].reshape(NPOS, L).T)
    for a in range(2):
        put(f"b1k{a}", p["cmpk_b1"][C * a:C * a + C])
        put(f"b1v{a}", p["cmpv_b1"][C * a:C * a + C])
    put("b2k", p["cmpk_b2"])
    put("gate_b1", p["gate_b1"])
    put("gate_b2", p["gate_b2"])
    put("br", p["f_br"])
    half = (np.arange(128) // NPOS) % 2
    cols[:, COL["m0"]] = half == 0
    cols[:, COL["m1"]] = half == 1
    cols[:, COL_B1:COL_B1 + E * HC] = p["f_b1"].reshape(E * HC, 128).T
    cols[:, COL_G:COL_G + E] = p["f_ln_g"].T
    cols[:, COL_LB:COL_LB + E] = p["f_ln_b"].T
    cols[:, COL_POS:] = p["pos_embed"].reshape(C, NPOS)
    rows = np.zeros((1, NROW), np.float32)
    rows[0, ROW_BVW:ROW_BVW + C] = p["win_qkv_b"][2 * C:]
    rows[0, ROW_B2V:ROW_B2V + C] = p["cmpv_b2"]
    rows[0, ROW_PROJ:ROW_PROJ + 3 * C] = np.concatenate([p["proj_cmp_b"], p["proj_slc_b"], p["win_proj_b"]])
    rows[0, ROW_IOTA:ROW_IOTA + E] = np.arange(E)
    flipped = p["win_bias_table"].reshape(SIDE, SIDE, HEADS)[::-1, ::-1].transpose(2, 0, 1)
    arrays = {
        "x": p["x"].reshape(B, C, N),
        "wqkv_c": p["qkv_cmp_w"], "wqkv_s": wqkv_s, "wqkv_w": p["win_qkv_w"],
        "w1k": p["cmpk_w1"], "w1v": p["cmpv_w1"], "w2k": p["cmpk_w2"], "w2v": p["cmpv_w2"],
        "gate_w1": p["gate_w1"], "gate_w2": p["gate_w2"],
        "projs": np.stack([p["proj_cmp_w"], p["proj_slc_w"], p["win_proj_w"]]),
        "wr": p["f_Wr"], "fw1": p["f_W1"], "fw2": p["f_W2"], "fb2": p["f_b2"],
        "bias_tab": np.stack([flipped[:, WS - 1 - r:SIDE - r, WS - 1 - c:SIDE - c].reshape(-1)
                              for r in range(WS) for c in range(WS)]),
        "cols_d": cols, "rows_d": rows, "ident_d": np.eye(128, dtype=np.float32),
    }
    arrays = {k: np.ascontiguousarray(v) for k, v in arrays.items()}
    nc = bacc.Bacc("TRN2", target_bir_lowering=False, num_devices=1)
    aps = {k: nc.dram_tensor(k, v.shape, F32, kind="ExternalInput").ap() for k, v in arrays.items()}
    out = nc.dram_tensor("out", (B, C, N), F32, kind="ExternalOutput").ap()
    build(nc, out=out, **aps)
    got = run_bass_kernel_spmd(nc, [arrays], core_ids=[0])
    return got.results[0]["out"].reshape(B, C, H, W)
```

```python
import concourse.bass as bass
from concourse import mybir
from contextlib import ExitStack

F32 = mybir.dt.float32
U32 = mybir.dt.uint32
ALU = mybir.AluOpType
ACT = mybir.ActivationFunctionType
AX = mybir.AxisListType

B, C, H, W = 4, 128, 32, 32
N = H * W
NT = N // 128
HEADS, HD = 4, 32
SCALE = HD ** -0.5
KS = 4
NPOS = KS * KS
NBH = (H - KS) // 2 + 1
NB = NBH * NBH
M0, M1 = 128, NB - 128
NSEL = 16
NBLK = (H // KS) * (W // KS)
WS = 7
GRID = 5
WTOK = WS * WS
GH = C // 4
SIDE = 2 * WS - 1
NWIN = GRID * GRID
NPAIR = (NWIN + 1) // 2
NGRP = (NPAIR + 1) // 2
E, HF = 8, 512
HC = HF // 128
EPS_C, EPS_T = 1e-6, 1e-5
T_LAG = 2
NRING = T_LAG + 1
O_LAG = 6
PW_LAG, OW_LAG = 2, 3
SEL_STEP = NGRP - 1
WPARTS = [(0, 10), (10, 10), (20, 5)]

ROW = C + 2
CAP = B * N + 128
NTILE = 2 * B * N // 128 + E
AHEAD = 2
NTAB = NTILE + 4
NPAD = NTAB - 2 * B * N // 128
ZROWS = 2 * B * N + (E + NPAD) * 128
O_B1, O_G, O_LB = HF, HF + HC, HF + HC + 1
W1X = HF + HC + 2
WPK = W1X + HC * C
TSTEP = 32

COLS = ["bq_c", "bk_c", "bv_c", "bq_s", "bk_s", "bv_s", "bq_w", "bk_w", "b1k0", "b1k1", "b1v0", "b1v1",
        "b2k", "gate_b1", "gate_b2", "br", "m0", "m1", "j", "j128"]
COL = {n: i for i, n in enumerate(COLS)}
COL_POS = len(COLS)
COL_DEST = COL_POS + NPOS
NCOL = COL_DEST + 2 * NT
ROW_BVW, ROW_B2V, ROW_PROJ, ROW_IOTA, ROW_BASE, ROW_STEP = 0, 128, 256, 640, 648, 656
NROW = ROW_STEP + TSTEP


def psum_plan():
    plan, uses, at = {}, [0] * 8, [0]

    def fill(*names, pair=False):
        if pair and at[0] % 2:
            at[0] += 1
        for name in names:
            bank = at[0] % 8
            plan[name] = (bank, uses[bank])
            uses[bank] += 1
            at[0] += 1

    fill("xt0", "xt1", "xh0", "xh1", "kc0", "kc1", "vc0", "vc1", "qc0", "qc1", "gh0", "gh1",
         "kw0", "kw1", "kw2", "qw0", "qw1", "qw2", "gz0", "gz1", "gt", "mk0", "mk1", "mv0", "mv1", "k2")
    fill(*(f"vw{g}" for g in range(NGRP)))
    fill("v2")
    for s in "cs":
        for t in range(NT + T_LAG):
            if t < NT:
                fill(f"S{s}{t}a", f"S{s}{t}b", pair=True)
            if t >= T_LAG:
                fill(f"T{s}{t - T_LAG}a", f"T{s}{t - T_LAG}b")
            if t == O_LAG:
                fill(f"O{s}0")
        if s == "c":
            fill("qs0", "qs1", "Oc1")
            for g in range(NGRP + OW_LAG):
                if g < NGRP:
                    fill(f"SW{g}")
                if g == 0:
                    fill("imp")
                if 0 <= g - PW_LAG < NGRP:
                    fill(*(f"PW{p}" for p in pairs_of(g - PW_LAG)))
                if 0 <= g - OW_LAG < NGRP:
                    fill(f"OW{g - OW_LAG}")
                if g == SEL_STEP:
                    fill("ks", "vs")
            fill("vt")
        else:
            fill("Os1")
    fill(*(f"pj{t}" for t in range(NT)))
    fill("tt0", "tt1", "rl0", "rl1", "rt", "rk")
    return plan, uses


def pairs_of(g):
    return [p for p in (2 * g, 2 * g + 1) if p < NPAIR]


def pair_rows(p):
    return 64 * (len(windows_of(p)) - 1) + WTOK


def group_shape(g):
    return HEADS * len(pairs_of(g)), pair_rows(2 * g)


def windows_of(p):
    return [w for w in (2 * p, 2 * p + 1) if w < NWIN]


def build(nc, x, wqkv_c, wqkv_s, wqkv_w, w1k, w1v, w2k, w2v, gate_w1, gate_w2, projs, wr, fw1, fw2, fb1,
          fgb, fb2, bias_tab, cols_d, rows_d, ident_d, before_d, pad_d, xs_d, z_d, t_d, out):
    plan, uses = psum_plan()
    DVE_LINKS = 80

    with ExitStack() as ctx:
        def sb(name, shape, dt=F32):
            return ctx.enter_context(nc.sbuf_tensor(name, shape, dt))

        def sem(name):
            return ctx.enter_context(nc.semaphore(name))

        qkvc_sb = sb("qkvc_sb", [128, 3 * C])
        qkvs_sb = sb("qkvs_sb", [128, 3 * C])
        qkvw_sb = sb("qkvw_sb", [128, 3 * C])
        w1k_sb = sb("w1k_sb", [128, NPOS, 2 * C])
        w1v_sb = sb("w1v_sb", [128, NPOS, 2 * C])
        w2k_sb = sb("w2k_sb", [128, 2, C])
        w2v_sb = sb("w2v_sb", [128, 2, C])
        gw1_sb = sb("gw1_sb", [128, 128])
        gw2_sb = sb("gw2_sb", [128, 3])
        proj_sb = sb("proj_sb", [128, 3, C])
        wr_sb = sb("wr_sb", [128, E])
        fw_sb = sb("fw_sb", [128, E, WPK])
        before = sb("before", [128, 128])
        ones = sb("ones", [128, 128])
        wbias = sb("wbias", [128, HEADS, WTOK])
        cols = sb("cols", [128, NCOL])
        rows = sb("rows", [128, NROW])
        ident = sb("ident", [128, 128])
        minus_half = sb("minus_half", [128, NT])

        def col(name, p0=0, p1=128):
            return cols[p0:p1, COL[name]:COL[name] + 1]

        x_sb = sb("x_sb", [128, N])
        x_tok = sb("x_tok", [128, NT, C])
        r_xhat = sb("r_xhat", [128, N])
        xhat_tok = r_xhat[:, :].rearrange("p (t c) -> p t c", t=NT)
        osT = r_xhat
        xhatT = sb("xhatT", [128, H, W])
        xblk = sb("xblk", [128, NBLK, NPOS])
        xwin = sb("xwin", [128, NWIN, WTOK])
        r_kc = sb("r_kc", [128, N])
        kcT = r_kc[:, :].rearrange("p (r c) -> p r c", r=H)
        ocT = r_kc
        r_vc = sb("r_vc", [128, N])
        vcT = r_vc[:, :].rearrange("p (r c) -> p r c", r=H)
        owT = r_vc
        qT = sb("qT", [128, N])
        r_gh = sb("r_gh", [128, N])
        gh = r_gh
        hk = r_gh[:, 0:2 * NB].rearrange("p (a m) -> p a m", a=2)
        hv = r_gh[:, 2 * NB:4 * NB].rearrange("p (a m) -> p a m", a=2)
        r_kp = sb("r_kp", [128, NPOS * NB])
        kp = r_kp[:, :].rearrange("p (s m) -> p s m", s=NPOS)
        vw = r_kp[0:WTOK, 0:NWIN * C].rearrange("p (w c) -> p w c", w=NWIN)
        kbdw = sb("kbdw", [128, HEADS, NWIN * WTOK])
        kbd = sb("kbd", [128, HEADS, 256])
        qwT = sb("qwT", [128, NWIN * WTOK])
        v_sb = sb("v_sb", [128, 2, C])
        r_P = sb("r_P", [128, 2 * HEADS * 256])
        Pb = [v.rearrange("p (h m) -> p h m", h=HEADS)
              for v in (r_P[:, 0:HEADS * 256], r_P[:, HEADS * 256:2 * HEADS * 256], r_gh[:, :])]
        t_tok = r_P[:, 0:N].rearrange("p (t c) -> p t c", t=NT)
        R = sb("R", [128, 2 * HEADS * N])
        PT = R[:, :].rearrange("p (a h n) -> p a h n", a=2, h=HEADS)
        at = [0]

        def part(n):
            at[0] += n
            return R[:, at[0] - n:at[0]]

        tw = part(3 * 392).rearrange("p (r n) -> p r n", r=3)
        ew = part(3 * 392).rearrange("p (r n) -> p r n", r=3)
        ptw = part(4 * 512).rearrange("p (r h n) -> p r h n", r=4, h=HEADS)
        xg = part(NSEL * NPOS).rearrange("p (k s) -> p k s", k=NSEL)
        kdup = part(2 * NSEL * NPOS).rearrange("p (k a s) -> p k a s", k=NSEL, a=2)
        kflip = part(2 * NSEL * NPOS).rearrange("p (k a s) -> p k a s", k=NSEL, a=2)
        khalf = part(NSEL * NPOS).rearrange("p (k s) -> p k s", k=NSEL)
        vselT = part(NSEL * NPOS)
        at[0] = 0
        gz = R[:, 0:N]
        at[0] = N
        pj = part(6 * C).rearrange("p (r n) -> p r n", r=2)
        xtT = part(N)
        pay = part(2 * NT * ROW).rearrange("p (k t c) -> p k t c", k=2, t=NT)
        xt_tok = r_xhat[:, :].rearrange("p (t c) -> p t c", t=NT)
        at[0] = 0
        wx = part(4 * W1X).rearrange("p (r n) -> p r n", r=4)
        xrow = part(4 * ROW).rearrange("p (r n) -> p r n", r=4)
        wd = part(4 * 2).rearrange("p (r n) -> p r n", r=4)
        xe = part(2 * C).rearrange("p (r n) -> p r n", r=2)
        hT = part(2 * HF).rearrange("p (r c n) -> p r c n", r=2, c=HC)
        yb = part(2 * C).rearrange("p (r n) -> p r n", r=2)
        yrow = part(4 * C).rearrange("p (r n) -> p r n", r=4)
        at[0] = 2 * N + 6 * C + 2 * NT * ROW
        steps = part(E * TSTEP).rearrange("p (e s) -> p e s", e=E)
        cnt = part(E)
        ntl = part(E)
        upto = part(E)
        past = part(2 * E)[0:NTAB, :].rearrange("p (k e) -> p k e", k=2)
        tab = part(2)[0:NTAB, :]
        tabf = part(2)
        tab_i = part(2 * NTAB)[0:1, :].bitcast(U32).rearrange("p (k j) -> p k j", k=2)
        tailf = part(E)[0:1, :]
        tail_i = part(E)[0:1, :].bitcast(U32)
        t_all = w1k_sb[:, :, :].rearrange("p s n -> p (s n)")
        b2_all = w1v_sb[:, 0:4, :].rearrange("p s n -> p (s n)")
        zz = kbdw[:, :, :].rearrange("p h m -> p (h m)")[:, 0:4 * N].rearrange("p (r k n) -> p r k n", r=2, k=2)
        xo = w1v_sb[:, 4:12, :].rearrange("p s n -> p (s n)").rearrange("p (r n) -> p r n", r=2)
        stats = sb("stats", [128, NT, 6])
        mv = sb("mv", [128, NT, 2])
        rstd = sb("rstd", [128, NT])
        vpe = sb("vpe", [128, NT])
        gtok = sb("gtok", [128, NT, 3])
        ge = sb("ge", [128, NT, 3])
        nmx = sb("nmx", [128, NRING, HEADS])
        Z = sb("Z", [128, NRING, HEADS])
        rZ = sb("rZ", [128, NRING, HEADS])
        nmw = sb("nmw", [128, 3, 2 * HEADS])
        Zw = sb("Zw", [128, 3, 2 * HEADS])
        rZw = sb("rZw", [128, 3, 2 * HEADS])
        impacc = sb("impacc", [128, 2, NT])
        impcol = sb("impcol", [128, 2])
        imprun = sb("imprun", [1, 2, NB])
        top = sb("top", [1, 16])
        topi = sb("topi", [1, 16], U32)
        topc = sb("topc", [1, 16], U32)
        lg = sb("lg", [128, NT, E])
        lmax = sb("lmax", [128, NT, 8])
        lidx = sb("lidx", [128, NT, 8], U32)
        lidxf = sb("lidxf", [128, NT, 2])
        ldif = sb("ldif", [128, 3, NT])
        wtop = sb("wtop", [128, 2, NT])
        oneh = sb("oneh", [128, 2, NT, E])
        picks = sb("picks", [128, NT, E])
        cum = sb("cum", [128, NT + 1, E])
        token = sb("token", [1, 1])
        rkb = sb("rkb", [128, NT, E])
        posf = sb("posf", [128, 2, NT])
        pos = sb("pos", [128, 2 * NT], U32)
        dest = sb("dest", [128, 2 * NT])

        ps = ctx.enter_context(nc.psum_tensor("ps", [128, 8 * 512], F32))

        bank_full = [sem(f"bank_full{i}") for i in range(8)]
        bank_read = [sem(f"bank_read{i}") for i in range(8)]
        const_in, proj_in, wk_in, wv_in = sem("const_in"), sem("proj_in"), sem("wk_in"), sem("wv_in")
        w2_in, win_in, tail_in, ffn_in = sem("w2_in"), sem("win_in"), sem("tail_in"), sem("ffn_in")
        bias_in = sem("bias_in")
        x_in, out_done = sem("x_in"), [sem(f"out_done{i}") for i in range(2)]
        zeroed = sem("zeroed")
        var_ready, rstd_ready = sem("var_ready"), sem("rstd_ready")
        xhat_tok_ready, xblk_ready = sem("xhat_tok_ready"), sem("xblk_ready")
        xwin_ready = sem("xwin_ready")
        kp_ready, gz_exp_ready, g_ready = sem("kp_ready"), sem("gz_exp_ready"), sem("g_ready")
        max_ready, prob_ready = sem("max_ready"), sem("prob_ready")
        impcol_ready, sel_ready, xg_in = sem("impcol_ready"), sem("sel_ready"), sem("xg_in")
        kbd_sel_ready, vselT_ready = sem("kbd_sel_ready"), sem("vselT_ready")
        wmax_ready, wsub_ready, wexp_ready = sem("wmax_ready"), sem("wsub_ready"), sem("wexp_ready")
        wrz_ready, wprob_ready = sem("wrz_ready"), sem("wprob_ready")
        xt_ready, xn_ready = sem("xt_ready"), sem("xn_ready")
        ldif_ready, lexp_ready, picks_ready = sem("ldif_ready"), sem("lexp_ready"), sem("picks_ready")
        t_ready, t_stored = sem("t_ready"), sem("t_stored")
        pay_ready, pay2_ready, scattered = sem("pay_ready"), sem("pay2_ready"), sem("scattered")
        dve_done = sem("dve_done")
        cnt_full, cnt_ready, table_step = sem("cnt_full"), sem("cnt_ready"), sem("table_step")
        tail_ready, tab_ready, tab_full, table_in = sem("tail_ready"), sem("tab_ready"), sem("tab_full"), sem("table_in")
        pad_in, t_in = sem("pad_in"), sem("t_in")
        xrow_in = [sem(f"xrow_in{i}") for i in range(4)]
        tr_full, xe_ready, h_full, h_ready = sem("tr_full"), sem("xe_ready"), sem("h_full"), sem("h_ready")
        y_full, yb_ready, y_ready, wd_ready = sem("y_full"), sem("yb_ready"), sem("y_ready"), sem("wd_ready")
        y_out = [sem(f"y_out{i}") for i in range(4)]
        zz_in = [sem(f"zz_in{i}") for i in range(2)]
        sum_half, sum_ready, wx_ready, dest_ready, res_full, xo_ready, place_free = (
            sem(n) for n in ("sum_half", "sum_ready", "wx_ready", "dest_ready", "res_full", "xo_ready", "place_free"))

        def bank(name):
            k = plan[name][0]
            return ps[:, 512 * k:512 * k + 512]

        def free_for(b, name):
            k, n = plan[name]
            return bank_read[k], b * uses[k] + n + 1

        def filled(b, name):
            k, n = plan[name]
            return bank_full[k], b * uses[k] + n + 1

        def copied(b, name):
            k, n = plan[name]
            return bank_read[k], b * uses[k] + n + 2

        def full_sem(name):
            return bank_full[plan[name][0]]

        def read_sem(name):
            return bank_read[plan[name][0]]

        def window(w):
            r, c = divmod(w, GRID)
            return WS * r, min(WS, H - WS * r), WS * c, min(WS, W - WS * c)

        def keys_to_blocks(eng, ops, b, i):
            w0, nw = WPARTS[i]
            name = f"kw{i}"
            eng.wait_ge(zeroed, 7)
            eng.wait_ge(*filled(b, name))
            for h in range(HEADS):
                p0, p1 = HD * h, HD * h + HD
                dst = kbdw[p0:p1, h, w0 * WTOK:(w0 + nw) * WTOK]
                src = bank(name)[p0:p1, 0:nw * WTOK]
                if ops is nc.scalar:
                    last = ops.activation(dst, src, ACT.Identity, bias=col("bk_w", p0, p1))
                else:
                    last = ops.tensor_scalar(dst, src, col("bk_w", p0, p1), None, ALU.add)
            last.then_inc(read_sem(name), 1)

        def hid(r):
            return ps[:, 512 * (2 + r % 2):512 * (2 + r % 2) + 512]

        def turned(r):
            return ps[:, 512 * (r % 2):512 * (r % 2) + C]

        def outputs(r):
            return ps[:, 512 * (4 + r % 2):512 * (4 + r % 2) + C]

        block = ctx.enter_context(nc.Block())

        @block.sync
        def _(sp):
            sp.dma_start(x_sb[:, :], x[0, :, :]).then_inc(x_in, 16)
            sp.dma_start(ident[:, :], ident_d).then_inc(const_in, 16)
            sp.dma_start(cols[:, :], cols_d).then_inc(const_in, 16)
            sp.dma_start(rows[:, :], rows_d[0, :].partition_broadcast(128)).then_inc(const_in, 16)
            sp.dma_start(qkvc_sb[:, :], wqkv_c).then_inc(proj_in, 16)
            sp.dma_start(qkvw_sb[:, :], wqkv_w).then_inc(proj_in, 16)
            sp.wait_ge(zeroed, 5)
            for j in range(2):
                sp.dma_start(wbias[64 * j:64 * j + WTOK, :, :].rearrange("p h m -> p (h m)"), bias_tab).then_inc(bias_in, 16)
            sp.dma_start(w1k_sb[:, :, :], w1k.rearrange("(c s) n -> c s n", s=NPOS)).then_inc(wk_in, 16)
            sp.dma_start(w1v_sb[:, :, :], w1v.rearrange("(c s) n -> c s n", s=NPOS)).then_inc(wv_in, 16)
            sp.dma_start(w2k_sb[:, :, :], w2k.rearrange("(a p) n -> p a n", p=128)).then_inc(w2_in, 16)
            sp.dma_start(w2v_sb[:, :, :], w2v.rearrange("(a p) n -> p a n", p=128)).then_inc(w2_in, 16)
            sp.dma_start(qkvs_sb[:, :], wqkv_s).then_inc(tail_in, 16)
            sp.dma_start(proj_sb[:, :, :], projs.rearrange("a p n -> p a n")).then_inc(tail_in, 16)
            sp.dma_start(wr_sb[:, :], wr).then_inc(tail_in, 16)
            sp.dma_start(before[:, :], before_d).then_inc(tail_in, 16)
            sp.dma_start(fw_sb[:, :, 0:HF], fw1.rearrange("e p n -> p e n")).then_inc(ffn_in, 16)
            for c in range(HC):
                sp.dma_start(fw_sb[:, :, W1X + C * c:W1X + C * c + C],
                             fw2[:, C * c:C * c + C, :].rearrange("e p n -> p e n")).then_inc(ffn_in, 16)
            sp.dma_start(fw_sb[:, :, O_B1:O_B1 + HC], fb1).then_inc(ffn_in, 16)
            sp.dma_start(fw_sb[:, :, O_G:O_G + 2], fgb).then_inc(ffn_in, 16)
            sp.dma_start(xs_d[E * CAP:E * CAP + NPAD * 128, :], pad_d[E * 128:(E + NPAD) * 128, :]).then_inc(pad_in, 16)

            def select_tokens(b):
                sp.wait_ge(xblk_ready, b + 1)
                sp.wait_ge(sel_ready, b + 1)
                sp.nop(nofuse=True)
                for i in range(NSEL):
                    idx = sp.value_load(topc[0:1, i:i + 1], min_val=0, max_val=NBLK - 1)
                    sp.dma_start(xg[:, i, :], xblk[:, bass.ds(idx, 1), :].rearrange("p a s -> p (a s)")).then_inc(xg_in, 16)

            def store_t(b):
                sp.wait_ge(t_ready, b + 1)
                sp.dma_start(t_d[bass.ds(b, 1), :, :].rearrange("a p n -> (a p) n") if not isinstance(b, int) else t_d[b, :, :],
                             r_P[:, 0:N]).then_inc(t_stored, 16)

            with sp.Fori(1, B) as b:
                sp.wait_ge(*filled(b - 1, "xt1"))
                sp.dma_start(x_sb[:, :], x[bass.ds(b, 1), :, :].rearrange("a p n -> (a p) n")).then_inc(x_in, 16)
                select_tokens(b - 1)
                store_t(b - 1)
            select_tokens(B - 1)
            sp.wait_ge(*copied(B - 1, "mv1"))
            sp.dma_start(b2_all, fb2[0, :].partition_broadcast(128)).then_inc(table_in, 16)
            store_t(B - 1)
            sp.wait_ge(t_stored, 16 * B)
            sp.dma_start(t_all.rearrange("p (b n) -> p b n", b=B), t_d.rearrange("b p n -> p b n")).then_inc(t_in, 16)
            sp.wait_ge(tail_ready, 1)
            for e in range(E):
                row = sp.value_load(tail_i[0:1, e:e + 1], min_val=0, max_val=E * CAP - 128)
                sp.dma_start(xs_d[bass.ds(row, 128), :], pad_d[128 * e:128 * e + 128, :]).then_inc(pad_in, 16)
            sp.wait_ge(pad_in, 16 * (E + 1))
            sp.wait_ge(scattered, 16 * 2 * NT * B)
            sp.wait_ge(tab_ready, 2)

            def load_rows(i, k):
                row = sp.value_load(tab_i[0:1, 1, bass.ds(4 * i + k, 1)],
                                    min_val=0, max_val=E * CAP + (NPAD - 1) * 128)
                sp.dma_start(xrow[:, k, :], xs_d[bass.ds(row, 128), :]).then_inc(xrow_in[k], 16)

            for k in range(4):
                load_rows(0, k)
            with sp.Fori(1, NTAB // 4) as i:
                for k in range(4):
                    sp.wait_ge(tr_full, 4 * i + k - 3)
                    sp.wait_ge(wd_ready, 4 * i + k - 3)
                    load_rows(i, k)
            for k in range(4):
                sp.wait_ge(xrow_in[k], 16 * (NTAB // 4))
                sp.wait_ge(y_out[k], 16 * (NTILE // 4))
            for b in range(B):
                if b >= 2:
                    sp.wait_ge(res_full, 2 * b - 2)
                for j in range(2):
                    sp.dma_start(zz[:, b % 2, j, :], z_d[(j * B + b) * N:(j * B + b + 1) * N, :].rearrange("(p t) c -> p (t c)", p=128))\
                      .then_inc(zz_in[b % 2], 16)
            sp.wait_ge(t_in, 16)
            for k in range(2):
                sp.wait_ge(out_done[k], 16 * (B // 2))

        @block.gpsimd
        def _(pool):
            gp = nc.gpsimd
            gp.memset(minus_half[:, :], -0.5).then_inc(place_free, 1)
            gp.memset(ones[:, :], 1.0).then_inc(zeroed, 1)
            gp.memset(xwin[:, :, :], 0.0).then_inc(zeroed, 1)
            gp.memset(gw1_sb[:, :], 0.0).then_inc(zeroed, 1)
            gp.memset(gw2_sb[:, :], 0.0).then_inc(zeroed, 1)
            gp.memset(wbias[:, :, :], 0.0).then_inc(zeroed, 1)
            pool.wait_ge(zeroed, 5)
            pool.dma_start(gw1_sb[:, 0:GH], gate_w1).then_inc(win_in, 16)
            pool.dma_start(gw2_sb[0:GH, :], gate_w2).then_inc(win_in, 16)
            gp.memset(kbdw[:, :, :], 0.0).then_inc(zeroed, 1)
            gp.memset(kbd[:, :, :], 0.0).then_inc(zeroed, 1)

            def inverse_root(b, k):
                pool.wait_ge(var_ready, b * 3 + k + 1)
                gp.tensor_tensor(rstd[:, :], vpe[:, :], minus_half[:, :], ALU.pow).then_inc(rstd_ready, 1)

            def head(b):
                inverse_root(b, 0)
                pool.wait_ge(*copied(b, "xh0"))
                pool.wait_ge(*copied(b, "xh1"))
                pool.nop(nofuse=True)
                for wr in range(GRID):
                    nr = min(WS, H - WS * wr)
                    for wc, nw in ((0, GRID - 1), (GRID - 1, 1)):
                        ncol = WS if wc == 0 else W - WS * wc
                        last = gp.tensor_copy(
                            xwin[:, GRID * wr + wc:GRID * wr + wc + nw, :].rearrange("p w (r c) -> p w r c", r=WS)[:, :, 0:nr, 0:ncol],
                            xhatT[:, WS * wr:WS * wr + nr, WS * wc:WS * wc + nw * ncol].rearrange("p r (w c) -> p w r c", w=nw))
                last.then_inc(xwin_ready, 1)
                for br in range(H // KS):
                    last = gp.tensor_copy(
                        xblk[:, 8 * br:8 * br + 8, :].rearrange("p k (r c) -> p k r c", r=KS),
                        xhatT[:, KS * br:KS * br + KS, :].rearrange("p r (k c) -> p k r c", c=KS))
                last.then_inc(xblk_ready, 1)

            def windows(b):
                for g in range(NGRP + 1):
                    if g < NGRP:
                        n, np_ = group_shape(g)
                        pool.wait_ge(wmax_ready, b * NGRP + g + 1)
                        v = tw[0:np_, g % 3, 0:n * WTOK].rearrange("p (a m) -> p a m", m=WTOK)
                        gp.tensor_tensor(v, v, nmw[0:np_, g % 3, 0:n].unsqueeze(2).to_broadcast([np_, n, WTOK]),
                                         ALU.add).then_inc(wsub_ready, 1)
                    if g >= 1:
                        n, np_ = group_shape(g - 1)
                        k = (g - 1) % 3
                        pool.wait_ge(wrz_ready, b * NGRP + g)
                        v = ew[0:np_, k, 0:n * WTOK].rearrange("p (a m) -> p a m", m=WTOK)
                        gp.tensor_tensor(v, v, rZw[0:np_, k, 0:n].unsqueeze(2).to_broadcast([np_, n, WTOK]),
                                         ALU.mult).then_inc(wprob_ready, 1)
                inverse_root(b, 1)
                inverse_root(b, 2)

            def scatter_rows(b):
                for k in range(2):
                    pool.wait_ge(pay2_ready if k else pay_ready, b + 1)
                    pool.nop(nofuse=True)
                    for t in range(NT):
                        gp.indirect_dma_start(xs_d, bass.IndirectOffsetOnAxis(pos[:, NT * k + t:NT * k + t + 1], 0),
                                              pay[:, k, t, :], None).then_inc(scattered, 16)

            head(0)
            with pool.Fori(0, B - 1) as b:
                windows(b)
                head(b + 1)
                scatter_rows(b)
                pool.wait_ge(scattered, 16 * 2 * NT * (b + 1))
                pool.wait_ge(t_stored, 16 * (b + 1))
                pool.nop(nofuse=True)
                gp.memset(token[:, :], 0.0).then_inc(place_free, 1)
            windows(B - 1)
            scatter_rows(B - 1)

            def weight_and_place(i, n):
                k, turn = n % 4, i + n // 4
                pool.wait_ge(xrow_in[k], 16 * turn + 16)
                if not isinstance(turn, int) or turn > 0:
                    pool.wait_ge(y_out[k], 16 * turn)
                pool.nop(nofuse=True)
                gp.tensor_copy(wd[:, k, :], xrow[:, k, C:C + 2]).then_inc(wd_ready, 1)

            def outputs_out(i):
                for r in range(4):
                    weight_and_place(i, r + 1)
                    pool.wait_ge(wd_ready, 4 * i + r + 1)
                    pool.wait_ge(y_ready, 4 * i + r + 3)
                    pool.nop(nofuse=True)
                    gp.indirect_dma_start(z_d, bass.IndirectOffsetOnAxis(wd[:, r, 1:2].bitcast(U32), 0),
                                          yrow[:, r, :], None).then_inc(y_out[r], 16)

            weight_and_place(0, 0)
            outputs_out(0)
            with pool.Fori(1, NTILE // 4) as i:
                outputs_out(i)

        @block.scalar
        def _(act):
            sc = nc.scalar
            with act.Fori(0, B) as b:
                act.wait_ge(const_in, 48)
                for i in range(2):
                    act.wait_ge(*filled(b, f"xt{i}"))
                    sc.activation(x_tok[:, 4 * i:4 * i + 4, :].rearrange("p t c -> p (t c)"), bank(f"xt{i}"),
                                  ACT.Copy).then_inc(read_sem(f"xt{i}"), 1)
                for i in range(2):
                    act.wait_ge(*filled(b, f"xh{i}"))
                    sc.activation(xhatT[:, 16 * i:16 * i + 16, :].rearrange("p r c -> p (r c)"), bank(f"xh{i}"),
                                  ACT.Copy).then_inc(read_sem(f"xh{i}"), 1)
                for i in range(2):
                    act.wait_ge(*filled(b, f"kc{i}"))
                    sc.activation(kcT[:, 16 * i:16 * i + 16, :].rearrange("p r c -> p (r c)"), bank(f"kc{i}"),
                                  ACT.Identity, bias=col("bk_c")).then_inc(read_sem(f"kc{i}"), 1)
                for i in range(2):
                    act.wait_ge(*filled(b, f"gh{i}"))
                    sc.activation(gh[:, 512 * i:512 * i + 512], bank(f"gh{i}"), ACT.Gelu,
                                  bias=col("gate_b1")).then_inc(read_sem(f"gh{i}"), 1)
                keys_to_blocks(act, sc, b, 1)
                for i in (0, 2):
                    w0, nw = WPARTS[i]
                    act.wait_ge(*filled(b, f"qw{i}"))
                    sc.activation(qwT[:, w0 * WTOK:(w0 + nw) * WTOK], bank(f"qw{i}")[:, 0:nw * WTOK],
                                  ACT.Identity, bias=col("bq_w")).then_inc(read_sem(f"qw{i}"), 1)
                for i in range(2):
                    act.wait_ge(*filled(b, f"gz{i}"))
                    sc.activation(gz[0:3, 512 * i:512 * i + 512], bank(f"gz{i}")[0:3, :], ACT.Identity,
                                  bias=col("gate_b2", 0, 3)).then_inc(read_sem(f"gz{i}"), 1)
                act.wait_ge(*filled(b, "gt"))
                sc.activation(ge[:, :, :].rearrange("p t g -> p (t g)"), bank("gt")[:, 0:3 * NT], ACT.Exp,
                              scale=-1.0).then_inc(read_sem("gt"), 1)
                for name, h, bias in (("mk", hk, "b1k"), ("mv", hv, "b1v")):
                    for a in range(2):
                        act.wait_ge(*filled(b, f"{name}{a}"))
                        sc.activation(h[:, a, :], bank(f"{name}{a}")[:, 0:NB], ACT.Gelu,
                                      bias=col(f"{bias}{a}")).then_inc(read_sem(f"{name}{a}"), 1)
                act.wait_ge(*filled(b, "k2"))
                for h in range(HEADS):
                    q = slice(HD * h, HD * h + HD)
                    last = sc.activation(kbd[q, h, 0:NB], bank("k2")[q, 0:NB], ACT.Identity,
                                         bias=col("b2k", HD * h, HD * h + HD))
                last.then_inc(read_sem("k2"), 1)

                def exps(s, base, t, m):
                    act.wait_ge(max_ready, b * 2 * NT + base + t + 1)
                    for h in range(HEADS):
                        name = f"S{s}{t}{'ab'[h // 2]}"
                        last = sc.activation(Pb[t % NRING][:, h, 0:m], bank(name)[:, (h % 2) * m:(h % 2) * m + m], ACT.Exp,
                                             bias=nmx[:, t % NRING, h:h + 1], accum_out=Z[:, t % NRING, h:h + 1])
                        if h % 2:
                            last.then_inc(read_sem(name), 1)

                def second_chunk(s, t, m1):
                    name = f"T{s}{t}b"
                    act.wait_ge(*filled(b, name))
                    dst = PT[0:m1, 1, :, 128 * t:128 * t + 128]
                    src = bank(name)[0:m1, :].rearrange("p (h n) -> p h n", h=HEADS)
                    if s == "c":
                        sc.activation(dst, src, ACT.Copy, accum_out=impacc[0:m1, 1, t:t + 1]).then_inc(read_sem(name), 1)
                    else:
                        sc.activation(dst, src, ACT.Copy).then_inc(read_sem(name), 1)

                act.wait_ge(place_free, b + 1)
                for t in range(NT + T_LAG):
                    if t < NT:
                        exps("c", 0, t, NB)
                    if t >= T_LAG:
                        second_chunk("c", t - T_LAG, M1)

                for g in range(NGRP + OW_LAG):
                    if g < NGRP:
                        n, np_ = group_shape(g)
                        act.wait_ge(wsub_ready, b * NGRP + g + 1)
                        sc.activation(ew[0:np_, g % 3, 0:n * WTOK], tw[0:np_, g % 3, 0:n * WTOK], ACT.Exp)\
                          .then_inc(wexp_ready, 1)
                    if 0 <= g - PW_LAG < NGRP:
                        for p in pairs_of(g - PW_LAG):
                            np_ = pair_rows(p)
                            act.wait_ge(*filled(b, f"PW{p}"))
                            sc.activation(ptw[0:WTOK, p % 4, :, 0:np_],
                                          bank(f"PW{p}")[0:WTOK, :].rearrange("p (h n) -> p h n", h=HEADS)[:, :, 0:np_],
                                          ACT.Copy).then_inc(read_sem(f"PW{p}"), 1)
                act.wait_ge(*filled(b, "vt"))
                sc.activation(v_sb[:, :, :].rearrange("p a c -> p (a c)"), bank("vt")[:, 0:2 * C],
                              ACT.Copy).then_inc(read_sem("vt"), 1)
                for t in range(NT + T_LAG):
                    if t < NT:
                        exps("s", NT, t, 256)
                    if t >= T_LAG:
                        second_chunk("s", t - T_LAG, 128)

                for i in range(2):
                    act.wait_ge(*filled(b, f"tt{i}"))
                    sc.activation(xtT[:, 512 * i:512 * i + 512], bank(f"tt{i}"), ACT.Copy)\
                      .then_inc(read_sem(f"tt{i}"), 1)
                for i in range(2):
                    act.wait_ge(*filled(b, f"rl{i}"))
                    sc.activation(gz[0:E, 512 * i:512 * i + 512], bank(f"rl{i}")[0:E, :], ACT.Identity,
                                  bias=col("br", 0, E)).then_inc(read_sem(f"rl{i}"), 1)
                act.wait_ge(ldif_ready, b + 1)
                sc.activation(ldif[:, 1, :], ldif[:, 0, :], ACT.Exp).then_inc(lexp_ready, 1)
                act.wait_ge(xn_ready, 2 * b + 2)
                sc.activation(pay[:, 1, :, 0:C], pay[:, 0, :, 0:C], ACT.Copy).then_inc(pay2_ready, 1)

            def expert_weights(i, n):
                e = act.value_load(tab_i[0:1, 0, bass.ds(4 * i + n, 1)], min_val=0, max_val=E - 1)
                sc.activation(wx[:, n % 4, :], fw_sb[:, bass.ds(e, 1), 0:W1X].rearrange("p a n -> p (a n)"), ACT.Copy)\
                  .then_inc(wx_ready, 1)

            def hidden(r, n):
                act.wait_ge(h_full, n)
                for c in range(HC):
                    last = sc.activation(hT[:, r % 2, c, :], hid(r)[:, C * c:C * c + C], ACT.Gelu,
                                         bias=wx[:, r, O_B1 + c:O_B1 + c + 1])
                last.then_inc(h_ready, 1)

            act.wait_ge(ffn_in, 16 * (HC + 3))
            act.wait_ge(tab_ready, 2)
            for n in range(AHEAD):
                expert_weights(0, n)
            hidden(0, 1)
            with act.Fori(0, NTILE // 4) as i:
                for r in range(4):
                    expert_weights(i, r + AHEAD)
                    hidden((r + 1) % 4, 4 * i + r + 2)
            for b in range(B):
                k = b % 2
                if b >= 2:
                    act.wait_ge(out_done[k], 16 * (b // 2))
                for j in range(2):
                    act.wait_ge(res_full, 2 * b + j + 1)
                    sc.activation(xo[:, k, 512 * j:512 * j + 512], ps[:, 512 * (2 * b + j):512 * (2 * b + j) + 512], ACT.Copy)\
                      .then_inc(xo_ready, 1)
                act.wait_ge(xo_ready, 2 * b + 2)
                act.dma_start(out[b, :, :], xo[:, k, :]).then_inc(out_done[k], 16)

        @block.vector
        def _(dve):
            ve = nc.vector
            for k in range(8):
                ve.memset(ps[:, 512 * k:512 * k + 512], 0.0).then_inc(bank_read[k], 1)
            for t in (NT, 0):
                ve.memset(cum[:, t, :], 0.0).then_inc(y_ready, 1)
            dve.wait_ge(y_ready, 2)
            dve.wait_ge(const_in, 48)
            ve.tensor_copy(dest[:, :], cols[:, COL_DEST:COL_DEST + 2 * NT]).then_inc(dest_ready, 1)
            with dve.Fori(0, B) as b:
                links = [0]

                def link(ins):
                    links[0] += 1
                    ins.then_inc(dve_done, 1)
                    dve.wait_ge(dve_done, b * DVE_LINKS + links[0])

                def normalise(k, src, dst, eps, ready):
                    for t in range(NT):
                        last = ve.bn_stats(stats[:, t, :], src[:, t, :])
                        if t == 0 and k == 1:
                            last.then_inc(t_ready, 1)
                    link(last)
                    dve.nop(nofuse=True)
                    for t in range(NT):
                        last = ve.bn_aggr(mv[:, t, :], stats[:, t, :])
                    link(last)
                    ve.tensor_scalar(vpe[:, :], mv[:, :, 1], eps, None, ALU.add).then_inc(var_ready, 1)
                    dve.wait_ge(rstd_ready, b * 3 + k + 1)
                    for t in range(NT):
                        last = ve.tensor_scalar(dst[:, t, :], src[:, t, :], mv[:, t, 0:1], rstd[:, t:t + 1],
                                                ALU.subtract, ALU.mult)
                        if t % 4 == 3:
                            last.then_inc(ready, 1)

                dve.wait_ge(const_in, 48)
                dve.wait_ge(*copied(b, "xt0"))
                dve.wait_ge(*copied(b, "xt1"))
                normalise(0, x_tok, xhat_tok, EPS_C, xhat_tok_ready)
                dve.wait_ge(*copied(b, "kc0"))
                dve.wait_ge(*copied(b, "kc1"))
                for s in range(NPOS):
                    r, c = divmod(s, KS)
                    ve.tensor_scalar(kp[:, s, :].rearrange("p (r c) -> p r c", r=NBH),
                                     kcT[:, r:r + 2 * NBH - 1:2, c:c + 2 * NBH - 1:2],
                                     cols[:, COL_POS + s:COL_POS + s + 1], None, ALU.add).then_inc(kp_ready, 1)
                for i in range(2):
                    dve.wait_ge(*filled(b, f"vc{i}"))
                    ve.tensor_scalar(vcT[:, 16 * i:16 * i + 16, :].rearrange("p r c -> p (r c)"), bank(f"vc{i}"),
                                     col("bv_c"), None, ALU.add).then_inc(read_sem(f"vc{i}"), 1)

                def queries(name, bias):
                    for i in range(2):
                        dve.wait_ge(*filled(b, f"{name}{i}"))
                        ve.tensor_scalar(qT[:, 512 * i:512 * i + 512], bank(f"{name}{i}"), col(bias), SCALE,
                                         ALU.add, ALU.mult).then_inc(read_sem(f"{name}{i}"), 1)

                queries("qc", "bq_c")
                keys_to_blocks(dve, ve, b, 0)
                keys_to_blocks(dve, ve, b, 2)
                dve.wait_ge(*filled(b, "qw1"))
                w0, nw = WPARTS[1]
                ve.tensor_scalar(qwT[:, w0 * WTOK:(w0 + nw) * WTOK], bank("qw1")[:, 0:nw * WTOK],
                                 col("bq_w"), None, ALU.add).then_inc(read_sem("qw1"), 1)
                dve.wait_ge(*copied(b, "gt"))
                link(ve.tensor_scalar(ge[:, :, :], ge[:, :, :], 1.0, None, ALU.add))
                link(ve.reciprocal(gtok[:, :, :], ge[:, :, :]))
                for g in range(NGRP):
                    n = min(4, NWIN - 4 * g)
                    dve.wait_ge(*filled(b, f"vw{g}"))
                    ve.tensor_tensor(vw[:, 4 * g:4 * g + n, :],
                                     bank(f"vw{g}")[0:WTOK, 0:n * C].rearrange("p (w c) -> p w c", c=C),
                                     rows[0:WTOK, ROW_BVW:ROW_BVW + C].unsqueeze(1).to_broadcast([WTOK, n, C]),
                                     ALU.add).then_inc(read_sem(f"vw{g}"), 1)
                dve.wait_ge(*filled(b, "v2"))
                ve.tensor_tensor(v_sb[:, 0, :], bank("v2")[:, 0:C], rows[:, ROW_B2V:ROW_B2V + C], ALU.add)
                ve.tensor_tensor(v_sb[0:M1, 1, :], bank("v2")[0:M1, C:2 * C], rows[0:M1, ROW_B2V:ROW_B2V + C],
                                 ALU.add).then_inc(read_sem("v2"), 1)

                def maxima(s, t, m):
                    dve.wait_ge(*filled(b, f"S{s}{t}a"))
                    dve.wait_ge(*filled(b, f"S{s}{t}b"))
                    k = plan[f"S{s}{t}a"][0]
                    v = ps[:, 512 * k:512 * k + 1024].rearrange("p (a n) -> p a n", a=2)[:, :, 0:2 * m]
                    ve.tensor_reduce(nmx[:, t % NRING, :].rearrange("p (a h) -> p a h", a=2),
                                     v.rearrange("p a (h m) -> p a h m", h=2), AX.X, ALU.max, negate=True)\
                      .then_inc(max_ready, 1)

                def divide(s, t, m):
                    dve.wait_ge(*copied(b, f"S{s}{t}b"))
                    link(ve.reciprocal(rZ[:, t % NRING, :], Z[:, t % NRING, :]))
                    for h in range(HEADS):
                        v = Pb[t % NRING][:, h, 0:m]
                        last = ve.tensor_scalar(v, v, rZ[:, t % NRING, h:h + 1],
                                                None, ALU.mult)
                    last.then_inc(prob_ready, 1)

                def first_chunk(s, t):
                    name = f"T{s}{t}a"
                    dve.wait_ge(*filled(b, name))
                    dst = PT[:, 0, :, 128 * t:128 * t + 128]
                    src = bank(name).rearrange("p (h n) -> p h n", h=HEADS)
                    if s == "c":
                        ve.tensor_scalar(dst, src, 1.0, None, ALU.mult, ALU.add,
                                         accum_out=impacc[:, 0, t:t + 1]).then_inc(read_sem(name), 1)
                    else:
                        ve.tensor_copy(dst, src).then_inc(read_sem(name), 1)

                def branch_output(s, i, dst):
                    dve.wait_ge(*filled(b, f"O{s}{i}"))
                    ve.tensor_copy(dst[:, 512 * i:512 * i + 512], bank(f"O{s}{i}")).then_inc(read_sem(f"O{s}{i}"), 1)

                def tiles(s, m, dst):
                    for t in range(NT + T_LAG):
                        if t < NT:
                            maxima(s, t, m)
                        if 1 <= t <= NT:
                            divide(s, t - 1, m)
                        if t >= T_LAG:
                            first_chunk(s, t - T_LAG)
                        if t == O_LAG + 1:
                            branch_output(s, 0, dst)

                dve.wait_ge(place_free, b + 1)
                tiles("c", NB, ocT)
                dve.wait_ge(*copied(b, f"Tc{NT - 1}a"))
                dve.wait_ge(*copied(b, f"Tc{NT - 1}b"))
                ve.tensor_reduce(impcol[:, 0:1], impacc[:, 0, :], AX.X, ALU.add)
                ve.tensor_reduce(impcol[0:M1, 1:2], impacc[0:M1, 1, :], AX.X, ALU.add).then_inc(impcol_ready, 1)
                queries("qs", "bq_s")
                branch_output("c", 1, ocT)

                def top_blocks():
                    dve.wait_ge(*filled(b, "imp"))
                    ve.tensor_copy(imprun[0:1, 0, :], bank("imp")[0:1, 0:NB]).then_inc(read_sem("imp"), 1)
                    dve.wait_ge(*copied(b, "imp"))
                    dve.nop(nofuse=True)
                    link(ve.max(top[0:1, 0:8], imprun[0:1, 0, :]))
                    dve.nop(nofuse=True)
                    ve.max_index(topi[0:1, 0:8], top[0:1, 0:8], imprun[0:1, 0, :])
                    link(ve.match_replace(imprun[0:1, 1, :], top[0:1, 0:8], imprun[0:1, 0, :], -1.0))
                    dve.nop(nofuse=True)
                    link(ve.max(top[0:1, 8:16], imprun[0:1, 1, :]))
                    dve.nop(nofuse=True)
                    link(ve.max_index(topi[0:1, 8:16], top[0:1, 8:16], imprun[0:1, 1, :]))
                    ve.tensor_scalar(topc[0:1, :], topi[0:1, :], float(NBLK - 1), None, ALU.min).then_inc(sel_ready, 1)

                def flip(name, bias):
                    dve.wait_ge(*filled(b, name))
                    ve.tensor_scalar(kdup[:, :, :, :],
                                     bank(name)[:, 0:NSEL * NPOS].rearrange("p (k s) -> p k s", s=NPOS)
                                     .unsqueeze(2).to_broadcast([128, NSEL, 2, NPOS]),
                                     col(bias), None, ALU.add).then_inc(read_sem(name), 1)
                    dve.wait_ge(*copied(b, name))
                    link(ve.transpose(kflip[:, :, :, :].rearrange("p k a s -> p (k a s)"),
                                      kdup[:, :, :, :].rearrange("p k a s -> p (k a s)")))
                    link(ve.tensor_scalar(khalf[:, :, :], kflip[:, :, 0, :], col("m0"), None, ALU.mult))

                def selected_keys():
                    flip("ks", "bk_s")
                    for h in range(HEADS):
                        p0, p1 = HD * h, HD * h + HD
                        last = ve.scalar_tensor_tensor(
                            out=kbd[p0:p1, h, :].rearrange("p (k i) -> p k i", i=NPOS), in0=kflip[p0:p1, :, 1, :],
                            scalar=col("m1", p0, p1), in1=khalf[p0:p1, :, :], op0=ALU.mult, op1=ALU.add)
                    last.then_inc(kbd_sel_ready, 1)
                    dve.wait_ge(kbd_sel_ready, b + 1)

                def selected_values():
                    flip("vs", "bv_s")
                    ve.scalar_tensor_tensor(
                        out=vselT[:, :].rearrange("p (k i) -> p k i", i=NPOS), in0=kflip[:, :, 1, :],
                        scalar=col("m1"), in1=khalf[:, :, :], op0=ALU.mult, op1=ALU.add).then_inc(vselT_ready, 1)

                dve.wait_ge(bias_in, 32)
                for g in range(NGRP + OW_LAG):
                    if g < NGRP:
                        n, np_ = group_shape(g)
                        k, m = g % 3, n * WTOK
                        dve.wait_ge(*filled(b, f"SW{g}"))
                        if n > HEADS:
                            ve.scalar_tensor_tensor(
                                out=tw[0:np_, k, 0:m].rearrange("p (a m) -> p a m", a=2),
                                in0=bank(f"SW{g}")[0:np_, 0:m].rearrange("p (a m) -> p a m", a=2), scalar=SCALE,
                                in1=wbias[0:np_, :, :].rearrange("p h m -> p (h m)").unsqueeze(1)
                                .to_broadcast([np_, 2, HEADS * WTOK]),
                                op0=ALU.mult, op1=ALU.add).then_inc(read_sem(f"SW{g}"), 1)
                        else:
                            ve.scalar_tensor_tensor(
                                out=tw[0:np_, k, 0:m], in0=bank(f"SW{g}")[0:np_, 0:m], scalar=SCALE,
                                in1=wbias[0:np_, :, :].rearrange("p h m -> p (h m)"),
                                op0=ALU.mult, op1=ALU.add).then_inc(read_sem(f"SW{g}"), 1)
                        dve.wait_ge(*copied(b, f"SW{g}"))
                        ve.tensor_reduce(nmw[0:np_, k, 0:n], tw[0:np_, k, 0:m].rearrange("p (a m) -> p a m", m=WTOK),
                                         AX.X, ALU.max, negate=True).then_inc(wmax_ready, 1)
                    if g == 0:
                        top_blocks()
                    if 1 <= g <= NGRP:
                        n, np_ = group_shape(g - 1)
                        k = (g - 1) % 3
                        dve.wait_ge(wexp_ready, b * NGRP + g)
                        link(ve.tensor_reduce(Zw[0:np_, k, 0:n],
                                              ew[0:np_, k, 0:n * WTOK].rearrange("p (a m) -> p a m", m=WTOK),
                                              AX.X, ALU.add))
                        ve.reciprocal(rZw[0:np_, k, 0:n], Zw[0:np_, k, 0:n]).then_inc(wrz_ready, 1)
                    if 0 <= g - OW_LAG < NGRP:
                        q = g - OW_LAG
                        dve.wait_ge(*filled(b, f"OW{q}"))
                        for w in range(4 * q, min(4 * q + 4, NWIN)):
                            r0, nr, c0, ncol = window(w)
                            last = ve.tensor_copy(
                                owT[:, :].rearrange("p (r c) -> p r c", c=W)[:, r0:r0 + nr, c0:c0 + ncol],
                                bank(f"OW{q}")[:, WTOK * (w % 4):WTOK * (w % 4) + WTOK]
                                .rearrange("p (r c) -> p r c", r=WS)[:, 0:nr, 0:ncol])
                        last.then_inc(read_sem(f"OW{q}"), 1)
                    if g == SEL_STEP + 1:
                        selected_keys()
                    if g == SEL_STEP + 2:
                        selected_values()
                tiles("s", 256, osT)
                branch_output("s", 1, osT)

                for t in range(NT):
                    dve.wait_ge(*filled(b, f"pj{t}"))
                    ve.tensor_tensor(pj[:, t % 2, :], bank(f"pj{t}")[:, 0:3 * C], rows[:, ROW_PROJ:ROW_PROJ + 3 * C],
                                     ALU.add).then_inc(read_sem(f"pj{t}"), 1)
                    dve.wait_ge(*copied(b, f"pj{t}"))
                    for i in range(3):
                        link(ve.scalar_tensor_tensor(
                            out=t_tok[:, t, :], in0=pj[:, t % 2, C * i:C * i + C], scalar=gtok[:, t, i:i + 1],
                            in1=(t_tok if i else x_tok)[:, t, :], op0=ALU.mult, op1=ALU.add))
                normalise(1, t_tok, xt_tok, EPS_T, xt_ready)
                dve.wait_ge(xt_ready, b * 2 + 2)
                normalise(2, xt_tok, pay[:, 0, :, 0:C], EPS_T, xn_ready)

                dve.wait_ge(*filled(b, "rt"))
                ve.tensor_copy(lg[:, :, :].rearrange("p t e -> p (t e)"), bank("rt")[:, 0:NT * E])\
                  .then_inc(read_sem("rt"), 1)
                dve.wait_ge(*copied(b, "rt"))
                dve.nop(nofuse=True)
                for t in range(NT):
                    last = ve.max(lmax[:, t, :], lg[:, t, :])
                link(last)
                ve.tensor_tensor(ldif[:, 0, :], lmax[:, :, 1], lmax[:, :, 0], ALU.subtract).then_inc(ldif_ready, 1)
                for t in range(NT):
                    last = ve.max_index(lidx[:, t, :], lmax[:, t, :], lg[:, t, :])
                link(last)
                link(ve.tensor_copy(lidxf[:, :, :], lidx[:, :, 0:2]))
                for i in range(2):
                    last = ve.tensor_tensor(oneh[:, i, :, :],
                                            rows[:, ROW_IOTA:ROW_IOTA + E].unsqueeze(1).to_broadcast([128, NT, E]),
                                            lidxf[:, :, i:i + 1].to_broadcast([128, NT, E]), ALU.is_equal)
                link(last)
                ve.tensor_tensor(picks[:, :, :], oneh[:, 0, :, :], oneh[:, 1, :, :], ALU.add)
                dve.wait_ge(lexp_ready, b + 1)
                link(ve.tensor_scalar(ldif[:, 2, :], ldif[:, 1, :], 1.0, None, ALU.add))
                link(ve.reciprocal(wtop[:, 0, :], ldif[:, 2, :]))
                for t in range(NT):
                    link(ve.tensor_tensor(cum[:, t + 1, :], cum[:, t, :], picks[:, t, :], ALU.add))
                link(ve.tensor_tensor(wtop[:, 1, :], wtop[:, 0, :], ldif[:, 1, :], ALU.mult))
                ve.tensor_copy(pay[:, :, :, C], wtop[:, :, :]).then_inc(picks_ready, 1)
                dve.wait_ge(dest_ready, b + 1)
                ve.tensor_copy(pay[:, :, :, C + 1].bitcast(U32), dest[:, :].rearrange("p (k t) -> p k t", k=2))
                ve.tensor_scalar(dest[:, :], dest[:, :], float(N), None, ALU.add).then_inc(dest_ready, 1)
                dve.wait_ge(*filled(b, "rk"))
                ve.tensor_tensor(rkb[:, :, :], bank("rk")[:, 0:NT * E].rearrange("p (t e) -> p t e", e=E),
                                 rows[:, ROW_BASE:ROW_BASE + E].unsqueeze(1).to_broadcast([128, NT, E]),
                                 ALU.add).then_inc(read_sem("rk"), 1)
                ve.tensor_copy(cum[:, 0, :], cum[:, NT, :])
                dve.wait_ge(*copied(b, "rk"))
                for i in range(2):
                    last = ve.tensor_tensor(oneh[:, i, :, :], oneh[:, i, :, :], rkb[:, :, :], ALU.mult)
                link(last)
                link(ve.tensor_reduce(posf[:, :, :], oneh[:, :, :, :], AX.X, ALU.add))
                ve.tensor_copy(pos[:, :], posf[:, :, :].rearrange("p k t -> p (k t)")).then_inc(pay_ready, 1)
                assert links[0] == DVE_LINKS, links[0]


            done = [0]

            def step(ins):
                done[0] += 1
                ins.then_inc(table_step, 1)
                dve.wait_ge(table_step, done[0])

            dve.wait_ge(cnt_full, 1)
            step(ve.tensor_copy(cnt[:, :], ps[:, 512 * 6:512 * 6 + E]))
            step(ve.tensor_tensor(tailf[:, :], cnt[0:1, :], rows[0:1, ROW_BASE:ROW_BASE + E], ALU.add))
            ve.tensor_copy(tail_i[:, :], tailf[:, :]).then_inc(tail_ready, 1)
            step(ve.tensor_tensor(steps, cnt[:, :].unsqueeze(2).to_broadcast([128, E, TSTEP]),
                                  rows[:, ROW_STEP:ROW_STEP + TSTEP].unsqueeze(1).to_broadcast([128, E, TSTEP]), ALU.is_gt))
            step(ve.tensor_reduce(ntl[:, :], steps, AX.X, ALU.add))
            step(ve.tensor_copy(upto[:, 0:1], ntl[:, 0:1]))
            for e in range(1, E):
                step(ve.tensor_tensor(upto[:, e:e + 1], upto[:, e - 1:e], ntl[:, e:e + 1], ALU.add))
            step(ve.tensor_scalar(past[:, 0, :], upto[0:NTAB, :], col("j", 0, NTAB), None, ALU.is_le))
            step(ve.tensor_scalar(past[:, 1, :], ntl[0:NTAB, :], -128.0, float(CAP), ALU.mult, ALU.add))
            step(ve.tensor_tensor(past[:, 1, :], past[:, 1, :], past[:, 0, :], ALU.mult))
            step(ve.tensor_reduce(tabf[0:NTAB, :], past[:, :, :], AX.X, ALU.add))
            ve.tensor_scalar(tab[:, 0:1], tabf[0:NTAB, 0:1], float(E - 1), None, ALU.min)
            ve.tensor_tensor(tab[:, 1:2], tabf[0:NTAB, 1:2], col("j128", 0, NTAB), ALU.add).then_inc(tab_ready, 1)
            dve.wait_ge(tab_full, 1)
            ve.tensor_copy(tab_i[:, :, :], ps[0:1, 512 * 7:512 * 7 + 2 * 128].rearrange("p (k j) -> p k j", k=2)[:, :, 0:NTAB])\
              .then_inc(tab_ready, 1)
            dve.wait_ge(tab_ready, 2)

            def expert_input(i, n):
                r = n % 4
                dve.wait_ge(wx_ready, 4 * i + n + 1)
                dve.wait_ge(tr_full, 4 * i + n + 1)
                ve.tensor_scalar(xe[:, r % 2, :], turned(r), wx[:, r, O_G:O_G + 1], wx[:, r, O_LB:O_LB + 1],
                                 ALU.mult, ALU.add).then_inc(xe_ready, 1)

            def tiles4(i):
                for r in range(4):
                    expert_input(i, r + AHEAD)
                    e = dve.value_load(tab_i[0:1, 0, bass.ds(4 * i + r, 1)], min_val=0, max_val=E - 1)
                    dve.wait_ge(y_full, 4 * i + r + 1)
                    ve.tensor_tensor(yb[:, r % 2, :], outputs(r), b2_all[:, bass.ds(e * C, C)], ALU.add).then_inc(yb_ready, 1)
                    dve.wait_ge(wd_ready, 4 * i + r + 1)
                    if not isinstance(i, int):
                        dve.wait_ge(y_out[r], 16 * i)
                    dve.wait_ge(yb_ready, 4 * i + r + 1)
                    ve.tensor_scalar(yrow[:, r, :], yb[:, r % 2, :], wd[:, r, 0:1], None, ALU.mult).then_inc(y_ready, 1)

            dve.wait_ge(table_in, 16)
            for n in range(AHEAD):
                expert_input(0, n)
            tiles4(0)
            with dve.Fori(1, NTILE // 4) as i:
                tiles4(i)
            dve.wait_ge(t_in, 16)
            for b in range(B):
                k = b % 2
                dve.wait_ge(zz_in[k], 32 * (b // 2) + 32)
                ve.tensor_tensor(zz[:, k, 0, :], zz[:, k, 0, :], zz[:, k, 1, :], ALU.add).then_inc(sum_half, 1)
                dve.wait_ge(sum_half, b + 1)
                ve.tensor_tensor(zz[:, k, 0, :], zz[:, k, 0, :], t_all[:, N * b:N * b + N], ALU.add).then_inc(sum_ready, 1)

        @block.tensor
        def _(pe):
            mm, tr = nc.tensor.matmul, nc.tensor.transpose
            with pe.Fori(0, B) as b:

                def transposes(name, srcs, k, m):
                    pe.wait_ge(*free_for(b, name))
                    for j, src in enumerate(srcs):
                        last = tr(bank(name)[0:m, k * j:k * j + k], src, ident[0:k, 0:k])
                    last.then_inc(full_sem(name), 1)

                pe.wait_ge(const_in, 48)
                pe.wait_ge(x_in, b * 16 + 16)
                for i in range(2):
                    transposes(f"xt{i}", [x_sb[:, 512 * i + 128 * j:512 * i + 128 * j + 128] for j in range(4)], 128, 128)
                for i in range(2):
                    pe.wait_ge(xhat_tok_ready, b * 2 + i + 1)
                    transposes(f"xh{i}", [xhat_tok[:, 4 * i + j, :] for j in range(4)], 128, 128)
                pe.wait_ge(proj_in, 32)

                def project(name, weights, rhs, n, m=128):
                    pe.wait_ge(*free_for(b, name))
                    dst = bank(name)[0:m, 0:n]
                    mm(dst, weights, rhs, start=True, stop=True).then_inc(full_sem(name), 1)

                def pixels(i):
                    return xhatT[:, 16 * i:16 * i + 16, :]

                for i in range(2):
                    pe.wait_ge(*copied(b, f"xh{i}"))
                    project(f"kc{i}", qkvc_sb[:, C:2 * C], pixels(i), 512)
                for i in range(2):
                    project(f"vc{i}", qkvc_sb[:, 2 * C:3 * C], pixels(i), 512)
                for i in range(2):
                    project(f"qc{i}", qkvc_sb[:, 0:C], pixels(i), 512)
                pe.wait_ge(win_in, 32)
                for i in range(2):
                    project(f"gh{i}", gw1_sb[:, :], pixels(i), 512)
                pe.wait_ge(xwin_ready, b + 1)
                for name, k in (("kw", 1), ("qw", 0)):
                    for i, (w0, nw) in enumerate(WPARTS):
                        project(f"{name}{i}", qkvw_sb[:, C * k:C * k + C], xwin[:, w0:w0 + nw, :], nw * WTOK)
                for i in range(2):
                    pe.wait_ge(*copied(b, f"gh{i}"))
                    project(f"gz{i}", gw2_sb[:, :], gh[:, 512 * i:512 * i + 512], 512, m=3)
                for i in range(2):
                    pe.wait_ge(*copied(b, f"gz{i}"))
                pe.wait_ge(*free_for(b, "gt"))
                pe.nop(nofuse=True)
                for t in range(NT):
                    last = tr(bank("gt")[:, 3 * t:3 * t + 3], gz[0:3, 128 * t:128 * t + 128], ident[0:3, 0:3])
                last.then_inc(full_sem("gt"), 1)

                pe.wait_ge(wk_in, 16)
                pe.wait_ge(*free_for(b, "mk0"))
                pe.wait_ge(*free_for(b, "mk1"))
                for s in range(NPOS):
                    pe.wait_ge(kp_ready, b * NPOS + s + 1)
                    for a in range(2):
                        last = mm(bank(f"mk{a}")[:, 0:NB], w1k_sb[:, s, C * a:C * a + C], kp[:, s, :],
                                  start=(s == 0), stop=(s == NPOS - 1))
                        if s == NPOS - 1:
                            last.then_inc(full_sem(f"mk{a}"), 1)
                pe.wait_ge(wv_in, 16)
                for i in range(2):
                    pe.wait_ge(*copied(b, f"vc{i}"))
                for a in range(2):
                    pe.wait_ge(*free_for(b, f"mv{a}"))
                    for s in range(NPOS):
                        r, c = divmod(s, KS)
                        last = mm(bank(f"mv{a}")[:, 0:NB],
                                  w1v_sb[:, s, C * a:C * a + C], vcT[:, r:r + 2 * NBH - 1:2, c:c + 2 * NBH - 1:2],
                                  start=(s == 0), stop=(s == NPOS - 1))
                    last.then_inc(full_sem(f"mv{a}"), 1)
                pe.wait_ge(w2_in, 32)
                for a in range(2):
                    pe.wait_ge(*copied(b, f"mk{a}"))
                pe.wait_ge(*free_for(b, "k2"))
                for a in range(2):
                    last = mm(bank("k2")[:, 0:NB], w2k_sb[:, a, :], hk[:, a, :], start=(a == 0), stop=(a == 1))
                last.then_inc(full_sem("k2"), 1)
                for g in range(NGRP):
                    pe.wait_ge(*free_for(b, f"vw{g}"))
                    for w in range(4 * g, min(4 * g + 4, NWIN)):
                        last = mm(bank(f"vw{g}")[0:WTOK, C * (w % 4):C * (w % 4) + C], xwin[:, w, :],
                                  qkvw_sb[:, 2 * C:3 * C], start=True, stop=True)
                    last.then_inc(full_sem(f"vw{g}"), 1)
                for a in range(2):
                    pe.wait_ge(*copied(b, f"mv{a}"))
                pe.wait_ge(*free_for(b, "v2"))
                for i, m in enumerate((M0, M1)):
                    for a in range(2):
                        last = mm(bank("v2")[0:m, C * i:C * i + C], hv[:, a, M0 * i:M0 * i + m], w2v_sb[:, a, :],
                                  start=(a == 0), stop=(a == 1))
                last.then_inc(full_sem("v2"), 1)

                def branch_output(s, i, chunks):
                    for k in "ab":
                        pe.wait_ge(*copied(b, f"T{s}{4 * i + 3}{k}"))
                    name = f"O{s}{i}"
                    pe.wait_ge(*free_for(b, name))
                    for a, m in enumerate(chunks):
                        for h in range(HEADS):
                            last = mm(bank(name)[HD * h:HD * h + HD, :], v_sb[0:m, a, HD * h:HD * h + HD],
                                      PT[0:m, a, h, 512 * i:512 * i + 512], start=(a == 0), stop=(a == 1))
                    last.then_inc(full_sem(name), 1)

                def tiles(s, base, chunks):
                    mk = sum(chunks)
                    for t in range(NT + T_LAG):
                        if t < NT:
                            for k in range(2):
                                name = f"S{s}{t}{'ab'[k]}"
                                pe.wait_ge(*free_for(b, name))
                                mm(bank(name)[:, 0:2 * mk], qT[:, 128 * t:128 * t + 128],
                                   kbd[:, 2 * k:2 * k + 2, 0:mk], start=True, stop=True).then_inc(full_sem(name), 1)
                        q = t - T_LAG
                        if q >= 0:
                            pe.wait_ge(prob_ready, b * 2 * NT + base + q + 1)
                            for a, m in enumerate(chunks):
                                name = f"T{s}{q}{'ab'[a]}"
                                transposes(name, [Pb[q % NRING][:, h, M0 * a:M0 * a + m] for h in range(HEADS)], 128, m)
                        if t == O_LAG:
                            branch_output(s, 0, chunks)

                pe.wait_ge(*copied(b, "qc1"))
                pe.wait_ge(*copied(b, "k2"))
                pe.wait_ge(*copied(b, "v2"))
                tiles("c", 0, (M0, M1))
                pe.wait_ge(tail_in, 64)
                for i in range(2):
                    project(f"qs{i}", qkvs_sb[:, 0:C], pixels(i), 512)
                branch_output("c", 1, (M0, M1))

                for i in range(len(WPARTS)):
                    pe.wait_ge(*copied(b, f"kw{i}"))
                    pe.wait_ge(*copied(b, f"qw{i}"))
                pe.wait_ge(*copied(b, f"vw{NGRP - 1}"))
                pe.nop(nofuse=True)
                for g in range(NGRP + OW_LAG):
                    if g < NGRP:
                        pe.wait_ge(*free_for(b, f"SW{g}"))
                        for i, p in enumerate(pairs_of(g)):
                            for j, w in enumerate(windows_of(p)):
                                last = mm(bank(f"SW{g}")[64 * j:64 * j + WTOK, HEADS * WTOK * i:HEADS * WTOK * (i + 1)],
                                          qwT[:, WTOK * w:WTOK * w + WTOK], kbdw[:, :, WTOK * w:WTOK * w + WTOK],
                                          start=True, stop=True)
                        last.then_inc(full_sem(f"SW{g}"), 1)
                    if g == 0:
                        pe.wait_ge(impcol_ready, b + 1)
                        pe.wait_ge(*free_for(b, "imp"))
                        mm(bank("imp")[0:1, 0:M0], impcol[:, 0:1], ident[:, :], start=True, stop=True)
                        mm(bank("imp")[0:1, M0:NB], impcol[0:M1, 1:2], ident[0:M1, 0:M1], start=True, stop=True)\
                            .then_inc(full_sem("imp"), 1)
                    if 0 <= g - PW_LAG < NGRP:
                        q = g - PW_LAG
                        pe.wait_ge(wprob_ready, b * NGRP + q + 1)
                        for i, p in enumerate(pairs_of(q)):
                            np_ = pair_rows(p)
                            pe.wait_ge(*free_for(b, f"PW{p}"))
                            pe.nop(nofuse=True)
                            for h in range(HEADS):
                                o = (HEADS * i + h) * WTOK
                                last = tr(bank(f"PW{p}")[0:WTOK, 128 * h:128 * h + np_],
                                          ew[0:np_, q % 3, o:o + WTOK], ident[0:np_, 0:np_])
                            last.then_inc(full_sem(f"PW{p}"), 1)
                    if 0 <= g - OW_LAG < NGRP:
                        q = g - OW_LAG
                        pe.wait_ge(*free_for(b, f"OW{q}"))
                        for i, p in enumerate(pairs_of(q)):
                            pe.wait_ge(*copied(b, f"PW{p}"))
                            pe.nop(nofuse=True)
                            for j, w in enumerate(windows_of(p)):
                                for h in range(HEADS):
                                    last = mm(bank(f"OW{q}")[HD * h:HD * h + HD, WTOK * (w % 4):WTOK * (w % 4) + WTOK],
                                              vw[:, w, HD * h:HD * h + HD], ptw[0:WTOK, p % 4, h, 64 * j:64 * j + WTOK],
                                              start=True, stop=True)
                        last.then_inc(full_sem(f"OW{q}"), 1)
                    if g == SEL_STEP:
                        pe.wait_ge(xg_in, 16 * NSEL * (b + 1))
                        for name, k in (("ks", 1), ("vs", 2)):
                            project(name, qkvs_sb[:, C * k:C * k + C],
                                    xg[:, :, :].rearrange("p k s -> p (k s)"), NSEL * NPOS)
                pe.wait_ge(vselT_ready, b + 1)
                transposes("vt", [vselT[:, 128 * a:128 * a + 128] for a in range(2)], 128, 128)

                for i in range(2):
                    pe.wait_ge(*copied(b, f"qs{i}"))
                pe.nop(nofuse=True)
                pe.wait_ge(kbd_sel_ready, b + 1)
                pe.wait_ge(*copied(b, "vt"))
                tiles("s", NT, (128, 128))
                branch_output("s", 1, (128, 128))

                pe.wait_ge(*copied(b, "Oc1"))
                pe.wait_ge(*copied(b, "Os1"))
                pe.wait_ge(*copied(b, f"OW{NGRP - 1}"))
                for t in range(NT):
                    name = f"pj{t}"
                    pe.wait_ge(*free_for(b, name))
                    for i, src in enumerate((ocT[:, 128 * t:128 * t + 128], osT[:, 128 * t:128 * t + 128],
                                             owT[:, 128 * t:128 * t + 128])):
                        last = mm(bank(name)[:, C * i:C * i + C], src, proj_sb[:, i, :], start=True, stop=True)
                    last.then_inc(full_sem(name), 1)
                for i in range(2):
                    pe.wait_ge(xt_ready, b * 2 + i + 1)
                    transposes(f"tt{i}", [xt_tok[:, 4 * i + j, :] for j in range(4)], 128, 128)
                for i in range(2):
                    pe.wait_ge(*copied(b, f"tt{i}"))
                    project(f"rl{i}", wr_sb[:, :], xtT[:, 512 * i:512 * i + 512], 512, m=E)
                for i in range(2):
                    pe.wait_ge(*copied(b, f"rl{i}"))
                pe.wait_ge(*free_for(b, "rt"))
                pe.nop(nofuse=True)
                for t in range(NT):
                    last = tr(bank("rt")[:, E * t:E * t + E], gz[0:E, 128 * t:128 * t + 128], ident[0:E, 0:E])
                last.then_inc(full_sem("rt"), 1)
                pe.wait_ge(picks_ready, b + 1)
                pe.wait_ge(*free_for(b, "rk"))
                mm(bank("rk")[:, 0:NT * E], before[:, :], picks[:, :, :], start=True, stop=False)
                mm(bank("rk")[:, 0:NT * E], ones[:, :], cum[:, 0:NT, :], start=False, stop=True)\
                    .then_inc(full_sem("rk"), 1)

            for k in range(8):
                pe.wait_ge(bank_read[k], B * uses[k] + 1)
            mm(ps[:, 512 * 6:512 * 6 + E], ones[:, :], cum[:, NT, :], start=True, stop=True).then_inc(cnt_full, 1)
            pe.wait_ge(tab_ready, 1)
            for k in range(2):
                last = mm(ps[0:1, 512 * 7 + 128 * k:512 * 7 + 128 * k + NTAB], tab[:, k:k + 1], ident[0:NTAB, 0:NTAB],
                          start=True, stop=True)
            last.then_inc(tab_full, 1)

            def turn_rows(r, loaded):
                pe.wait_ge(xrow_in[r], loaded)
                tr(turned(r), xrow[:, r, 0:C], ident[:, :]).then_inc(tr_full, 1)

            def first_layer(r, n):
                pe.wait_ge(xe_ready, n)
                for c in range(HC):
                    last = mm(hid(r)[:, C * c:C * c + C], wx[:, r, C * c:C * c + C], xe[:, r % 2, :], start=True, stop=True)
                last.then_inc(h_full, 1)

            turn_rows(0, 16)
            turn_rows(1, 16)
            first_layer(0, 1)
            with pe.Fori(0, NTILE // 4) as i:
                for r in range(4):
                    turn_rows((r + AHEAD) % 4, 16 * i + 16 * ((r + AHEAD) // 4) + 16)
                    first_layer((r + 1) % 4, 4 * i + r + 2)
                    e = pe.value_load(tab_i[0:1, 0, bass.ds(4 * i + r, 1)], min_val=0, max_val=E - 1)
                    pe.wait_ge(h_ready, 4 * i + r + 1)
                    pe.wait_ge(y_ready, 4 * i + r + 1)
                    for c in range(HC):
                        last = mm(outputs(r), hT[:, r % 2, c, :],
                                  fw_sb[:, bass.ds(e, 1), W1X + C * c:W1X + C * c + C].rearrange("p a n -> p (a n)"),
                                  start=(c == 0), stop=(c == HC - 1))
                    last.then_inc(y_full, 1)
            pe.wait_ge(y_ready, NTILE + 2)
            pe.wait_ge(h_ready, NTILE + 1)
            pe.wait_ge(xe_ready, NTILE + AHEAD)
            for b in range(B):
                pe.wait_ge(sum_ready, b + 1)
                for j in range(2):
                    for q in range(4):
                        last = tr(ps[:, 512 * (2 * b + j) + 128 * q:512 * (2 * b + j) + 128 * q + 128],
                                  zz[:, b % 2, 0, 128 * (4 * j + q):128 * (4 * j + q) + 128], ident[:, :])
                    last.then_inc(res_full, 1)


def kernel(**inputs):
    import numpy as np
    import concourse.bacc as bacc
    from concourse.bass_utils import run_bass_kernel_spmd

    p = {k.replace("L0_conv_", "").replace("L0_ffn_", "f_"): np.asarray(v) for k, v in inputs.items()}
    cols = np.zeros((128, NCOL), np.float32)

    def put(name, v):
        v = v.reshape(-1)
        cols[:v.size, COL[name]] = v

    L = C // NPOS
    ws = p["qkv_slc_w"].reshape(C, 3, NPOS, L)
    wqkv_s = np.concatenate([ws[:, 0].reshape(C, C), ws[:, 1].transpose(0, 2, 1).reshape(C, C),
                             ws[:, 2].transpose(0, 2, 1).reshape(C, C)], axis=1)
    for s, k in (("c", "cmp"), ("s", "slc"), ("w", "win")):
        bias = p[f"qkv_{k}_b" if s != "w" else "win_qkv_b"]
        put(f"bq_{s}", bias[0:C])
        if s != "s":
            put(f"bk_{s}", bias[C:2 * C])
        if s == "c":
            put("bv_c", bias[2 * C:])
        if s == "s":
            put("bk_s", bias[C:2 * C].reshape(NPOS, L).T)
            put("bv_s", bias[2 * C:].reshape(NPOS, L).T)
    for a in range(2):
        put(f"b1k{a}", p["cmpk_b1"][C * a:C * a + C])
        put(f"b1v{a}", p["cmpv_b1"][C * a:C * a + C])
    put("b2k", p["cmpk_b2"])
    put("gate_b1", p["gate_b1"])
    put("gate_b2", p["gate_b2"])
    put("br", p["f_br"])
    half = (np.arange(128) // NPOS) % 2
    cols[:, COL["m0"]] = half == 0
    cols[:, COL["m1"]] = half == 1
    cols[:, COL["j"]] = np.arange(128)
    cols[:, COL["j128"]] = 128 * np.arange(128)
    cols[:, COL_POS:COL_POS + NPOS] = p["pos_embed"].reshape(C, NPOS)
    cols[:, COL_DEST:] = (np.arange(128)[:, None, None] * NT + np.arange(NT) + np.array([0, B * N])[:, None]).reshape(128, -1)
    rows = np.zeros((1, NROW), np.float32)
    rows[0, ROW_BVW:ROW_BVW + C] = p["win_qkv_b"][2 * C:]
    rows[0, ROW_B2V:ROW_B2V + C] = p["cmpv_b2"]
    rows[0, ROW_PROJ:ROW_PROJ + 3 * C] = np.concatenate([p["proj_cmp_b"], p["proj_slc_b"], p["win_proj_b"]])
    rows[0, ROW_IOTA:ROW_IOTA + E] = np.arange(E)
    rows[0, ROW_BASE:ROW_BASE + E] = CAP * np.arange(E)
    rows[0, ROW_STEP:] = 128 * np.arange(TSTEP)
    pad = np.zeros(((E + NPAD) * 128, ROW), np.float32)
    pad[:, C + 1] = (2 * B * N + np.arange((E + NPAD) * 128, dtype=np.int32)).view(np.float32)
    flipped = p["win_bias_table"].reshape(SIDE, SIDE, HEADS)[::-1, ::-1].transpose(2, 0, 1)
    arrays = {
        "x": p["x"].reshape(B, C, N),
        "wqkv_c": p["qkv_cmp_w"], "wqkv_s": wqkv_s, "wqkv_w": p["win_qkv_w"],
        "w1k": p["cmpk_w1"], "w1v": p["cmpv_w1"], "w2k": p["cmpk_w2"], "w2v": p["cmpv_w2"],
        "gate_w1": p["gate_w1"], "gate_w2": p["gate_w2"],
        "projs": np.stack([p["proj_cmp_w"], p["proj_slc_w"], p["win_proj_w"]]),
        "wr": p["f_Wr"], "fw1": p["f_W1"], "fw2": p["f_W2"], "fb2": p["f_b2"].reshape(1, E * C),
        "fb1": p["f_b1"].reshape(E, HC, 128).transpose(2, 0, 1),
        "fgb": np.stack([p["f_ln_g"].T, p["f_ln_b"].T], axis=2), "pad_d": pad,
        "before_d": np.triu(np.ones((128, 128), np.float32), 1),
        "bias_tab": np.stack([flipped[:, WS - 1 - r:SIDE - r, WS - 1 - c:SIDE - c].reshape(-1)
                              for r in range(WS) for c in range(WS)]),
        "cols_d": cols, "rows_d": rows, "ident_d": np.eye(128, dtype=np.float32),
    }
    arrays = {k: np.ascontiguousarray(v) for k, v in arrays.items()}
    nc = bacc.Bacc("TRN2", target_bir_lowering=False, num_devices=1)
    aps = {k: nc.dram_tensor(k, v.shape, F32, kind="ExternalInput").ap() for k, v in arrays.items()}
    out = nc.dram_tensor("out", (B, C, N), F32, kind="ExternalOutput").ap()
    for name, shape in (("xs_d", (E * CAP + NPAD * 128, ROW)), ("z_d", (ZROWS, C)), ("t_d", (B, 128, N))):
        aps[name] = nc.dram_tensor(name, shape, F32, kind="Internal").ap()
    build(nc, out=out, **aps)
    got = run_bass_kernel_spmd(nc, [arrays], core_ids=[0])
    return got.results[0]["out"].reshape(B, C, H, W)
```

```python
import concourse.bass as bass
from concourse import mybir
from contextlib import ExitStack

F32 = mybir.dt.float32
U32 = mybir.dt.uint32
ALU = mybir.AluOpType
ACT = mybir.ActivationFunctionType
AX = mybir.AxisListType

B, C, H, W = 4, 128, 32, 32
N = H * W
NT = N // 128
HEADS, HD = 4, 32
SCALE = HD ** -0.5
KS = 4
NPOS = KS * KS
NBH = (H - KS) // 2 + 1
NB = NBH * NBH
M0, M1 = 128, NB - 128
NSEL = 16
NBLK = (H // KS) * (W // KS)
WS = 7
GRID = 5
WTOK = WS * WS
GH = C // 4
SIDE = 2 * WS - 1
NWIN = GRID * GRID
NPAIR = (NWIN + 1) // 2
NGRP = (NPAIR + 1) // 2
E, HF = 8, 512
HC = HF // 128
EPS_C, EPS_T = 1e-6, 1e-5
T_LAG = 2
NRING = T_LAG + 1
PSLOT = 6
O_LAG = 6
PW_LAG, OW_LAG = 2, 3
W_EARLY = 2
PJ_FIRST = 4
SEL_SP = 8
SEL_STEP = NGRP - 2
WPARTS = [(0, 10), (10, 10), (20, 5)]

ROW = C + 2
CAP = B * N + 128
NTILE = 2 * B * N // 128 + E
AHEAD = 2
NTAB = NTILE + 4
NPAD = NTAB - 2 * B * N // 128
ZROWS = 2 * B * N + (E + NPAD) * 128
O_B1, O_G, O_LB = HF, HF + HC, HF + HC + 1
W1X = HF + HC + 2
WPK = W1X + HC * C
TSTEP = 32

COLS = ["bq_c", "bk_c", "bv_c", "bq_s", "bk_s", "bv_s", "bq_w", "bk_w", "b1k0", "b1k1", "b1v0", "b1v1",
        "b2k", "gate_b1", "m0", "m1", "j", "j128"]
COL = {n: i for i, n in enumerate(COLS)}
COL_POS = len(COLS)
COL_DEST = COL_POS + NPOS
NCOL = COL_DEST + 2 * NT
ROW_BVW, ROW_B2V, ROW_PROJ, ROW_IOTA, ROW_BASE, ROW_STEP = 0, 128, 256, 640, 648, 656
ROW_GB, ROW_BR = ROW_STEP + TSTEP, ROW_STEP + TSTEP + 3
NROW = ROW_BR + E


def psum_plan(attention, tail, head):
    plan, uses, at = {}, [0] * 8, [0]

    def fill(*names, when=True, pair=False):
        if not when:
            return
        if pair and at[0] % 2:
            at[0] += 1
        for name in names:
            bank = at[0] % 8
            plan[name] = (bank, uses[bank])
            uses[bank] += 1
            at[0] += 1

    for s in "cs" if attention else "":
        for t in range(NT + T_LAG):
            if t < NT:
                fill(f"S{s}{t}a", f"S{s}{t}b", pair=True)
            if t >= NT and s == "c":
                fill(f"SW{t - NT}")
            if t == NT and s == "s":
                fill("xt0", "xt1", when=head)
            if t == T_LAG and s == "s":
                fill("vt")
            if t >= T_LAG:
                fill(f"T{s}{t - T_LAG}a", f"T{s}{t - T_LAG}b")
            if t == O_LAG:
                fill(f"O{s}0")
        if s == "c":
            fill("imp", "qs0", "qs1", "Oc1")
            for g in range(W_EARLY, NGRP + OW_LAG):
                if g < NGRP:
                    fill(f"SW{g}")
                if 0 <= g - PW_LAG < NGRP:
                    fill(*(f"PW{p}" for p in pairs_of(g - PW_LAG)))
                if 0 <= g - OW_LAG < NGRP:
                    fill(f"OW{g - OW_LAG}")
                if g == SEL_STEP:
                    fill("ks", "vs")
    fill("xt0", "xt1", when=head and not attention)
    fill("Os1", *(f"pj{t}" for t in range(PJ_FIRST)), when=tail)
    fill("xh0", "xh1", when=head)
    fill(*(f"pj{t}" for t in range(PJ_FIRST, NT)), when=tail)
    fill("kc0", "kc1", "vc0", "vc1", "qc0", "qc1", "gh0", "gh1", "kw0", "kw1", "kw2", "qw0", "qw1", "qw2",
         "gt", "mk0", "mk1", when=head)
    fill("tt0", "tt1", when=tail)
    fill("mv0", when=head)
    fill("rt", when=tail)
    fill("mv1", *(f"vw{g}" for g in range(NGRP)), "k2", "v2", when=head)
    fill("rk", when=tail)
    return plan, uses


class Phase:

    def __init__(self, planned, base, turn=0):
        self.plan, self.uses = planned
        self.base, self.turn = base, turn

    def before(self, bank):
        return self.base[bank] + self.turn * self.uses[bank]


def pairs_of(g):
    return [p for p in (2 * g, 2 * g + 1) if p < NPAIR]


def pair_rows(p):
    return 64 * (len(windows_of(p)) - 1) + WTOK


def group_shape(g):
    return HEADS * len(pairs_of(g)), pair_rows(2 * g)


def windows_of(p):
    return [w for w in (2 * p, 2 * p + 1) if w < NWIN]


def build(nc, x, wqkv_c, wqkv_s, wqkv_w, w1k, w1v, w2k, w2v, gate_w1, gate_w2, projs, wr, fw1, fw2, fb1,
          fgb, fb2, bias_tab, cols_d, rows_d, ident_d, before_d, pad_d, xs_d, z_d, t_d, out):
    first, middle, last_one = psum_plan(False, False, True), psum_plan(True, True, True), psum_plan(True, True, False)
    fills = [first[1][k] + (B - 1) * middle[1][k] + last_one[1][k] for k in range(8)]
    LINKS_FIRST, LINKS_MIDDLE = 7, 67

    def opening():
        return Phase(first, [0] * 8)

    def middle_one(b):
        return Phase(middle, first[1], b)

    def closing():
        return Phase(last_one, [first[1][k] + (B - 1) * middle[1][k] for k in range(8)])

    with ExitStack() as ctx:
        def sb(name, shape, dt=F32):
            return ctx.enter_context(nc.sbuf_tensor(name, shape, dt))

        def sem(name):
            return ctx.enter_context(nc.semaphore(name))

        qkvc_sb = sb("qkvc_sb", [128, 3 * C])
        qkvs_sb = sb("qkvs_sb", [128, 3 * C])
        qkvw_sb = sb("qkvw_sb", [128, 3 * C])
        w1k_sb = sb("w1k_sb", [128, NPOS, 2 * C])
        w1v_sb = sb("w1v_sb", [128, NPOS, 2 * C])
        w2k_sb = sb("w2k_sb", [128, 2, C])
        w2v_sb = sb("w2v_sb", [128, 2, C])
        gw1_sb = sb("gw1_sb", [128, 128])
        gw2_sb = sb("gw2_sb", [128, 3])
        proj_sb = sb("proj_sb", [128, 3, C])
        wr_sb = sb("wr_sb", [128, E])
        fw_sb = sb("fw_sb", [128, E, WPK])
        before = sb("before", [128, 128])
        ones = sb("ones", [128, 128])
        wbias = sb("wbias", [128, HEADS, WTOK])
        cols = sb("cols", [128, NCOL])
        rows = sb("rows", [128, NROW])
        ident = sb("ident", [128, 128])
        minus_half = sb("minus_half", [128, NT])

        def col(name, p0=0, p1=128):
            return cols[p0:p1, COL[name]:COL[name] + 1]

        x_sb = sb("x_sb", [128, N])
        x_tok = sb("x_tok", [128, NT, C])
        r_xhat = sb("r_xhat", [128, N])
        osT = r_xhat
        xhatT = sb("xhatT", [128, H, W])
        xblk = sb("xblk", [128, NBLK, NPOS])
        xwin = sb("xwin", [128, NWIN, WTOK])
        r_kc = sb("r_kc", [128, N])
        kcT = r_kc[:, :].rearrange("p (r c) -> p r c", r=H)
        ocT = r_kc
        r_vc = sb("r_vc", [128, N])
        vcT = r_vc[:, :].rearrange("p (r c) -> p r c", r=H)
        owT = r_vc
        qT = sb("qT", [128, N])
        r_gh = sb("r_gh", [128, N])
        gh = r_gh
        hk = r_gh[:, 0:2 * NB].rearrange("p (a m) -> p a m", a=2)
        hv = r_gh[:, 2 * NB:4 * NB].rearrange("p (a m) -> p a m", a=2)
        r_kp = sb("r_kp", [128, NPOS * NB])
        kp = r_kp[:, :].rearrange("p (s m) -> p s m", s=NPOS)
        vw = r_kp[0:WTOK, 0:NWIN * C].rearrange("p (w c) -> p w c", w=NWIN)
        kbdw = sb("kbdw", [128, HEADS, NWIN * WTOK])
        kbd = sb("kbd", [128, HEADS, 256])
        qwT = sb("qwT", [128, NWIN * WTOK])
        v_sb = sb("v_sb", [128, 2, C])
        r_P = sb("r_P", [128, 2 * HEADS * 256])
        Pb = [v.rearrange("p (h m) -> p h m", h=HEADS)
              for v in (r_P[:, 0:HEADS * 256], r_P[:, HEADS * 256:2 * HEADS * 256], r_gh[:, :])]
        t_tok = r_P[:, 0:N].rearrange("p (t c) -> p t c", t=NT)
        x_res = r_P[:, N:2 * N].rearrange("p (t c) -> p t c", t=NT)
        R = sb("R", [128, 6192])
        PT = R[:, 0:2 * HEADS * PSLOT * 128].rearrange("p (a h n) -> p a h n", a=2, h=HEADS)
        pay = sb("pay", [128, 2, NT, ROW])
        at = [0]

        def part(n):
            at[0] += n
            return R[:, at[0] - n:at[0]]

        WIN = 2 * HEADS * WTOK
        tw = [r_gh[:, 0:WIN], r_gh[:, WIN:2 * WIN], r_P[:, 0:WIN]]
        ew = [r_P[:, WIN * k:WIN * k + WIN] for k in range(1, 4)]
        ptw = part(4 * 512).rearrange("p (r h n) -> p r h n", r=4, h=HEADS)
        xg = r_P[:, 4 * WIN:4 * WIN + NSEL * NPOS].rearrange("p (k s) -> p k s", k=NSEL)
        kdup = part(2 * NSEL * NPOS).rearrange("p (k a s) -> p k a s", k=NSEL, a=2)
        kflip = part(2 * NSEL * NPOS).rearrange("p (k a s) -> p k a s", k=NSEL, a=2)
        khalf = part(NSEL * NPOS).rearrange("p (k s) -> p k s", k=NSEL)
        vselT = part(NSEL * NPOS)
        at[0] = 0
        xtT = part(N)
        xhat_tok = part(N).rearrange("p (t c) -> p t c", t=NT)
        xt_tok = r_xhat[:, :].rearrange("p (t c) -> p t c", t=NT)
        at[0] = 0
        wx = part(4 * W1X).rearrange("p (r n) -> p r n", r=4)
        xrow = part(4 * ROW).rearrange("p (r n) -> p r n", r=4)
        wd = part(4 * 2).rearrange("p (r n) -> p r n", r=4)
        xe = part(2 * C).rearrange("p (r n) -> p r n", r=2)
        hT = part(2 * HF).rearrange("p (r c n) -> p r c n", r=2, c=HC)
        yb = part(2 * C).rearrange("p (r n) -> p r n", r=2)
        yrow = part(4 * C).rearrange("p (r n) -> p r n", r=4)
        steps = part(E * TSTEP).rearrange("p (e s) -> p e s", e=E)
        cnt = part(E)
        ntl = part(E)
        upto = part(E)
        past = part(2 * E)[0:NTAB, :].rearrange("p (k e) -> p k e", k=2)
        tab = part(2)[0:NTAB, :]
        tabf = part(2)
        tab_i = part(2 * NTAB)[0:1, :].bitcast(U32).rearrange("p (k j) -> p k j", k=2)
        tailf = part(E)[0:1, :]
        tail_i = part(E)[0:1, :].bitcast(U32)
        t_all = w1k_sb[:, :, :].rearrange("p s n -> p (s n)")
        b2_all = w1v_sb[:, 0:4, :].rearrange("p s n -> p (s n)")
        zz = kbdw[:, :, :].rearrange("p h m -> p (h m)")[:, 0:4 * N].rearrange("p (r k n) -> p r k n", r=2, k=2)
        xo = w1v_sb[:, 4:12, :].rearrange("p s n -> p (s n)").rearrange("p (r n) -> p r n", r=2)
        stats = sb("stats", [128, NT, 6])
        mv = sb("mv", [128, NT, 2])
        rstd = sb("rstd", [128, NT])
        vpe = sb("vpe", [128, NT])
        gtok = sb("gtok", [128, NT, 3])
        ge = sb("ge", [128, NT, 3])
        nmx = sb("nmx", [128, NRING, HEADS])
        Z = sb("Z", [128, NRING, HEADS])
        rZ = sb("rZ", [128, NRING, HEADS])
        nmw = sb("nmw", [128, 3, 2 * HEADS])
        Zw = sb("Zw", [128, 3, 2 * HEADS])
        rZw = sb("rZw", [128, 3, 2 * HEADS])
        impacc = sb("impacc", [128, 2, NT])
        impcol = sb("impcol", [128, 2])
        imprun = sb("imprun", [1, 2, NB])
        top = sb("top", [1, 16])
        topi = sb("topi", [1, 16], U32)
        topc = sb("topc", [1, 16], U32)
        lg = sb("lg", [128, NT, E])
        lmax = sb("lmax", [128, NT, 8])
        lidx = sb("lidx", [128, NT, 8], U32)
        lidxf = sb("lidxf", [128, NT, 2])
        ldif = sb("ldif", [128, 3, NT])
        wtop = sb("wtop", [128, 2, NT])
        oneh = sb("oneh", [128, 2, NT, E])
        picks = sb("picks", [128, NT, E])
        cum = sb("cum", [128, NT + 1, E])
        token = sb("token", [1, 1])
        rkb = sb("rkb", [128, NT, E])
        posf = sb("posf", [128, 2, NT])
        pos = sb("pos", [128, 2 * NT], U32)
        dest = sb("dest", [128, 2 * NT])

        ps = ctx.enter_context(nc.psum_tensor("ps", [128, 8 * 512], F32))

        bank_full = [sem(f"bank_full{i}") for i in range(8)]
        bank_read = [sem(f"bank_read{i}") for i in range(8)]
        const_in, proj_in, wk_in, wv_in = sem("const_in"), sem("proj_in"), sem("wk_in"), sem("wv_in")
        w2_in, win_in, tail_in, ffn_in = sem("w2_in"), sem("win_in"), sem("tail_in"), sem("ffn_in")
        bias_in = sem("bias_in")
        xres_ready = sem("xres_ready")
        x_in, out_done = sem("x_in"), [sem(f"out_done{i}") for i in range(2)]
        zeroed = sem("zeroed")
        var_ready, rstd_ready = sem("var_ready"), sem("rstd_ready")
        xhat_tok_ready, xblk_ready = sem("xhat_tok_ready"), sem("xblk_ready")
        xwin_ready = sem("xwin_ready")
        kp_ready, gate_exp_ready = sem("kp_ready"), sem("gate_exp_ready")
        max_ready, prob_ready = sem("max_ready"), sem("prob_ready")
        impcol_ready, sel_ready, xg_in = sem("impcol_ready"), sem("sel_ready"), sem("xg_in")
        xg_ready = sem("xg_ready")
        kbd_sel_ready, vselT_ready = sem("kbd_sel_ready"), sem("vselT_ready")
        wmax_ready, wsub_ready, wexp_ready = sem("wmax_ready"), sem("wsub_ready"), sem("wexp_ready")
        wrz_ready, wprob_ready = sem("wrz_ready"), sem("wprob_ready")
        xt_ready, xn_ready = sem("xt_ready"), sem("xn_ready")
        ldif_ready, lexp_ready, picks_ready = sem("ldif_ready"), sem("lexp_ready"), sem("picks_ready")
        t_ready, t_stored = sem("t_ready"), sem("t_stored")
        pay_ready, pay2_ready, scattered = sem("pay_ready"), sem("pay2_ready"), sem("scattered")
        dve_done = sem("dve_done")
        cnt_full, table_step = sem("cnt_full"), sem("table_step")
        tail_ready, tab_ready, tab_full, table_in = sem("tail_ready"), sem("tab_ready"), sem("tab_full"), sem("table_in")
        pad_in, t_in = sem("pad_in"), sem("t_in")
        xrow_in = [sem(f"xrow_in{i}") for i in range(4)]
        tr_full, xe_ready, h_full, h_ready = sem("tr_full"), sem("xe_ready"), sem("h_full"), sem("h_ready")
        y_full, yb_ready, y_ready, wd_ready = sem("y_full"), sem("yb_ready"), sem("y_ready"), sem("wd_ready")
        y_out = [sem(f"y_out{i}") for i in range(4)]
        zz_in = [sem(f"zz_in{i}") for i in range(2)]
        sum_half, sum_ready, wx_ready, dest_ready, res_full, xo_ready, place_free = (
            sem(n) for n in ("sum_half", "sum_ready", "wx_ready", "dest_ready", "res_full", "xo_ready", "place_free"))

        def bank(ph, name):
            k = ph.plan[name][0]
            return ps[:, 512 * k:512 * k + 512]

        def free_for(ph, name):
            k, n = ph.plan[name]
            return bank_read[k], ph.before(k) + n + 1

        def filled(ph, name):
            k, n = ph.plan[name]
            return bank_full[k], ph.before(k) + n + 1

        def copied(ph, name):
            k, n = ph.plan[name]
            return bank_read[k], ph.before(k) + n + 2

        def full_sem(ph, name):
            return bank_full[ph.plan[name][0]]

        def read_sem(ph, name):
            return bank_read[ph.plan[name][0]]

        def window(w):
            r, c = divmod(w, GRID)
            return WS * r, min(WS, H - WS * r), WS * c, min(WS, W - WS * c)

        def keys_to_blocks(eng, ops, ph, i):
            w0, nw = WPARTS[i]
            name = f"kw{i}"
            eng.wait_ge(zeroed, 7)
            eng.wait_ge(*filled(ph, name))
            for h in range(HEADS):
                p0, p1 = HD * h, HD * h + HD
                dst = kbdw[p0:p1, h, w0 * WTOK:(w0 + nw) * WTOK]
                src = bank(ph, name)[p0:p1, 0:nw * WTOK]
                if ops is nc.scalar:
                    last = ops.activation(dst, src, ACT.Identity, bias=col("bk_w", p0, p1))
                else:
                    last = ops.tensor_scalar(dst, src, col("bk_w", p0, p1), None, ALU.add)
            last.then_inc(read_sem(ph, name), 1)

        def hid(r):
            return ps[:, 512 * (2 + r % 2):512 * (2 + r % 2) + 512]

        def turned(r):
            return ps[:, 512 * (r % 2):512 * (r % 2) + C]

        def outputs(r):
            return ps[:, 512 * (4 + r % 2):512 * (4 + r % 2) + C]

        block = ctx.enter_context(nc.Block())

        @block.sync
        def _(sp):
            sp.dma_start(x_sb[:, :], x[0, :, :]).then_inc(x_in, 16)
            sp.dma_start(ident[:, :], ident_d).then_inc(const_in, 16)
            sp.dma_start(cols[:, :], cols_d).then_inc(const_in, 16)
            sp.dma_start(rows[:, :], rows_d[0, :].partition_broadcast(128)).then_inc(const_in, 16)
            sp.dma_start(qkvc_sb[:, :], wqkv_c).then_inc(proj_in, 16)
            sp.dma_start(qkvw_sb[:, :], wqkv_w).then_inc(proj_in, 16)
            sp.wait_ge(zeroed, 5)
            for j in range(2):
                sp.dma_start(wbias[64 * j:64 * j + WTOK, :, :].rearrange("p h m -> p (h m)"), bias_tab).then_inc(bias_in, 16)
            sp.dma_start(w1k_sb[:, :, :], w1k.rearrange("(c s) n -> c s n", s=NPOS)).then_inc(wk_in, 16)
            sp.dma_start(w1v_sb[:, :, :], w1v.rearrange("(c s) n -> c s n", s=NPOS)).then_inc(wv_in, 16)
            sp.dma_start(w2k_sb[:, :, :], w2k.rearrange("(a p) n -> p a n", p=128)).then_inc(w2_in, 16)
            sp.dma_start(w2v_sb[:, :, :], w2v.rearrange("(a p) n -> p a n", p=128)).then_inc(w2_in, 16)
            sp.dma_start(qkvs_sb[:, :], wqkv_s).then_inc(tail_in, 16)
            sp.dma_start(proj_sb[:, :, :], projs.rearrange("a p n -> p a n")).then_inc(tail_in, 16)
            sp.dma_start(wr_sb[:, :], wr).then_inc(tail_in, 16)
            sp.dma_start(before[:, :], before_d).then_inc(tail_in, 16)
            sp.dma_start(fw_sb[:, :, 0:HF], fw1.rearrange("e p n -> p e n")).then_inc(ffn_in, 16)
            for c in range(HC):
                sp.dma_start(fw_sb[:, :, W1X + C * c:W1X + C * c + C],
                             fw2[:, C * c:C * c + C, :].rearrange("e p n -> p e n")).then_inc(ffn_in, 16)
            sp.dma_start(fw_sb[:, :, O_B1:O_B1 + HC], fb1).then_inc(ffn_in, 16)
            sp.dma_start(fw_sb[:, :, O_G:O_G + 2], fgb).then_inc(ffn_in, 16)
            sp.dma_start(xs_d[E * CAP:E * CAP + NPAD * 128, :], pad_d[E * 128:(E + NPAD) * 128, :]).then_inc(pad_in, 16)

            def select_tokens(b):
                sp.wait_ge(xblk_ready, b + 1)
                sp.wait_ge(sel_ready, b + 1)
                sp.nop(nofuse=True)
                for i in range(SEL_SP):
                    idx = sp.value_load(topc[0:1, i:i + 1], min_val=0, max_val=NBLK - 1)
                    sp.dma_start(xg[:, i, :], xblk[:, bass.ds(idx, 1), :].rearrange("p a s -> p (a s)")).then_inc(xg_in, 16)

            def store_t(b):
                sp.wait_ge(t_ready, b + 1)
                sp.dma_start(t_d[bass.ds(b, 1), :, :].rearrange("a p n -> (a p) n") if not isinstance(b, int) else t_d[b, :, :],
                             r_P[:, 0:N]).then_inc(t_stored, 16)

            sp.wait_ge(*filled(opening(), "xt1"))
            sp.dma_start(x_sb[:, :], x[1, :, :]).then_inc(x_in, 16)
            with sp.Fori(0, B - 2) as b:
                select_tokens(b)
                sp.wait_ge(*filled(middle_one(b), "xt1"))
                sp.dma_start(x_sb[:, :], x[bass.ds(b + 2, 1), :, :].rearrange("a p n -> (a p) n")).then_inc(x_in, 16)
                store_t(b)
            select_tokens(B - 2)
            store_t(B - 2)
            select_tokens(B - 1)
            sp.wait_ge(*copied(middle_one(B - 2), "mv1"))
            sp.dma_start(b2_all, fb2[0, :].partition_broadcast(128)).then_inc(table_in, 16)
            store_t(B - 1)
            sp.wait_ge(t_stored, 16 * B + 16)
            sp.dma_start(t_all.rearrange("p (b n) -> p b n", b=B), t_d.rearrange("b p n -> p b n")).then_inc(t_in, 16)
            sp.wait_ge(tail_ready, 1)
            for e in range(E):
                row = sp.value_load(tail_i[0:1, e:e + 1], min_val=0, max_val=E * CAP - 128)
                sp.dma_start(xs_d[bass.ds(row, 128), :], pad_d[128 * e:128 * e + 128, :]).then_inc(pad_in, 16)
            sp.wait_ge(pad_in, 16 * (E + 1))
            sp.wait_ge(scattered, 16 * 2 * NT * B)
            sp.wait_ge(tab_ready, 2)

            def load_rows(i, k):
                row = sp.value_load(tab_i[0:1, 1, bass.ds(4 * i + k, 1)],
                                    min_val=0, max_val=E * CAP + (NPAD - 1) * 128)
                sp.dma_start(xrow[:, k, :], xs_d[bass.ds(row, 128), :]).then_inc(xrow_in[k], 16)

            for k in range(4):
                load_rows(0, k)
            with sp.Fori(1, NTAB // 4) as i:
                for k in range(4):
                    sp.wait_ge(tr_full, 4 * i + k - 3)
                    sp.wait_ge(wd_ready, 4 * i + k - 3)
                    load_rows(i, k)
            for k in range(4):
                sp.wait_ge(xrow_in[k], 16 * (NTAB // 4))
                sp.wait_ge(y_out[k], 16 * (NTILE // 4))
            for b in range(B):
                if b >= 2:
                    sp.wait_ge(res_full, 2 * b - 2)
                for j in range(2):
                    sp.dma_start(zz[:, b % 2, j, :], z_d[(j * B + b) * N:(j * B + b + 1) * N, :].rearrange("(p t) c -> p (t c)", p=128))\
                      .then_inc(zz_in[b % 2], 16)
            sp.wait_ge(t_in, 16)
            for k in range(2):
                sp.wait_ge(out_done[k], 32 * (B // 2))

        @block.gpsimd
        def _(pool):
            gp = nc.gpsimd
            gp.memset(token[:, :], 0.0).then_inc(place_free, 1)
            gp.memset(minus_half[:, :], -0.5).then_inc(t_stored, 16)
            gp.memset(ones[:, :], 1.0).then_inc(zeroed, 1)
            gp.memset(xwin[:, :, :], 0.0).then_inc(zeroed, 1)
            gp.memset(gw1_sb[:, :], 0.0).then_inc(zeroed, 1)
            gp.memset(gw2_sb[:, :], 0.0).then_inc(zeroed, 1)
            gp.memset(wbias[:, :, :], 0.0).then_inc(zeroed, 1)
            pool.wait_ge(zeroed, 5)
            pool.dma_start(gw1_sb[:, 0:GH], gate_w1).then_inc(win_in, 16)
            pool.dma_start(gw2_sb[0:GH, :], gate_w2).then_inc(win_in, 16)
            gp.memset(kbdw[:, :, :], 0.0).then_inc(zeroed, 1)
            gp.memset(kbd[:, :, :], 0.0).then_inc(zeroed, 1)

            def inverse_root(k):
                pool.wait_ge(var_ready, k + 1)
                gp.tensor_tensor(rstd[:, :], vpe[:, :], minus_half[:, :], ALU.pow).then_inc(rstd_ready, 1)

            def head(ph, b, norm):
                inverse_root(norm)
                pool.wait_ge(*copied(ph, "xh0"))
                pool.wait_ge(*copied(ph, "xh1"))
                pool.nop(nofuse=True)
                for wr in range(GRID):
                    nr = min(WS, H - WS * wr)
                    for wc, nw in ((0, GRID - 1), (GRID - 1, 1)):
                        ncol = WS if wc == 0 else W - WS * wc
                        last = gp.tensor_copy(
                            xwin[:, GRID * wr + wc:GRID * wr + wc + nw, :].rearrange("p w (r c) -> p w r c", r=WS)[:, :, 0:nr, 0:ncol],
                            xhatT[:, WS * wr:WS * wr + nr, WS * wc:WS * wc + nw * ncol].rearrange("p r (w c) -> p w r c", w=nw))
                last.then_inc(xwin_ready, 1)
                for br in range(H // KS):
                    last = gp.tensor_copy(
                        xblk[:, 8 * br:8 * br + 8, :].rearrange("p k (r c) -> p k r c", r=KS),
                        xhatT[:, KS * br:KS * br + KS, :].rearrange("p r (k c) -> p k r c", c=KS))
                last.then_inc(xblk_ready, 1)

            def windows(b):
                for g in range(NGRP + 1):
                    if g < NGRP:
                        n, np_ = group_shape(g)
                        pool.wait_ge(wmax_ready, b * NGRP + g + 1)
                        v = tw[g % 3][0:np_, 0:n * WTOK].rearrange("p (a m) -> p a m", m=WTOK)
                        gp.tensor_tensor(v, v, nmw[0:np_, g % 3, 0:n].unsqueeze(2).to_broadcast([np_, n, WTOK]),
                                         ALU.add).then_inc(wsub_ready, 1)
                    if g >= 1:
                        n, np_ = group_shape(g - 1)
                        k = (g - 1) % 3
                        pool.wait_ge(wrz_ready, b * NGRP + g)
                        v = ew[k][0:np_, 0:n * WTOK].rearrange("p (a m) -> p a m", m=WTOK)
                        gp.tensor_tensor(v, v, rZw[0:np_, k, 0:n].unsqueeze(2).to_broadcast([np_, n, WTOK]),
                                         ALU.mult).then_inc(wprob_ready, 1)
                    if g in (3, 4):
                        pool.wait_ge(sel_ready, b + 1)
                        pool.nop(nofuse=True)
                        n = (NSEL - SEL_SP) // 2
                        for i in range(SEL_SP + n * (g - 3), SEL_SP + n * (g - 2)):
                            idx = pool.value_load(topc[0:1, i:i + 1], min_val=0, max_val=NBLK - 1)
                            last = gp.tensor_copy(xg[:, i, :], xblk[:, bass.ds(idx, 1), :].rearrange("p a s -> p (a s)"))
                        last.then_inc(xg_ready, 1)

            def scatter_rows(b):
                for k in range(2):
                    pool.wait_ge(pay2_ready if k else pay_ready, b + 1)
                    pool.nop(nofuse=True)
                    for t in range(NT):
                        gp.indirect_dma_start(xs_d, bass.IndirectOffsetOnAxis(pos[:, NT * k + t:NT * k + t + 1], 0),
                                              pay[:, k, t, :], None).then_inc(scattered, 16)

            head(opening(), 0, 0)
            with pool.Fori(0, B - 1) as b:
                windows(b)
                head(middle_one(b), b + 1, 3 * b + 1)
                inverse_root(3 * b + 2)
                inverse_root(3 * b + 3)
                scatter_rows(b)
                pool.wait_ge(scattered, 16 * 2 * NT * (b + 1))
                pool.nop(nofuse=True)
                gp.memset(token[:, :], 0.0).then_inc(place_free, 1)
            windows(B - 1)
            inverse_root(3 * B - 2)
            inverse_root(3 * B - 1)
            scatter_rows(B - 1)

            def weight_and_place(i, n):
                k, turn = n % 4, i + n // 4
                pool.wait_ge(xrow_in[k], 16 * turn + 16)
                if not isinstance(turn, int) or turn > 0:
                    pool.wait_ge(y_out[k], 16 * turn)
                pool.nop(nofuse=True)
                gp.tensor_copy(wd[:, k, :], xrow[:, k, C:C + 2]).then_inc(wd_ready, 1)

            def outputs_out(i):
                for r in range(4):
                    weight_and_place(i, r + 1)
                    pool.wait_ge(wd_ready, 4 * i + r + 1)
                    pool.wait_ge(y_ready, 4 * i + r + 3)
                    pool.nop(nofuse=True)
                    gp.indirect_dma_start(z_d, bass.IndirectOffsetOnAxis(wd[:, r, 1:2].bitcast(U32), 0),
                                          yrow[:, r, :], None).then_inc(y_out[r], 16)

            weight_and_place(0, 0)
            outputs_out(0)
            with pool.Fori(1, NTILE // 4) as i:
                outputs_out(i)

        @block.scalar
        def _(act):
            sc = nc.scalar
            def hidden_units(ph, name, a):
                h, bias = {"mk": (hk, "b1k"), "mv": (hv, "b1v")}[name]
                act.wait_ge(*filled(ph, f"{name}{a}"))
                sc.activation(h[:, a, :], bank(ph, f"{name}{a}")[:, 0:NB], ACT.Gelu,
                              bias=col(f"{bias}{a}")).then_inc(read_sem(ph, f"{name}{a}"), 1)

            def attention(ph, b):
                def exps(s, base, t, m):
                    act.wait_ge(max_ready, b * 2 * NT + base + t + 1)
                    for h in range(HEADS):
                        name = f"S{s}{t}{'ab'[h // 2]}"
                        last = sc.activation(Pb[t % NRING][:, h, 0:m], bank(ph, name)[:, (h % 2) * m:(h % 2) * m + m], ACT.Exp,
                                             bias=nmx[:, t % NRING, h:h + 1], accum_out=Z[:, t % NRING, h:h + 1])
                        if h % 2:
                            last.then_inc(read_sem(ph, name), 1)

                def second_chunk(s, t, m1):
                    name = f"T{s}{t}b"
                    act.wait_ge(*filled(ph, name))
                    dst = PT[0:m1, 1, :, 128 * (t % PSLOT):128 * (t % PSLOT) + 128]
                    src = bank(ph, name)[0:m1, :].rearrange("p (h n) -> p h n", h=HEADS)
                    if s == "c":
                        sc.activation(dst, src, ACT.Copy, accum_out=impacc[0:m1, 1, t:t + 1]).then_inc(read_sem(ph, name), 1)
                    else:
                        sc.activation(dst, src, ACT.Copy).then_inc(read_sem(ph, name), 1)

                act.wait_ge(t_stored, 16 * b + 16)
                for t in range(NT + T_LAG):
                    if t < NT:
                        exps("c", 0, t, NB)
                    if t >= T_LAG:
                        second_chunk("c", t - T_LAG, M1)

                for g in range(NGRP + OW_LAG):
                    if g < NGRP:
                        n, np_ = group_shape(g)
                        act.wait_ge(wsub_ready, b * NGRP + g + 1)
                        sc.activation(ew[g % 3][0:np_, 0:n * WTOK], tw[g % 3][0:np_, 0:n * WTOK], ACT.Exp)\
                          .then_inc(wexp_ready, 1)
                    if 0 <= g - PW_LAG < NGRP:
                        for p in pairs_of(g - PW_LAG):
                            np_ = pair_rows(p)
                            act.wait_ge(*filled(ph, f"PW{p}"))
                            sc.activation(ptw[0:WTOK, p % 4, :, 0:np_],
                                          bank(ph, f"PW{p}")[0:WTOK, :].rearrange("p (h n) -> p h n", h=HEADS)[:, :, 0:np_],
                                          ACT.Copy).then_inc(read_sem(ph, f"PW{p}"), 1)
                for t in range(NT + T_LAG):
                    if t < NT:
                        exps("s", NT, t, 256)
                    if t == T_LAG:
                        act.wait_ge(*filled(ph, "vt"))
                        sc.activation(v_sb[:, :, :].rearrange("p a c -> p (a c)"), bank(ph, "vt")[:, 0:2 * C],
                                      ACT.Copy).then_inc(read_sem(ph, "vt"), 1)
                    if t >= T_LAG:
                        second_chunk("s", t - T_LAG, 128)


            def seam(ph, t, h):
                if t is not None:
                    sc.activation(x_res, x_tok[:, :, :], ACT.Copy).then_inc(xres_ready, 1)
                    act.wait_ge(xres_ready, t + 1)
                if h is not None:
                    for i in range(2):
                        act.wait_ge(*filled(ph, f"xt{i}"))
                        sc.activation(x_tok[:, 4 * i:4 * i + 4, :].rearrange("p t c -> p (t c)"), bank(ph, f"xt{i}"),
                                      ACT.Copy).then_inc(read_sem(ph, f"xt{i}"), 1)
                    for i in range(2):
                        act.wait_ge(*filled(ph, f"xh{i}"))
                        sc.activation(xhatT[:, 16 * i:16 * i + 16, :].rearrange("p r c -> p (r c)"), bank(ph, f"xh{i}"),
                                      ACT.Copy).then_inc(read_sem(ph, f"xh{i}"), 1)
                    for i in range(2):
                        act.wait_ge(*filled(ph, f"kc{i}"))
                        sc.activation(kcT[:, 16 * i:16 * i + 16, :].rearrange("p r c -> p (r c)"), bank(ph, f"kc{i}"),
                                      ACT.Identity, bias=col("bk_c")).then_inc(read_sem(ph, f"kc{i}"), 1)
                    for i in range(2):
                        act.wait_ge(*filled(ph, f"gh{i}"))
                        sc.activation(gh[:, 512 * i:512 * i + 512], bank(ph, f"gh{i}"), ACT.Gelu,
                                      bias=col("gate_b1")).then_inc(read_sem(ph, f"gh{i}"), 1)
                    keys_to_blocks(act, sc, ph, 1)
                    for i in (0, 2):
                        w0, nw = WPARTS[i]
                        act.wait_ge(*filled(ph, f"qw{i}"))
                        sc.activation(qwT[:, w0 * WTOK:(w0 + nw) * WTOK], bank(ph, f"qw{i}")[:, 0:nw * WTOK],
                                      ACT.Identity, bias=col("bq_w")).then_inc(read_sem(ph, f"qw{i}"), 1)
                    for a in range(2):
                        hidden_units(ph, "mk", a)
                    act.wait_ge(*copied(ph, "gt"))
                    sc.activation(ge[:, :, :], ge[:, :, :], ACT.Exp, scale=-1.0).then_inc(gate_exp_ready, 1)
                if t is not None:
                    for i in range(2):
                        act.wait_ge(*filled(ph, f"tt{i}"))
                        sc.activation(xtT[:, 512 * i:512 * i + 512], bank(ph, f"tt{i}"), ACT.Copy)\
                          .then_inc(read_sem(ph, f"tt{i}"), 1)
                if h is not None:
                    hidden_units(ph, "mv", 0)
                if t is not None:
                    act.wait_ge(xn_ready, 2 * t + 2)
                    sc.activation(pay[:, 1, :, 0:C], pay[:, 0, :, 0:C], ACT.Copy).then_inc(pay2_ready, 1)
                    act.wait_ge(ldif_ready, t + 1)
                    sc.activation(ldif[:, 1, :], ldif[:, 0, :], ACT.Exp).then_inc(lexp_ready, 1)
                if h is not None:
                    hidden_units(ph, "mv", 1)
                    act.wait_ge(*filled(ph, "k2"))
                    for h in range(HEADS):
                        q = slice(HD * h, HD * h + HD)
                        last = sc.activation(kbd[q, h, 0:NB], bank(ph, "k2")[q, 0:NB], ACT.Identity,
                                             bias=col("b2k", HD * h, HD * h + HD))
                    last.then_inc(read_sem(ph, "k2"), 1)


            act.wait_ge(const_in, 48)
            seam(opening(), None, 0)
            with act.Fori(0, B - 1) as b:
                attention(middle_one(b), b)
                seam(middle_one(b), b, b + 1)
            attention(closing(), B - 1)
            seam(closing(), B - 1, None)

            def expert_weights(i, n):
                e = act.value_load(tab_i[0:1, 0, bass.ds(4 * i + n, 1)], min_val=0, max_val=E - 1)
                sc.activation(wx[:, n % 4, :], fw_sb[:, bass.ds(e, 1), 0:W1X].rearrange("p a n -> p (a n)"), ACT.Copy)\
                  .then_inc(wx_ready, 1)

            def hidden(r, n):
                act.wait_ge(h_full, n)
                for c in range(HC):
                    last = sc.activation(hT[:, r % 2, c, :], hid(r)[:, C * c:C * c + C], ACT.Gelu,
                                         bias=wx[:, r, O_B1 + c:O_B1 + c + 1])
                last.then_inc(h_ready, 1)

            act.wait_ge(ffn_in, 16 * (HC + 3))
            act.wait_ge(tab_ready, 2)
            for n in range(AHEAD):
                expert_weights(0, n)
            hidden(0, 1)
            with act.Fori(0, NTILE // 4) as i:
                for r in range(4):
                    expert_weights(i, r + AHEAD)
                    hidden((r + 1) % 4, 4 * i + r + 2)
            for b in range(B):
                k = b % 2
                if b >= 2:
                    act.wait_ge(out_done[k], 32 * (b // 2))
                for j in range(2):
                    act.wait_ge(res_full, 2 * b + j + 1)
                    sc.activation(xo[:, k, 512 * j:512 * j + 512], ps[:, 512 * (2 * b + j):512 * (2 * b + j) + 512], ACT.Copy)\
                      .then_inc(xo_ready, 1)
                    act.wait_ge(xo_ready, 2 * b + j + 1)
                    act.dma_start(out[b, :, 512 * j:512 * j + 512], xo[:, k, 512 * j:512 * j + 512]).then_inc(out_done[k], 16)

        @block.vector
        def _(dve):
            ve = nc.vector
            for k in range(8):
                ve.memset(ps[:, 512 * k:512 * k + 512], 0.0).then_inc(bank_read[k], 1)
            for t in (NT, 0):
                ve.memset(cum[:, t, :], 0.0).then_inc(y_ready, 1)
            dve.wait_ge(y_ready, 2)
            dve.wait_ge(const_in, 48)
            ve.tensor_copy(dest[:, :], cols[:, COL_DEST:COL_DEST + 2 * NT]).then_inc(dest_ready, 1)
            links = [0, 0]

            def link(ins):
                links[1] += 1
                ins.then_inc(dve_done, 1)
                dve.wait_ge(dve_done, links[0] + links[1])

            def normalise(k, src, dst, eps, ready, started=None):
                for t in range(NT):
                    last = ve.bn_stats(stats[:, t, :], src[:, t, :])
                    if t == 0 and started is not None:
                        last.then_inc(started, 1)
                link(last)
                dve.nop(nofuse=True)
                for t in range(NT):
                    last = ve.bn_aggr(mv[:, t, :], stats[:, t, :])
                link(last)
                ve.tensor_scalar(vpe[:, :], mv[:, :, 1], eps, None, ALU.add).then_inc(var_ready, 1)
                dve.wait_ge(rstd_ready, k + 1)
                for t in range(NT):
                    last = ve.tensor_scalar(dst[:, t, :], src[:, t, :], mv[:, t, 0:1], rstd[:, t:t + 1],
                                            ALU.subtract, ALU.mult)
                    if t % 4 == 3:
                        last.then_inc(ready, 1)

            def queries(ph, name, bias):
                for i in range(2):
                    dve.wait_ge(*filled(ph, f"{name}{i}"))
                    ve.tensor_scalar(qT[:, 512 * i:512 * i + 512], bank(ph, f"{name}{i}"), col(bias), SCALE,
                                     ALU.add, ALU.mult).then_inc(read_sem(ph, f"{name}{i}"), 1)

            def branch_output(ph, s, i, dst):
                dve.wait_ge(*filled(ph, f"O{s}{i}"))
                ve.tensor_copy(dst[:, 512 * i:512 * i + 512], bank(ph, f"O{s}{i}")).then_inc(read_sem(ph, f"O{s}{i}"), 1)

            def attention(ph, b):
                def maxima(s, t, m):
                    dve.wait_ge(*filled(ph, f"S{s}{t}a"))
                    dve.wait_ge(*filled(ph, f"S{s}{t}b"))
                    k = ph.plan[f"S{s}{t}a"][0]
                    v = ps[:, 512 * k:512 * k + 1024].rearrange("p (a n) -> p a n", a=2)[:, :, 0:2 * m]
                    ve.tensor_reduce(nmx[:, t % NRING, :].rearrange("p (a h) -> p a h", a=2),
                                     v.rearrange("p a (h m) -> p a h m", h=2), AX.X, ALU.max, negate=True)\
                      .then_inc(max_ready, 1)

                def divide(s, t, m):
                    dve.wait_ge(*copied(ph, f"S{s}{t}b"))
                    link(ve.reciprocal(rZ[:, t % NRING, :], Z[:, t % NRING, :]))
                    for h in range(HEADS):
                        v = Pb[t % NRING][:, h, 0:m]
                        last = ve.tensor_scalar(v, v, rZ[:, t % NRING, h:h + 1],
                                                None, ALU.mult)
                    last.then_inc(prob_ready, 1)

                def first_chunk(s, t):
                    name = f"T{s}{t}a"
                    dve.wait_ge(*filled(ph, name))
                    dst = PT[:, 0, :, 128 * (t % PSLOT):128 * (t % PSLOT) + 128]
                    src = bank(ph, name).rearrange("p (h n) -> p h n", h=HEADS)
                    if s == "c":
                        ve.tensor_scalar(dst, src, 1.0, None, ALU.mult, ALU.add,
                                         accum_out=impacc[:, 0, t:t + 1]).then_inc(read_sem(ph, name), 1)
                    else:
                        ve.tensor_copy(dst, src).then_inc(read_sem(ph, name), 1)

                def window_scores(g):
                    n, np_ = group_shape(g)
                    k, m = g % 3, n * WTOK
                    dve.wait_ge(*filled(ph, f"SW{g}"))
                    if n > HEADS:
                        ve.scalar_tensor_tensor(
                            out=tw[k][0:np_, 0:m].rearrange("p (a m) -> p a m", a=2),
                            in0=bank(ph, f"SW{g}")[0:np_, 0:m].rearrange("p (a m) -> p a m", a=2), scalar=SCALE,
                            in1=wbias[0:np_, :, :].rearrange("p h m -> p (h m)").unsqueeze(1)
                            .to_broadcast([np_, 2, HEADS * WTOK]),
                            op0=ALU.mult, op1=ALU.add).then_inc(read_sem(ph, f"SW{g}"), 1)
                    else:
                        ve.scalar_tensor_tensor(
                            out=tw[k][0:np_, 0:m], in0=bank(ph, f"SW{g}")[0:np_, 0:m], scalar=SCALE,
                            in1=wbias[0:np_, :, :].rearrange("p h m -> p (h m)"),
                            op0=ALU.mult, op1=ALU.add).then_inc(read_sem(ph, f"SW{g}"), 1)
                    dve.wait_ge(*copied(ph, f"SW{g}"))
                    ve.tensor_reduce(nmw[0:np_, k, 0:n], tw[k][0:np_, 0:m].rearrange("p (a m) -> p a m", m=WTOK),
                                     AX.X, ALU.max, negate=True).then_inc(wmax_ready, 1)

                def window_sums(g):
                    n, np_ = group_shape(g)
                    k = (g) % 3
                    dve.wait_ge(wexp_ready, b * NGRP + g + 1)
                    link(ve.tensor_reduce(Zw[0:np_, k, 0:n],
                                          ew[k][0:np_, 0:n * WTOK].rearrange("p (a m) -> p a m", m=WTOK),
                                          AX.X, ALU.add))
                    ve.reciprocal(rZw[0:np_, k, 0:n], Zw[0:np_, k, 0:n]).then_inc(wrz_ready, 1)

                def tiles(s, m, dst):
                    for t in range(NT + T_LAG):
                        if t < NT:
                            maxima(s, t, m)
                        if 1 <= t <= NT:
                            divide(s, t - 1, m)
                        if t >= T_LAG:
                            first_chunk(s, t - T_LAG)
                        if t >= NT and s == "c":
                            window_scores(t - NT)
                        if t == O_LAG + 1:
                            branch_output(ph, s, 0, dst)

                dve.wait_ge(bias_in, 32)
                tiles("c", NB, ocT)
                dve.wait_ge(*copied(ph, f"Tc{NT - 1}a"))
                dve.wait_ge(*copied(ph, f"Tc{NT - 1}b"))
                ve.tensor_reduce(impcol[:, 0:1], impacc[:, 0, :], AX.X, ALU.add)
                ve.tensor_reduce(impcol[0:M1, 1:2], impacc[0:M1, 1, :], AX.X, ALU.add).then_inc(impcol_ready, 1)
                def top_blocks():
                    dve.wait_ge(*filled(ph, "imp"))
                    ve.tensor_copy(imprun[0:1, 0, :], bank(ph, "imp")[0:1, 0:NB]).then_inc(read_sem(ph, "imp"), 1)
                    dve.wait_ge(*copied(ph, "imp"))
                    dve.nop(nofuse=True)
                    link(ve.max(top[0:1, 0:8], imprun[0:1, 0, :]))
                    dve.nop(nofuse=True)
                    ve.max_index(topi[0:1, 0:8], top[0:1, 0:8], imprun[0:1, 0, :])
                    link(ve.match_replace(imprun[0:1, 1, :], top[0:1, 0:8], imprun[0:1, 0, :], -1.0))
                    dve.nop(nofuse=True)
                    link(ve.max(top[0:1, 8:16], imprun[0:1, 1, :]))
                    dve.nop(nofuse=True)
                    link(ve.max_index(topi[0:1, 8:16], top[0:1, 8:16], imprun[0:1, 1, :]))
                    ve.tensor_scalar(topc[0:1, :], topi[0:1, :], float(NBLK - 1), None, ALU.min).then_inc(sel_ready, 1)

                top_blocks()
                queries(ph, "qs", "bq_s")
                window_sums(0)
                branch_output(ph, "c", 1, ocT)

                def flip(name, bias):
                    dve.wait_ge(*filled(ph, name))
                    ve.tensor_scalar(kdup[:, :, :, :],
                                     bank(ph, name)[:, 0:NSEL * NPOS].rearrange("p (k s) -> p k s", s=NPOS)
                                     .unsqueeze(2).to_broadcast([128, NSEL, 2, NPOS]),
                                     col(bias), None, ALU.add).then_inc(read_sem(ph, name), 1)
                    dve.wait_ge(*copied(ph, name))
                    link(ve.transpose(kflip[:, :, :, :].rearrange("p k a s -> p (k a s)"),
                                      kdup[:, :, :, :].rearrange("p k a s -> p (k a s)")))
                    link(ve.tensor_scalar(khalf[:, :, :], kflip[:, :, 0, :], col("m0"), None, ALU.mult))

                def selected_keys():
                    flip("ks", "bk_s")
                    for h in range(HEADS):
                        p0, p1 = HD * h, HD * h + HD
                        last = ve.scalar_tensor_tensor(
                            out=kbd[p0:p1, h, :].rearrange("p (k i) -> p k i", i=NPOS), in0=kflip[p0:p1, :, 1, :],
                            scalar=col("m1", p0, p1), in1=khalf[p0:p1, :, :], op0=ALU.mult, op1=ALU.add)
                    last.then_inc(kbd_sel_ready, 1)
                    dve.wait_ge(kbd_sel_ready, b + 1)

                def selected_values():
                    flip("vs", "bv_s")
                    ve.scalar_tensor_tensor(
                        out=vselT[:, :].rearrange("p (k i) -> p k i", i=NPOS), in0=kflip[:, :, 1, :],
                        scalar=col("m1"), in1=khalf[:, :, :], op0=ALU.mult, op1=ALU.add).then_inc(vselT_ready, 1)

                for g in range(W_EARLY, NGRP + OW_LAG):
                    if g < NGRP:
                        window_scores(g)
                    if g <= NGRP:
                        window_sums(g - 1)
                    if 0 <= g - OW_LAG < NGRP:
                        q = g - OW_LAG
                        dve.wait_ge(*filled(ph, f"OW{q}"))
                        for w in range(4 * q, min(4 * q + 4, NWIN)):
                            r0, nr, c0, ncol = window(w)
                            last = ve.tensor_copy(
                                owT[:, :].rearrange("p (r c) -> p r c", c=W)[:, r0:r0 + nr, c0:c0 + ncol],
                                bank(ph, f"OW{q}")[:, WTOK * (w % 4):WTOK * (w % 4) + WTOK]
                                .rearrange("p (r c) -> p r c", r=WS)[:, 0:nr, 0:ncol])
                        last.then_inc(read_sem(ph, f"OW{q}"), 1)
                    if g == SEL_STEP + 1:
                        selected_keys()
                    if g == SEL_STEP + 2:
                        selected_values()
                tiles("s", 256, osT)

            def combine(ph, b):
                dve.wait_ge(xres_ready, b + 1)
                for q in range(4):
                    for i in range(3):
                        for t in (2 * q, 2 * q + 1):
                            if i == 0:
                                dve.wait_ge(*filled(ph, f"pj{t}"))
                            last = ve.scalar_tensor_tensor(
                                out=t_tok[:, t, :], in0=bank(ph, f"pj{t}")[:, C * i:C * i + C],
                                scalar=gtok[:, t, i:i + 1], in1=(t_tok if i else x_res)[:, t, :],
                                op0=ALU.mult, op1=ALU.add)
                            if i == 2:
                                last.then_inc(read_sem(ph, f"pj{t}"), 1)
                        if i < 2:
                            link(last)

            def values(ph):
                for g in range(NGRP):
                    n = min(4, NWIN - 4 * g)
                    dve.wait_ge(*filled(ph, f"vw{g}"))
                    ve.tensor_tensor(vw[:, 4 * g:4 * g + n, :],
                                     bank(ph, f"vw{g}")[0:WTOK, 0:n * C].rearrange("p (w c) -> p w c", c=C),
                                     rows[0:WTOK, ROW_BVW:ROW_BVW + C].unsqueeze(1).to_broadcast([WTOK, n, C]),
                                     ALU.add).then_inc(read_sem(ph, f"vw{g}"), 1)

            def rows_of_picks(ph):
                dve.wait_ge(*filled(ph, "rk"))
                ve.tensor_tensor(rkb[:, :, :], bank(ph, "rk")[:, 0:NT * E].rearrange("p (t e) -> p t e", e=E),
                                 rows[:, ROW_BASE:ROW_BASE + E].unsqueeze(1).to_broadcast([128, NT, E]),
                                 ALU.add).then_inc(read_sem(ph, "rk"), 1)
                ve.tensor_copy(cum[:, 0, :], cum[:, NT, :])
                dve.wait_ge(*copied(ph, "rk"))
                for i in range(2):
                    last = ve.tensor_tensor(oneh[:, i, :, :], oneh[:, i, :, :], rkb[:, :, :], ALU.mult)
                link(last)
                link(ve.tensor_reduce(posf[:, :, :], oneh[:, :, :, :], AX.X, ALU.add))
                ve.tensor_copy(pos[:, :], posf[:, :, :].rearrange("p k t -> p (k t)")).then_inc(pay_ready, 1)

            def seam(ph, t_, h, norm):
                if t_ is not None:
                    branch_output(ph, "s", 1, osT)
                if h is not None:
                    for i in range(2):
                        dve.wait_ge(*copied(ph, f"xt{i}"))
                    normalise(norm, x_tok, xhat_tok, EPS_C, xhat_tok_ready)
                    norm = norm + 1
                if t_ is not None:
                    combine(ph, t_)
                if h is not None:
                    dve.wait_ge(*copied(ph, "kc0"))
                    dve.wait_ge(*copied(ph, "kc1"))
                    for s in range(NPOS):
                        r, c = divmod(s, KS)
                        ve.tensor_scalar(kp[:, s, :].rearrange("p (r c) -> p r c", r=NBH),
                                         kcT[:, r:r + 2 * NBH - 1:2, c:c + 2 * NBH - 1:2],
                                         cols[:, COL_POS + s:COL_POS + s + 1], None, ALU.add).then_inc(kp_ready, 1)
                    for i in range(2):
                        dve.wait_ge(*filled(ph, f"vc{i}"))
                        ve.tensor_scalar(vcT[:, 16 * i:16 * i + 16, :].rearrange("p r c -> p (r c)"), bank(ph, f"vc{i}"),
                                         col("bv_c"), None, ALU.add).then_inc(read_sem(ph, f"vc{i}"), 1)

                    queries(ph, "qc", "bq_c")
                    keys_to_blocks(dve, ve, ph, 0)
                    keys_to_blocks(dve, ve, ph, 2)
                    dve.wait_ge(*filled(ph, "qw1"))
                    w0, nw = WPARTS[1]
                    ve.tensor_scalar(qwT[:, w0 * WTOK:(w0 + nw) * WTOK], bank(ph, "qw1")[:, 0:nw * WTOK],
                                     col("bq_w"), None, ALU.add).then_inc(read_sem(ph, "qw1"), 1)
                    dve.wait_ge(*filled(ph, "gt"))
                    ve.tensor_tensor(ge[:, :, :], bank(ph, "gt")[:, 0:3 * NT].rearrange("p (t g) -> p t g", g=3),
                                     rows[:, ROW_GB:ROW_GB + 3].unsqueeze(1).to_broadcast([128, NT, 3]),
                                     ALU.add).then_inc(read_sem(ph, "gt"), 1)
                if t_ is not None:
                    for t in range(4, NT):
                        dve.wait_ge(*copied(ph, f"pj{t}"))
                    normalise(norm, t_tok, xt_tok, EPS_T, xt_ready, started=t_ready)
                    dve.wait_ge(xt_ready, t_ * 2 + 2)
                    dve.wait_ge(place_free, t_ + 1)
                    normalise(norm + 1, xt_tok, pay[:, 0, :, 0:C], EPS_T, xn_ready)
                if h is not None:
                    dve.wait_ge(gate_exp_ready, h + 1)
                    link(ve.tensor_scalar(ge[:, :, :], ge[:, :, :], 1.0, None, ALU.add))
                    link(ve.reciprocal(gtok[:, :, :], ge[:, :, :]))
                    for i in range(3):
                        for t in range(NT):
                            last = ve.scalar_tensor_tensor(
                                out=x_tok[:, t, :], in0=rows[:, ROW_PROJ + C * i:ROW_PROJ + C * i + C],
                                scalar=gtok[:, t, i:i + 1], in1=x_tok[:, t, :], op0=ALU.mult, op1=ALU.add)
                        link(last)
                if t_ is not None:
                    dve.wait_ge(*filled(ph, "rt"))
                    ve.tensor_tensor(lg[:, :, :], bank(ph, "rt")[:, 0:NT * E].rearrange("p (t e) -> p t e", e=E),
                                     rows[:, ROW_BR:ROW_BR + E].unsqueeze(1).to_broadcast([128, NT, E]), ALU.add)\
                      .then_inc(read_sem(ph, "rt"), 1)
                    dve.wait_ge(*copied(ph, "rt"))
                    dve.nop(nofuse=True)
                    for t in range(NT):
                        last = ve.max(lmax[:, t, :], lg[:, t, :])
                    link(last)
                    ve.tensor_tensor(ldif[:, 0, :], lmax[:, :, 1], lmax[:, :, 0], ALU.subtract).then_inc(ldif_ready, 1)
                    for t in range(NT):
                        last = ve.max_index(lidx[:, t, :], lmax[:, t, :], lg[:, t, :])
                    link(last)
                    link(ve.tensor_copy(lidxf[:, :, :], lidx[:, :, 0:2]))
                    for i in range(2):
                        last = ve.tensor_tensor(oneh[:, i, :, :],
                                                rows[:, ROW_IOTA:ROW_IOTA + E].unsqueeze(1).to_broadcast([128, NT, E]),
                                                lidxf[:, :, i:i + 1].to_broadcast([128, NT, E]), ALU.is_equal)
                    link(last)
                    ve.tensor_tensor(picks[:, :, :], oneh[:, 0, :, :], oneh[:, 1, :, :], ALU.add)
                    dve.wait_ge(lexp_ready, t_ + 1)
                    link(ve.tensor_scalar(ldif[:, 2, :], ldif[:, 1, :], 1.0, None, ALU.add))
                    link(ve.reciprocal(wtop[:, 0, :], ldif[:, 2, :]))
                    for t in range(NT):
                        link(ve.tensor_tensor(cum[:, t + 1, :], cum[:, t, :], picks[:, t, :], ALU.add))
                    link(ve.tensor_tensor(wtop[:, 1, :], wtop[:, 0, :], ldif[:, 1, :], ALU.mult))
                    ve.tensor_copy(pay[:, :, :, C], wtop[:, :, :]).then_inc(picks_ready, 1)
                    dve.wait_ge(dest_ready, t_ + 1)
                    ve.tensor_copy(pay[:, :, :, C + 1].bitcast(U32), dest[:, :].rearrange("p (k t) -> p k t", k=2))
                    ve.tensor_scalar(dest[:, :], dest[:, :], float(N), None, ALU.add).then_inc(dest_ready, 1)
                if h is not None:
                    values(ph)
                    dve.wait_ge(*filled(ph, "v2"))
                    ve.tensor_tensor(v_sb[:, 0, :], bank(ph, "v2")[:, 0:C], rows[:, ROW_B2V:ROW_B2V + C], ALU.add)
                    ve.tensor_tensor(v_sb[0:M1, 1, :], bank(ph, "v2")[0:M1, C:2 * C], rows[0:M1, ROW_B2V:ROW_B2V + C],
                                     ALU.add).then_inc(read_sem(ph, "v2"), 1)
                if t_ is not None:
                    rows_of_picks(ph)

            seam(opening(), None, 0, 0)
            assert links[1] == LINKS_FIRST, links
            with dve.Fori(0, B - 1) as b:
                links[0], links[1] = LINKS_FIRST + b * LINKS_MIDDLE, 0
                attention(middle_one(b), b)
                seam(middle_one(b), b, b + 1, 3 * b + 1)
                assert links[1] == LINKS_MIDDLE, links
            links[0], links[1] = LINKS_FIRST + (B - 1) * LINKS_MIDDLE, 0
            attention(closing(), B - 1)
            seam(closing(), B - 1, None, 3 * B - 2)

            done = [0]

            def step(ins):
                done[0] += 1
                ins.then_inc(table_step, 1)
                dve.wait_ge(table_step, done[0])

            dve.wait_ge(cnt_full, 1)
            step(ve.tensor_copy(cnt[:, :], ps[:, 512 * 6:512 * 6 + E]))
            step(ve.tensor_tensor(tailf[:, :], cnt[0:1, :], rows[0:1, ROW_BASE:ROW_BASE + E], ALU.add))
            ve.tensor_copy(tail_i[:, :], tailf[:, :]).then_inc(tail_ready, 1)
            step(ve.tensor_tensor(steps, cnt[:, :].unsqueeze(2).to_broadcast([128, E, TSTEP]),
                                  rows[:, ROW_STEP:ROW_STEP + TSTEP].unsqueeze(1).to_broadcast([128, E, TSTEP]), ALU.is_gt))
            step(ve.tensor_reduce(ntl[:, :], steps, AX.X, ALU.add))
            step(ve.tensor_copy(upto[:, 0:1], ntl[:, 0:1]))
            for e in range(1, E):
                step(ve.tensor_tensor(upto[:, e:e + 1], upto[:, e - 1:e], ntl[:, e:e + 1], ALU.add))
            step(ve.tensor_scalar(past[:, 0, :], upto[0:NTAB, :], col("j", 0, NTAB), None, ALU.is_le))
            step(ve.tensor_scalar(past[:, 1, :], ntl[0:NTAB, :], -128.0, float(CAP), ALU.mult, ALU.add))
            step(ve.tensor_tensor(past[:, 1, :], past[:, 1, :], past[:, 0, :], ALU.mult))
            step(ve.tensor_reduce(tabf[0:NTAB, :], past[:, :, :], AX.X, ALU.add))
            ve.tensor_scalar(tab[:, 0:1], tabf[0:NTAB, 0:1], float(E - 1), None, ALU.min)
            ve.tensor_tensor(tab[:, 1:2], tabf[0:NTAB, 1:2], col("j128", 0, NTAB), ALU.add).then_inc(tab_ready, 1)
            dve.wait_ge(tab_full, 1)
            ve.tensor_copy(tab_i[:, :, :], ps[0:1, 512 * 7:512 * 7 + 2 * 128].rearrange("p (k j) -> p k j", k=2)[:, :, 0:NTAB])\
              .then_inc(tab_ready, 1)
            dve.wait_ge(tab_ready, 2)

            def expert_input(i, n):
                r = n % 4
                dve.wait_ge(wx_ready, 4 * i + n + 1)
                dve.wait_ge(tr_full, 4 * i + n + 1)
                ve.tensor_scalar(xe[:, r % 2, :], turned(r), wx[:, r, O_G:O_G + 1], wx[:, r, O_LB:O_LB + 1],
                                 ALU.mult, ALU.add).then_inc(xe_ready, 1)

            def tiles4(i):
                for r in range(4):
                    expert_input(i, r + AHEAD)
                    e = dve.value_load(tab_i[0:1, 0, bass.ds(4 * i + r, 1)], min_val=0, max_val=E - 1)
                    dve.wait_ge(y_full, 4 * i + r + 1)
                    ve.tensor_tensor(yb[:, r % 2, :], outputs(r), b2_all[:, bass.ds(e * C, C)], ALU.add).then_inc(yb_ready, 1)
                    dve.wait_ge(wd_ready, 4 * i + r + 1)
                    if not isinstance(i, int):
                        dve.wait_ge(y_out[r], 16 * i)
                    dve.wait_ge(yb_ready, 4 * i + r + 1)
                    ve.tensor_scalar(yrow[:, r, :], yb[:, r % 2, :], wd[:, r, 0:1], None, ALU.mult).then_inc(y_ready, 1)

            dve.wait_ge(table_in, 16)
            for n in range(AHEAD):
                expert_input(0, n)
            tiles4(0)
            with dve.Fori(1, NTILE // 4) as i:
                tiles4(i)
            dve.wait_ge(t_in, 16)
            for b in range(B):
                k = b % 2
                dve.wait_ge(zz_in[k], 32 * (b // 2) + 32)
                halves = [slice(512 * j, 512 * j + 512) for j in range(2)]
                for q in halves:
                    ve.tensor_tensor(zz[:, k, 0, q], zz[:, k, 0, q], zz[:, k, 1, q], ALU.add).then_inc(sum_half, 1)
                for j, q in enumerate(halves):
                    dve.wait_ge(sum_half, 2 * b + j + 1)
                    ve.tensor_tensor(zz[:, k, 0, q], zz[:, k, 0, q], t_all[:, N * b + 512 * j:N * b + 512 * j + 512],
                                     ALU.add).then_inc(sum_ready, 1)

        @block.tensor
        def _(pe):
            mm, tr = nc.tensor.matmul, nc.tensor.transpose
            def transposes(ph, name, srcs, k, m):
                pe.wait_ge(*free_for(ph, name))
                for j, src in enumerate(srcs):
                    last = tr(bank(ph, name)[0:m, k * j:k * j + k], src, ident[0:k, 0:k])
                last.then_inc(full_sem(ph, name), 1)

            def project(ph, name, weights, rhs, n, m=128):
                pe.wait_ge(*free_for(ph, name))
                dst = bank(ph, name)[0:m, 0:n]
                mm(dst, weights, rhs, start=True, stop=True).then_inc(full_sem(ph, name), 1)

            def pixels(i):
                return xhatT[:, 16 * i:16 * i + 16, :]

            def pixels(i):
                return xhatT[:, 16 * i:16 * i + 16, :]

            def branch_output(ph, s, i, chunks):
                for k in "ab":
                    pe.wait_ge(*copied(ph, f"T{s}{4 * i + 3}{k}"))
                name = f"O{s}{i}"
                pe.wait_ge(*free_for(ph, name))
                for t0, t1 in ((0, 4),) if i == 0 else ((4, PSLOT), (PSLOT, NT)):
                    o, n = 128 * (t0 % PSLOT), 128 * (t1 - t0)
                    for a, m in enumerate(chunks):
                        for h in range(HEADS):
                            last = mm(bank(ph, name)[HD * h:HD * h + HD, 128 * (t0 - 4 * i):128 * (t1 - 4 * i)],
                                      v_sb[0:m, a, HD * h:HD * h + HD], PT[0:m, a, h, o:o + n],
                                      start=(a == 0), stop=(a == 1))
                last.then_inc(full_sem(ph, name), 1)

            def window_scores(ph, g):
                pe.wait_ge(*free_for(ph, f"SW{g}"))
                for i, p in enumerate(pairs_of(g)):
                    for j, w in enumerate(windows_of(p)):
                        last = mm(bank(ph, f"SW{g}")[64 * j:64 * j + WTOK, HEADS * WTOK * i:HEADS * WTOK * (i + 1)],
                                  qwT[:, WTOK * w:WTOK * w + WTOK], kbdw[:, :, WTOK * w:WTOK * w + WTOK],
                                  start=True, stop=True)
                last.then_inc(full_sem(ph, f"SW{g}"), 1)

            def image_by_tokens(ph, h):
                pe.wait_ge(x_in, h * 16 + 16)
                for i in range(2):
                    transposes(ph, f"xt{i}", [x_sb[:, 512 * i + 128 * j:512 * i + 128 * j + 128] for j in range(4)], 128, 128)

            def window_values(ph, gs):
                for g in gs:
                    pe.wait_ge(*free_for(ph, f"vw{g}"))
                    for w in range(4 * g, min(4 * g + 4, NWIN)):
                        last = mm(bank(ph, f"vw{g}")[0:WTOK, C * (w % 4):C * (w % 4) + C], xwin[:, w, :],
                                  qkvw_sb[:, 2 * C:3 * C], start=True, stop=True)
                    last.then_inc(full_sem(ph, f"vw{g}"), 1)

            def value_layer(ph, a):
                pe.wait_ge(*free_for(ph, f"mv{a}"))
                for s in range(NPOS):
                    r, c = divmod(s, KS)
                    last = mm(bank(ph, f"mv{a}")[:, 0:NB],
                              w1v_sb[:, s, C * a:C * a + C], vcT[:, r:r + 2 * NBH - 1:2, c:c + 2 * NBH - 1:2],
                              start=(s == 0), stop=(s == NPOS - 1))
                last.then_inc(full_sem(ph, f"mv{a}"), 1)

            def branches_by_tokens(ph, ts):
                for t in ts:
                    name = f"pj{t}"
                    pe.wait_ge(*free_for(ph, name))
                    for i, src in enumerate((ocT[:, 128 * t:128 * t + 128], osT[:, 128 * t:128 * t + 128],
                                             owT[:, 128 * t:128 * t + 128])):
                        last = mm(bank(ph, name)[:, C * i:C * i + C], src, proj_sb[:, i, :], start=True, stop=True)
                    last.then_inc(full_sem(ph, name), 1)

            def attention(ph, b, following):
                def tiles(s, base, chunks):
                    mk = sum(chunks)
                    for t in range(NT + T_LAG):
                        if t < NT:
                            for k in range(2):
                                name = f"S{s}{t}{'ab'[k]}"
                                pe.wait_ge(*free_for(ph, name))
                                mm(bank(ph, name)[:, 0:2 * mk], qT[:, 128 * t:128 * t + 128],
                                   kbd[:, 2 * k:2 * k + 2, 0:mk], start=True, stop=True).then_inc(full_sem(ph, name), 1)
                        if t >= NT and s == "c":
                            window_scores(ph, t - NT)
                        if t == NT and s == "s" and following is not None:
                            image_by_tokens(ph, following)
                        if t == T_LAG and s == "s":
                            pe.wait_ge(vselT_ready, b + 1)
                            transposes(ph, "vt", [vselT[:, 128 * a:128 * a + 128] for a in range(2)], 128, 128)
                        q = t - T_LAG
                        if q >= 0:
                            pe.wait_ge(prob_ready, b * 2 * NT + base + q + 1)
                            for a, m in enumerate(chunks):
                                name = f"T{s}{q}{'ab'[a]}"
                                transposes(ph, name, [Pb[q % NRING][:, h, M0 * a:M0 * a + m] for h in range(HEADS)], 128, m)
                        if t == O_LAG:
                            if s == "s":
                                pe.wait_ge(*copied(ph, "vt"))
                                pe.nop(nofuse=True)
                            branch_output(ph, s, 0, chunks)

                tiles("c", 0, (M0, M1))
                pe.wait_ge(impcol_ready, b + 1)
                pe.wait_ge(*free_for(ph, "imp"))
                mm(bank(ph, "imp")[0:1, 0:M0], impcol[:, 0:1], ident[:, :], start=True, stop=True)
                mm(bank(ph, "imp")[0:1, M0:NB], impcol[0:M1, 1:2], ident[0:M1, 0:M1], start=True, stop=True)\
                    .then_inc(full_sem(ph, "imp"), 1)
                pe.wait_ge(tail_in, 64)
                for i in range(2):
                    project(ph, f"qs{i}", qkvs_sb[:, 0:C], pixels(i), 512)
                branch_output(ph, "c", 1, (M0, M1))

                for g in range(W_EARLY, NGRP + OW_LAG):
                    if g < NGRP:
                        window_scores(ph, g)
                    if 0 <= g - PW_LAG < NGRP:
                        q = g - PW_LAG
                        pe.wait_ge(wprob_ready, b * NGRP + q + 1)
                        for i, p in enumerate(pairs_of(q)):
                            np_ = pair_rows(p)
                            pe.wait_ge(*free_for(ph, f"PW{p}"))
                            pe.nop(nofuse=True)
                            for h in range(HEADS):
                                o = (HEADS * i + h) * WTOK
                                last = tr(bank(ph, f"PW{p}")[0:WTOK, 128 * h:128 * h + np_],
                                          ew[q % 3][0:np_, o:o + WTOK], ident[0:np_, 0:np_])
                            last.then_inc(full_sem(ph, f"PW{p}"), 1)
                    if 0 <= g - OW_LAG < NGRP:
                        q = g - OW_LAG
                        pe.wait_ge(*free_for(ph, f"OW{q}"))
                        for i, p in enumerate(pairs_of(q)):
                            pe.wait_ge(*copied(ph, f"PW{p}"))
                            pe.nop(nofuse=True)
                            for j, w in enumerate(windows_of(p)):
                                for h in range(HEADS):
                                    last = mm(bank(ph, f"OW{q}")[HD * h:HD * h + HD, WTOK * (w % 4):WTOK * (w % 4) + WTOK],
                                              vw[:, w, HD * h:HD * h + HD], ptw[0:WTOK, p % 4, h, 64 * j:64 * j + WTOK],
                                              start=True, stop=True)
                        last.then_inc(full_sem(ph, f"OW{q}"), 1)
                    if g == SEL_STEP:
                        pe.wait_ge(xg_in, 16 * SEL_SP * (b + 1))
                        pe.wait_ge(xg_ready, 2 * b + 2)
                        for name, k in (("ks", 1), ("vs", 2)):
                            project(ph, name, qkvs_sb[:, C * k:C * k + C],
                                    xg[:, :, :].rearrange("p k s -> p (k s)"), NSEL * NPOS)

                for i in range(2):
                    pe.wait_ge(*copied(ph, f"qs{i}"))
                pe.nop(nofuse=True)
                pe.wait_ge(kbd_sel_ready, b + 1)
                tiles("s", NT, (128, 128))

            def seam(ph, t_, h):
                if h is not None and t_ is None:
                    image_by_tokens(ph, h)
                if t_ is not None:
                    branch_output(ph, "s", 1, (128, 128))
                    pe.wait_ge(*copied(ph, "Oc1"))
                    pe.wait_ge(*copied(ph, "Os1"))
                    pe.wait_ge(*copied(ph, f"OW{NGRP - 1}"))
                    branches_by_tokens(ph, range(PJ_FIRST))
                if h is not None:
                    for i in range(2):
                        pe.wait_ge(xhat_tok_ready, h * 2 + i + 1)
                        transposes(ph, f"xh{i}", [xhat_tok[:, 4 * i + j, :] for j in range(4)], 128, 128)
                if t_ is not None:
                    branches_by_tokens(ph, range(PJ_FIRST, NT))
                if h is not None:
                    pe.wait_ge(proj_in, 32)
                    for i in range(2):
                        pe.wait_ge(*copied(ph, f"xh{i}"))
                        project(ph, f"kc{i}", qkvc_sb[:, C:2 * C], pixels(i), 512)
                    for i in range(2):
                        project(ph, f"vc{i}", qkvc_sb[:, 2 * C:3 * C], pixels(i), 512)
                    for i in range(2):
                        project(ph, f"qc{i}", qkvc_sb[:, 0:C], pixels(i), 512)
                    pe.wait_ge(win_in, 32)
                    for i in range(2):
                        project(ph, f"gh{i}", gw1_sb[:, :], pixels(i), 512)
                    pe.wait_ge(xwin_ready, h + 1)
                    for name, k in (("kw", 1), ("qw", 0)):
                        for i, (w0, nw) in enumerate(WPARTS):
                            project(ph, f"{name}{i}", qkvw_sb[:, C * k:C * k + C], xwin[:, w0:w0 + nw, :], nw * WTOK)
                    for i in range(2):
                        pe.wait_ge(*copied(ph, f"gh{i}"))
                    pe.wait_ge(*free_for(ph, "gt"))
                    pe.nop(nofuse=True)
                    for t in range(NT):
                        last = mm(bank(ph, "gt")[:, 3 * t:3 * t + 3], gh[:, 128 * t:128 * t + 128], gw2_sb[:, :],
                                  start=True, stop=True)
                    last.then_inc(full_sem(ph, "gt"), 1)
                    pe.wait_ge(wk_in, 16)
                    pe.wait_ge(*free_for(ph, "mk0"))
                    pe.wait_ge(*free_for(ph, "mk1"))
                    for s in range(NPOS):
                        pe.wait_ge(kp_ready, h * NPOS + s + 1)
                        for a in range(2):
                            last = mm(bank(ph, f"mk{a}")[:, 0:NB], w1k_sb[:, s, C * a:C * a + C], kp[:, s, :],
                                      start=(s == 0), stop=(s == NPOS - 1))
                            if s == NPOS - 1:
                                last.then_inc(full_sem(ph, f"mk{a}"), 1)

                if t_ is not None:
                    for i in range(2):
                        pe.wait_ge(xt_ready, t_ * 2 + i + 1)
                        transposes(ph, f"tt{i}", [xt_tok[:, 4 * i + j, :] for j in range(4)], 128, 128)
                if h is not None:
                    pe.wait_ge(wv_in, 16)
                    for i in range(2):
                        pe.wait_ge(*copied(ph, f"vc{i}"))
                    value_layer(ph, 0)
                if t_ is not None:
                    for i in range(2):
                        pe.wait_ge(*copied(ph, f"tt{i}"))
                    pe.wait_ge(*free_for(ph, "rt"))
                    pe.nop(nofuse=True)
                    for t in range(NT):
                        last = mm(bank(ph, "rt")[:, E * t:E * t + E], xtT[:, 128 * t:128 * t + 128], wr_sb[:, :],
                                  start=True, stop=True)
                    last.then_inc(full_sem(ph, "rt"), 1)
                if h is not None:
                    value_layer(ph, 1)
                    window_values(ph, range(NGRP))
                    pe.wait_ge(w2_in, 32)
                    for a in range(2):
                        pe.wait_ge(*copied(ph, f"mk{a}"))
                    pe.wait_ge(*free_for(ph, "k2"))
                    for a in range(2):
                        last = mm(bank(ph, "k2")[:, 0:NB], w2k_sb[:, a, :], hk[:, a, :], start=(a == 0), stop=(a == 1))
                    last.then_inc(full_sem(ph, "k2"), 1)
                    for a in range(2):
                        pe.wait_ge(*copied(ph, f"mv{a}"))
                    pe.wait_ge(*free_for(ph, "v2"))
                    for i, m in enumerate((M0, M1)):
                        for a in range(2):
                            last = mm(bank(ph, "v2")[0:m, C * i:C * i + C], hv[:, a, M0 * i:M0 * i + m], w2v_sb[:, a, :],
                                      start=(a == 0), stop=(a == 1))
                    last.then_inc(full_sem(ph, "v2"), 1)

                if t_ is not None:
                    pe.wait_ge(picks_ready, t_ + 1)
                    pe.wait_ge(*free_for(ph, "rk"))
                    mm(bank(ph, "rk")[:, 0:NT * E], before[:, :], picks[:, :, :], start=True, stop=False)
                    mm(bank(ph, "rk")[:, 0:NT * E], ones[:, :], cum[:, 0:NT, :], start=False, stop=True)\
                        .then_inc(full_sem(ph, "rk"), 1)
                if h is not None:
                    for name in ("qc1", "k2", *(f"kw{i}" for i in range(len(WPARTS))),
                                 *(f"qw{i}" for i in range(len(WPARTS))), f"vw{NGRP - 1}", "v2"):
                        pe.wait_ge(*copied(ph, name))
                        pe.nop(nofuse=True)

            pe.wait_ge(const_in, 48)
            seam(opening(), None, 0)
            with pe.Fori(0, B - 1) as b:
                attention(middle_one(b), b, b + 1)
                seam(middle_one(b), b, b + 1)
            attention(closing(), B - 1, None)
            seam(closing(), B - 1, None)

            for k in range(8):
                pe.wait_ge(bank_read[k], fills[k] + 1)
            mm(ps[:, 512 * 6:512 * 6 + E], ones[:, :], cum[:, NT, :], start=True, stop=True).then_inc(cnt_full, 1)
            pe.wait_ge(tab_ready, 1)
            for k in range(2):
                last = mm(ps[0:1, 512 * 7 + 128 * k:512 * 7 + 128 * k + NTAB], tab[:, k:k + 1], ident[0:NTAB, 0:NTAB],
                          start=True, stop=True)
            last.then_inc(tab_full, 1)

            def turn_rows(r, loaded):
                pe.wait_ge(xrow_in[r], loaded)
                tr(turned(r), xrow[:, r, 0:C], ident[:, :]).then_inc(tr_full, 1)

            def first_layer(r, n):
                pe.wait_ge(xe_ready, n)
                for c in range(HC):
                    last = mm(hid(r)[:, C * c:C * c + C], wx[:, r, C * c:C * c + C], xe[:, r % 2, :], start=True, stop=True)
                last.then_inc(h_full, 1)

            turn_rows(0, 16)
            turn_rows(1, 16)
            first_layer(0, 1)
            with pe.Fori(0, NTILE // 4) as i:
                for r in range(4):
                    turn_rows((r + AHEAD) % 4, 16 * i + 16 * ((r + AHEAD) // 4) + 16)
                    first_layer((r + 1) % 4, 4 * i + r + 2)
                    e = pe.value_load(tab_i[0:1, 0, bass.ds(4 * i + r, 1)], min_val=0, max_val=E - 1)
                    pe.wait_ge(h_ready, 4 * i + r + 1)
                    pe.wait_ge(y_ready, 4 * i + r + 1)
                    for c in range(HC):
                        last = mm(outputs(r), hT[:, r % 2, c, :],
                                  fw_sb[:, bass.ds(e, 1), W1X + C * c:W1X + C * c + C].rearrange("p a n -> p (a n)"),
                                  start=(c == 0), stop=(c == HC - 1))
                    last.then_inc(y_full, 1)
            pe.wait_ge(y_ready, NTILE + 2)
            pe.wait_ge(h_ready, NTILE + 1)
            pe.wait_ge(xe_ready, NTILE + AHEAD)
            for b in range(B):
                for j in range(2):
                    pe.wait_ge(sum_ready, 2 * b + j + 1)
                    for q in range(4):
                        last = tr(ps[:, 512 * (2 * b + j) + 128 * q:512 * (2 * b + j) + 128 * q + 128],
                                  zz[:, b % 2, 0, 128 * (4 * j + q):128 * (4 * j + q) + 128], ident[:, :])
                    last.then_inc(res_full, 1)


def kernel(**inputs):
    import numpy as np
    import concourse.bacc as bacc
    from concourse.bass_utils import run_bass_kernel_spmd

    p = {k.replace("L0_conv_", "").replace("L0_ffn_", "f_"): np.asarray(v) for k, v in inputs.items()}
    cols = np.zeros((128, NCOL), np.float32)

    def put(name, v):
        v = v.reshape(-1)
        cols[:v.size, COL[name]] = v

    L = C // NPOS
    ws = p["qkv_slc_w"].reshape(C, 3, NPOS, L)
    wqkv_s = np.concatenate([ws[:, 0].reshape(C, C), ws[:, 1].transpose(0, 2, 1).reshape(C, C),
                             ws[:, 2].transpose(0, 2, 1).reshape(C, C)], axis=1)
    for s, k in (("c", "cmp"), ("s", "slc"), ("w", "win")):
        bias = p[f"qkv_{k}_b" if s != "w" else "win_qkv_b"]
        put(f"bq_{s}", bias[0:C])
        if s != "s":
            put(f"bk_{s}", bias[C:2 * C])
        if s == "c":
            put("bv_c", bias[2 * C:])
        if s == "s":
            put("bk_s", bias[C:2 * C].reshape(NPOS, L).T)
            put("bv_s", bias[2 * C:].reshape(NPOS, L).T)
    for a in range(2):
        put(f"b1k{a}", p["cmpk_b1"][C * a:C * a + C])
        put(f"b1v{a}", p["cmpv_b1"][C * a:C * a + C])
    put("b2k", p["cmpk_b2"])
    put("gate_b1", p["gate_b1"])
    half = (np.arange(128) // NPOS) % 2
    cols[:, COL["m0"]] = half == 0
    cols[:, COL["m1"]] = half == 1
    cols[:, COL["j"]] = np.arange(128)
    cols[:, COL["j128"]] = 128 * np.arange(128)
    cols[:, COL_POS:COL_POS + NPOS] = p["pos_embed"].reshape(C, NPOS)
    cols[:, COL_DEST:] = (np.arange(128)[:, None, None] * NT + np.arange(NT) + np.array([0, B * N])[:, None]).reshape(128, -1)
    rows = np.zeros((1, NROW), np.float32)
    rows[0, ROW_BVW:ROW_BVW + C] = p["win_qkv_b"][2 * C:]
    rows[0, ROW_B2V:ROW_B2V + C] = p["cmpv_b2"]
    rows[0, ROW_PROJ:ROW_PROJ + 3 * C] = np.concatenate([p["proj_cmp_b"], p["proj_slc_b"], p["win_proj_b"]])
    rows[0, ROW_IOTA:ROW_IOTA + E] = np.arange(E)
    rows[0, ROW_BASE:ROW_BASE + E] = CAP * np.arange(E)
    rows[0, ROW_STEP:ROW_STEP + TSTEP] = 128 * np.arange(TSTEP)
    rows[0, ROW_GB:ROW_GB + 3] = p["gate_b2"]
    rows[0, ROW_BR:ROW_BR + E] = p["f_br"]
    pad = np.zeros(((E + NPAD) * 128, ROW), np.float32)
    pad[:, C + 1] = (2 * B * N + np.arange((E + NPAD) * 128, dtype=np.int32)).view(np.float32)
    flipped = p["win_bias_table"].reshape(SIDE, SIDE, HEADS)[::-1, ::-1].transpose(2, 0, 1)
    arrays = {
        "x": p["x"].reshape(B, C, N),
        "wqkv_c": p["qkv_cmp_w"], "wqkv_s": wqkv_s, "wqkv_w": p["win_qkv_w"],
        "w1k": p["cmpk_w1"], "w1v": p["cmpv_w1"], "w2k": p["cmpk_w2"], "w2v": p["cmpv_w2"],
        "gate_w1": p["gate_w1"], "gate_w2": p["gate_w2"],
        "projs": np.stack([p["proj_cmp_w"], p["proj_slc_w"], p["win_proj_w"]]),
        "wr": p["f_Wr"], "fw1": p["f_W1"], "fw2": p["f_W2"], "fb2": p["f_b2"].reshape(1, E * C),
        "fb1": p["f_b1"].reshape(E, HC, 128).transpose(2, 0, 1),
        "fgb": np.stack([p["f_ln_g"].T, p["f_ln_b"].T], axis=2), "pad_d": pad,
        "before_d": np.triu(np.ones((128, 128), np.float32), 1),
        "bias_tab": np.stack([flipped[:, WS - 1 - r:SIDE - r, WS - 1 - c:SIDE - c].reshape(-1)
                              for r in range(WS) for c in range(WS)]),
        "cols_d": cols, "rows_d": rows, "ident_d": np.eye(128, dtype=np.float32),
    }
    arrays = {k: np.ascontiguousarray(v) for k, v in arrays.items()}
    nc = bacc.Bacc("TRN2", target_bir_lowering=False, num_devices=1)
    aps = {k: nc.dram_tensor(k, v.shape, F32, kind="ExternalInput").ap() for k, v in arrays.items()}
    out = nc.dram_tensor("out", (B, C, N), F32, kind="ExternalOutput").ap()
    for name, shape in (("xs_d", (E * CAP + NPAD * 128, ROW)), ("z_d", (ZROWS, C)), ("t_d", (B, 128, N))):
        aps[name] = nc.dram_tensor(name, shape, F32, kind="Internal").ap()
    build(nc, out=out, **aps)
    got = run_bass_kernel_spmd(nc, [arrays], core_ids=[0])
    return got.results[0]["out"].reshape(B, C, H, W)
```
